# Optimizing a Trainium2 kernel written in Bass

```python
import numpy as np
import jax
import jax.numpy as jnp

def _softmax(x, axis=-1):
    return jax.nn.softmax(x, axis=axis)

def _gelu(x):
    return jax.nn.gelu(x, approximate=True)

def _silu(x):
    return jax.nn.silu(x)

def _sigmoid(x):
    return jax.nn.sigmoid(x)

def _layernorm(x, axis=-1, eps=1e-05):
    m = jnp.mean(x, axis=axis, keepdims=True)
    v = jnp.var(x, axis=axis, keepdims=True)
    return (x - m) / jnp.sqrt(v + eps)

def _scatter_add(tgt, idx, src, axis=0):
    return tgt.at[idx].add(src)

def _segment_sum(src, seg, n):
    return jax.ops.segment_sum(src, seg, n)
kernel_name = 'mk_hybrid_d1_jaxref_r8_1fccc2'

def setup_inputs(seed: int=0):
    np.random.seed(seed)
    _w = jnp.asarray

    def _L0_attn_a_setup():
        import jax, jax.numpy as jnp
        import numpy as np
        import math
        B, N, DIM = (4, 512, 128)
        HEADS, DHEAD, NRF = (16, 64, 64)
        STAB = 1e-06

        def _phi(t, RF):
            return jax.nn.relu(jnp.einsum('bhnd,hdr->bhnr', t, RF))
        key = jax.random.key(seed)
        k1, k2, k3, k4 = jax.random.split(key, 4)
        x = jax.random.normal(k1, (B, N, DIM), dtype=jnp.float32)
        W_qkv = jax.random.normal(k2, (DIM, 3 * HEADS * DHEAD), dtype=jnp.float32) * (1.0 / math.sqrt(DIM))
        RF = jax.random.normal(k3, (HEADS, DHEAD, NRF), dtype=jnp.float32) / math.sqrt(NRF)
        W_out = jax.random.normal(k4, (HEADS * DHEAD, DIM), dtype=jnp.float32) * (1.0 / math.sqrt(HEADS * DHEAD))
        b_out = jnp.zeros((DIM,), dtype=jnp.float32)
        return {'x': x, 'W_qkv': W_qkv, 'RF': RF, 'W_out': W_out, 'b_out': b_out}
    _L0_attn_a_in = _L0_attn_a_setup()

    def _L0_attn_b_setup():
        import jax, jax.numpy as jnp
        import numpy as np
        N_HEAD, D_MODEL, D_HEAD = (16, 128, 64)
        EPS = 1e-05
        SCALE = 1.0 / np.sqrt(D_HEAD)

        def _layer_norm(x, g, b):
            mu = jnp.mean(x, axis=-1, keepdims=True)
            var = jnp.mean(jnp.square(x - mu), axis=-1, keepdims=True)
            return (x - mu) * jax.lax.rsqrt(var + EPS) * g + b

        def _fast_weight_memory(q, k, v, beta):
            b, hn, l, d = q.shape
            qs = jnp.moveaxis(q, 2, 0)
            ks = jnp.moveaxis(k, 2, 0)
            vs = jnp.moveaxis(v, 2, 0)
            bs = jnp.moveaxis(beta, 2, 0)

            def step(W, xs):
                qt, kt, vt, bt = xs
                v_old = jnp.einsum('bhij,bhj->bhi', W, kt)
                delta = bt * (vt - v_old)
                W = W + delta[..., :, None] * kt[..., None, :]
                out = jnp.einsum('bhij,bhj->bhi', W, qt)
                return (W, out)
            W0 = jnp.zeros((b, hn, d, d), dtype=q.dtype)
            _, outs = jax.lax.scan(step, W0, (qs, ks, vs, bs))
            return jnp.moveaxis(outs, 0, 2)
        key = jax.random.key(seed)
        k1, k2, k3 = jax.random.split(key, 3)
        slen, bsz = (256, 4)
        h = jax.random.normal(k1, (slen, bsz, D_MODEL), dtype=jnp.float32)
        w_qkvb = jax.random.normal(k2, (N_HEAD * (3 * D_HEAD + 1), D_MODEL), dtype=jnp.float32) / np.sqrt(D_MODEL)
        w_o = jax.random.normal(k3, (D_MODEL, N_HEAD * D_HEAD), dtype=jnp.float32) / np.sqrt(N_HEAD * D_HEAD)
        ln_g = jnp.ones((D_MODEL,), dtype=jnp.float32)
        ln_b = jnp.zeros((D_MODEL,), dtype=jnp.float32)
        return {'h': h, 'w_qkvb': w_qkvb, 'w_o': w_o, 'ln_g': ln_g, 'ln_b': ln_b}
    _L0_attn_b_in = _L0_attn_b_setup()

    def _L0_ffn_setup():
        import jax, jax.numpy as jnp
        import numpy as np
        B, S, H, E, F = (2, 256, 128, 8, 512)
        key = jax.random.key(seed)
        k1, k2, k3, k4 = jax.random.split(key, 4)
        h = jax.random.normal(k1, (B, S, H), dtype=jnp.float32)
        Wr = jax.random.normal(k2, (H, E), dtype=jnp.float32) / np.sqrt(H)
        W1 = jax.random.normal(k3, (E, H, F), dtype=jnp.float32) / np.sqrt(H)
        W2 = jax.random.normal(k4, (E, F, H), dtype=jnp.float32) / np.sqrt(F)
        return {'h': h, 'Wr': Wr, 'W1': W1, 'W2': W2}
    _L0_ffn_in = _L0_ffn_setup()
    _d = {'L0_attn_a_x': _L0_attn_a_in['x'], 'L0_attn_a_W_qkv': _L0_attn_a_in['W_qkv'], 'L0_attn_a_RF': _L0_attn_a_in['RF'], 'L0_attn_a_W_out': _L0_attn_a_in['W_out'], 'L0_attn_a_b_out': _L0_attn_a_in['b_out'], 'L0_attn_b_w_qkvb': _L0_attn_b_in['w_qkvb'], 'L0_attn_b_w_o': _L0_attn_b_in['w_o'], 'L0_attn_b_ln_g': _L0_attn_b_in['ln_g'], 'L0_attn_b_ln_b': _L0_attn_b_in['ln_b'], 'L0_ffn_Wr': _L0_ffn_in['Wr'], 'L0_ffn_W1': _L0_ffn_in['W1'], 'L0_ffn_W2': _L0_ffn_in['W2']}
    _x0 = _d['L0_attn_a_x']
    _d['L0_attn_a_x'] = jax.random.normal(jax.random.fold_in(jax.random.key(seed), 1), (8, 512, 128), dtype=_x0.dtype)
    del _x0
    return _d

def reference(L0_attn_a_x, L0_attn_a_W_qkv, L0_attn_a_RF, L0_attn_a_W_out, L0_attn_a_b_out, L0_attn_b_w_qkvb, L0_attn_b_w_o, L0_attn_b_ln_g, L0_attn_b_ln_b, L0_ffn_Wr, L0_ffn_W1, L0_ffn_W2):

    def _L0_attn_a_ref(x, W_qkv, RF, W_out, b_out):
        import jax, jax.numpy as jnp
        import numpy as np
        import math
        B, N, DIM = (4, 512, 128)
        HEADS, DHEAD, NRF = (16, 64, 64)
        STAB = 1e-06

        def _phi(t, RF):
            return jax.nn.relu(jnp.einsum('bhnd,hdr->bhnr', t, RF))
        b, n, _ = x.shape
        qkv = x @ W_qkv
        q, k, v = jnp.split(qkv, 3, axis=-1)

        def to_heads(t):
            return t.reshape(b, n, HEADS, DHEAD).transpose(0, 2, 1, 3)
        q, k, v = (to_heads(q), to_heads(k), to_heads(v))
        phi_q = _phi(q, RF)
        phi_k = _phi(k, RF)
        kv = jnp.einsum('bhnr,bhnd->bhrd', phi_k, v)
        out = jnp.einsum('bhnr,bhrd->bhnd', phi_q, kv)
        k_sum = phi_k.sum(axis=2)
        normalizer = jnp.einsum('bhnr,bhr->bhn', phi_q, k_sum)[..., None] + STAB
        out = out / normalizer
        out = out.transpose(0, 2, 1, 3).reshape(b, n, HEADS * DHEAD)
        out = out @ W_out + b_out
        return out

    def _L0_attn_b_ref(h, w_qkvb, w_o, ln_g, ln_b):
        import jax, jax.numpy as jnp
        import numpy as np
        N_HEAD, D_MODEL, D_HEAD = (16, 128, 64)
        EPS = 1e-05
        SCALE = 1.0 / np.sqrt(D_HEAD)

        def _layer_norm(x, g, b):
            mu = jnp.mean(x, axis=-1, keepdims=True)
            var = jnp.mean(jnp.square(x - mu), axis=-1, keepdims=True)
            return (x - mu) * jax.lax.rsqrt(var + EPS) * g + b

        def _fast_weight_memory(q, k, v, beta):
            b, hn, l, d = q.shape
            qs = jnp.moveaxis(q, 2, 0)
            ks = jnp.moveaxis(k, 2, 0)
            vs = jnp.moveaxis(v, 2, 0)
            bs = jnp.moveaxis(beta, 2, 0)

            def step(W, xs):
                qt, kt, vt, bt = xs
                v_old = jnp.einsum('bhij,bhj->bhi', W, kt)
                delta = bt * (vt - v_old)
                W = W + delta[..., :, None] * kt[..., None, :]
                out = jnp.einsum('bhij,bhj->bhi', W, qt)
                return (W, out)
            W0 = jnp.zeros((b, hn, d, d), dtype=q.dtype)
            _, outs = jax.lax.scan(step, W0, (qs, ks, vs, bs))
            return jnp.moveaxis(outs, 0, 2)
        slen, bsz, _ = h.shape
        qkvb = (h @ w_qkvb.T).reshape(slen, bsz, N_HEAD, 3 * D_HEAD + 1)
        q, k, v, beta = jnp.split(qkvb, [D_HEAD, 2 * D_HEAD, 3 * D_HEAD], axis=-1)
        beta = jax.nn.sigmoid(beta)
        q = jnp.transpose(q, (1, 2, 0, 3))
        k = jnp.transpose(k, (1, 2, 0, 3))
        v = jnp.transpose(v, (1, 2, 0, 3))
        beta = jnp.transpose(beta, (1, 2, 0, 3))
        q = jax.nn.elu(q) + 1.0
        k = jax.nn.elu(k) + 1.0
        k = k / jnp.sum(k, axis=-1, keepdims=True)
        q = q / jnp.sum(q, axis=-1, keepdims=True)
        denom_acc = jnp.cumsum(k, axis=2)
        shifted = jnp.concatenate([jnp.zeros_like(denom_acc[:, :, :1]), denom_acc[:, :, :-1]], axis=2)
        key_denom = jnp.einsum('bhld,bhld->bhl', shifted, k)
        key_denom = jnp.concatenate([jnp.ones_like(key_denom[:, :, :1]), key_denom[:, :, 1:]], axis=2)[..., None]
        beta = beta * key_denom
        k = k / (key_denom + EPS)
        denominator = jnp.einsum('bhld,bhld->bhl', denom_acc, q)[..., None]
        layer_out = _fast_weight_memory(q, k, v, beta)
        layer_out = SCALE * layer_out / (denominator + EPS)
        layer_out = jnp.transpose(layer_out, (0, 2, 1, 3)).reshape(layer_out.shape[0], slen, N_HEAD * D_HEAD)
        layer_out = jnp.transpose(layer_out, (1, 0, 2))
        attn_out = layer_out @ w_o.T
        return _layer_norm(h + attn_out, ln_g, ln_b)

    def _L0_ffn_ref(h, Wr, W1, W2):
        import jax, jax.numpy as jnp
        import numpy as np
        B, S, H, E, F = (2, 256, 128, 8, 512)
        g = jax.nn.softmax(h @ Wr, axis=-1)
        top2_w, top2_idx = jax.lax.top_k(g, 2)
        top2_w = top2_w / jnp.sum(top2_w, axis=-1, keepdims=True)
        hid = jax.nn.relu(jnp.einsum('bsh,ehf->bsef', h, W1))
        expert_out = jnp.einsum('bsef,efh->bseh', hid, W2)
        top2_out = jnp.take_along_axis(expert_out, top2_idx[..., None], axis=2)
        return jnp.sum(top2_out * top2_w[..., None], axis=2)
    x = L0_attn_a_x
    x = x + _L0_attn_a_ref(_layernorm(x, axis=-1), L0_attn_a_W_qkv, L0_attn_a_RF, L0_attn_a_W_out, L0_attn_a_b_out)
    x = x + _L0_ffn_ref(_layernorm(x, axis=-1), L0_ffn_Wr, L0_ffn_W1, L0_ffn_W2)
    x = x + _L0_attn_b_ref(_layernorm(x, axis=-1), L0_attn_b_w_qkvb, L0_attn_b_w_o, L0_attn_b_ln_g, L0_attn_b_ln_b)
    x = x + _L0_ffn_ref(_layernorm(x, axis=-1), L0_ffn_Wr, L0_ffn_W1, L0_ffn_W2)
    return x

_drawn_inputs = setup_inputs


def setup_inputs(seed=0):
    import zlib

    import numpy as np

    out = dict(_drawn_inputs(seed))
    spreads = {'L0_attn_a_b_out': (0.0, 0.1), 'L0_attn_b_ln_g': (1.0, 0.2), 'L0_attn_b_ln_b': (0.0, 0.1)}
    factors = {}
    for name, (base, spread) in spreads.items():
        noise = np.random.default_rng([zlib.crc32(name.encode()), seed]).standard_normal(out[name].shape)
        drawn = base * np.exp(spread * noise) if base else spread * noise
        out[name] = jnp.asarray(drawn.astype(out[name].dtype))
    for name, factor in factors.items():
        out[name] = (out[name] * factor).astype(out[name].dtype)
    return out
```

```python
from contextlib import ExitStack

import concourse.bass as bass
from concourse import mybir

F32 = mybir.dt.float32
U32 = mybir.dt.uint32
ALU = mybir.AluOpType
ACT = mybir.ActivationFunctionType
AX_X = mybir.AxisListType.X

P = 128
BATCH, SEQ, DIM = 8, 512, 128
NT = SEQ // P
HEADS, DH = 16, 64
PAIRS = HEADS // 2
HD = HEADS * DH
STAB = 1e-6
LN_EPS = 1e-5
EPS = 1e-5
EXPERTS, FF = 8, 512
FC = FF // P
T = BATCH
NG = SEQ // P
TOK = P * T
BL = P // T
NTAU = P // BL
SCALE = float(DH) ** -0.5


class Kernel:

    def __init__(self, nc, ctx):
        self.nc, self.ctx = nc, ctx

    def sem(self, name):
        return self.ctx.enter_context(self.nc.semaphore(name))

    def sb(self, ctx, name, shape, dt=F32):
        return ctx.enter_context(self.nc.sbuf_tensor(name, shape, dt))

    def pb(self, ctx, name, shape=(P, 512), dt=F32):
        return ctx.enter_context(self.nc.psum_tensor(name, list(shape), dt))


def wait_apart(eng, sem, value, passed):
    eng.wait_ge(sem, value)
    eng.sem_inc(passed, 1)


class LayerNorm:

    def __init__(self, K, ctx, tag, n):
        self.n = n
        self.stats = K.sb(ctx, f"{tag}_stats", [P, n, 6])
        self.meanvar = K.sb(ctx, f"{tag}_meanvar", [P, n, 2])
        self.var_eps = K.sb(ctx, f"{tag}_var_eps", [P, n])
        self.rstd = K.sb(ctx, f"{tag}_rstd", [P, n])
        self.stats_step = K.sem(f"{tag}_stats_step")
        self.passed = K.sem(f"{tag}_passed")
        self.var_ready = K.sem(f"{tag}_var_ready")
        self.rstd_ready = K.sem(f"{tag}_rstd_ready")

    def statistics(self, dve, tiles, k, eps=LN_EPS):
        for n, x in enumerate(tiles):
            ins = dve.bn_stats(self.stats[:, n, :], x)
        ins.then_inc(self.stats_step, 1)
        wait_apart(dve, self.stats_step, 2 * k + 1, self.passed)
        for n in range(self.n):
            ins = dve.bn_aggr(self.meanvar[:, n, :], self.stats[:, n, :])
        ins.then_inc(self.stats_step, 1)
        dve.wait_ge(self.stats_step, 2 * k + 2)
        dve.tensor_scalar(self.var_eps[:, :], self.meanvar[:, :, 1], eps, None, ALU.add).then_inc(self.var_ready, 1)

    def root(self, pool, minus_half, k):
        pool.wait_ge(self.var_ready, k + 1)
        pool.tensor_tensor(self.rstd[:, :], self.var_eps[:, :], minus_half[:, 0:self.n], ALU.pow).then_inc(self.rstd_ready, 1)

    def apply(self, dve, tiles, outs, k):
        dve.wait_ge(self.rstd_ready, k + 1)
        for n, (x, o) in enumerate(zip(tiles, outs)):
            ins = dve.tensor_scalar(o, x, self.meanvar[:, n, 0:1], self.rstd[:, n:n + 1], ALU.subtract, ALU.mult)
        return ins


def load_and_fold_weights(K, C, A, inp):
    nc = K.nc
    with ExitStack() as ctx:
        w_qkv = K.sb(ctx, "w_qkv", [P, 3 * HD])
        w_qkvT = K.sb(ctx, "w_qkvT", [P, 3 * PAIRS, P])
        rf_blk = K.sb(ctx, "rf_blk", [P, PAIRS, 2, DH])
        wout_blk = K.sb(ctx, "wout_blk", [P, PAIRS, 2, DIM])
        b_rows = K.sb(ctx, "b_rows", [P, 3 * PAIRS, DIM])
        beta_rows = K.sb(ctx, "beta_rows", [HEADS, DIM])
        wo_rows = K.sb(ctx, "wo_rows", [P, HD])
        banks = [K.pb(ctx, f"w_bank{i}") for i in range(8)]

        x_in = K.sem("x_in")
        wqkv_in = K.sem("wqkv_in")
        blk_zero = K.sem("blk_zero")
        blk_in = K.sem("blk_in")
        brows_in = K.sem("brows_in")
        ident_step = K.sem("ident_step")
        masks_ready = K.sem("masks_ready")
        w_bank_full = K.sem("w_bank_full")
        w_bank_read = K.sem("w_bank_read")
        block = ctx.enter_context(nc.Block())

        fills = [("qkvT", i) for i in range(6)] + [("feat", i) for i in range(4)] + [("vo", i) for i in range(4)] \
            + [("bT", i) for i in range(6)] + [("betaT", 0)] + [("woT", i) for i in range(2)]

        @block.sync
        def _(sp):
            sp.dma_start(w_qkv[:, :], inp["W_qkv"]).then_inc(wqkv_in, 16)
            for t in range(BATCH):
                sp.dma_start(C["x"][:, t * NT:(t + 1) * NT, :],
                             inp["x"][t].rearrange("(g p) c -> p g c", p=P)).then_inc(x_in, 16)
            sp.dma_start(C["b_out"][:, :], inp["b_out"].partition_broadcast(P)).then_inc(x_in, 16)
            sp.dma_start(C["ln_g"][:, :], inp["ln_g"].partition_broadcast(P)).then_inc(x_in, 16)
            sp.dma_start(C["ln_b"][:, :], inp["ln_b"].partition_broadcast(P)).then_inc(x_in, 16)
            sp.dma_start(C["w_r"][:, :], inp["Wr"]).then_inc(x_in, 16)
            sp.wait_ge(x_in, 16 * (BATCH + 4))

        @block.scalar
        def _(act):
            act.wait_ge(blk_zero, 2)
            for hh in range(2):
                rows = slice(hh * DH, (hh + 1) * DH)
                act.dma_start(rf_blk[rows, :, hh, :], inp["RF"].rearrange("(p e) d r -> e d p r", e=2)[hh]).then_inc(blk_in, 16)
                act.dma_start(wout_blk[rows, :, hh, :],
                              inp["W_out"].rearrange("(p e d) c -> e d p c", e=2, d=DH)[hh]).then_inc(blk_in, 16)
            qkvb = inp["w_qkvb"].rearrange("(p e r) c -> e r p c", e=2, r=3 * DH + 1)
            for kind in range(3):
                for hh in range(2):
                    act.dma_start(b_rows[hh * DH:(hh + 1) * DH, kind * PAIRS:(kind + 1) * PAIRS, :],
                                  qkvb[hh, kind * DH:(kind + 1) * DH]).then_inc(brows_in, 16)
            act.dma_start(beta_rows[:, :], inp["w_qkvb"].rearrange("(h r) c -> h r c", h=HEADS)[:, 3 * DH, :]).then_inc(brows_in, 16)
            act.dma_start(wo_rows[:, :], inp["w_o"]).then_inc(brows_in, 16)
            for n, (kind, i) in enumerate(fills):
                act.wait_ge(w_bank_full, n + 1)
                b = banks[n % 8]
                if kind == "qkvT":
                    ins = act.copy(w_qkvT[:, 4 * i:4 * i + 4, :], b[:, :])
                elif kind == "feat":
                    dst = A["feat_q"] if i < 2 else A["feat_k"]
                    ins = act.copy(dst[:, (i % 2) * 512:(i % 2) * 512 + 512], b[:, :])
                elif kind == "vo":
                    ins = act.copy(A["vo"][:, 4 * i:4 * i + 4, :], b[:, :])
                elif kind == "bT":
                    dst, o = (C["b_qkT"], i) if i < 4 else (C["b_vT"], i - 4)
                    ins = act.copy(dst[:, o * 512:o * 512 + 512], b[:, :])
                elif kind == "betaT":
                    act.wait_ge(masks_ready, 1)
                    ins = act.copy(C["b_betaT"][:, 0:HEADS], b[:, 0:HEADS])
                else:
                    ins = act.copy(C["b_oT"][:, 4 * i:4 * i + 4, :], b[:, :])
                ins.then_inc(w_bank_read, 1)

        @block.gpsimd
        def _(pool):
            pool.memset(rf_blk[:, :, :, :], 0.0).then_inc(blk_zero, 1)
            pool.memset(wout_blk[:, :, :, :], 0.0).then_inc(blk_zero, 1)
            pool.memset(C["ident"][:, :], 0.0).then_inc(ident_step, 1)
            pool.wait_ge(ident_step, 1)
            pool.affine_select(out=C["ident"][:, :], in_=C["ident"][:, :], compare_op=ALU.not_equal, fill=1.0, base=0,
                               pattern=[[-1, P]], channel_multiplier=1).then_inc(ident_step, 1)

        @block.vector
        def _(dve):
            dve.memset(C["b_betaT"][:, :], 0.0).then_inc(masks_ready, 1)
            dve.memset(C["head_ind"][:, :, :, :], 0.0).then_inc(masks_ready, 1)
            dve.memset(A["ones"][:, :], 1.0)
            dve.memset(C["minus_half"][:, :], -0.5)
            for e in range(EXPERTS):
                dve.memset(C["expert_ids"][:, e:e + 1], float(e))
            dve.wait_ge(masks_ready, 2)
            for kind in range(2):
                for p in range(PAIRS):
                    for hh in range(2):
                        col = HEADS * kind + 2 * p + hh
                        dve.memset(C["head_ind"][hh * DH:(hh + 1) * DH, kind, p, col:col + 1], 1.0)

        @block.tensor
        def _(pe):
            pe.wait_ge(ident_step, 2)
            ident = C["ident"]
            for n, (kind, i) in enumerate(fills):
                b = banks[n % 8]
                if n >= 8:
                    pe.wait_ge(w_bank_read, n - 7)
                if kind == "qkvT":
                    if i == 0:
                        pe.wait_ge(wqkv_in, 16)
                    for j in range(4):
                        q = 4 * i + j
                        ins = pe.transpose(b[:, j * P:(j + 1) * P], w_qkv[:, q * P:(q + 1) * P], ident[:, :])
                elif kind == "feat":
                    if i == 0:
                        pe.wait_ge(blk_in, 64)
                    pe.wait_ge(w_bank_read, 6)
                    for j in range(4):
                        q = 4 * i + j
                        ins = pe.matmul(b[:, j * P:(j + 1) * P], w_qkvT[:, q, :], rf_blk[:, q % PAIRS, :, :],
                                        start=True, stop=True)
                elif kind == "vo":
                    for j in range(2):
                        q = 2 * i + j
                        ins = pe.matmul(b[:, j * 256:(j + 1) * 256], w_qkvT[:, 2 * PAIRS + q, :], wout_blk[:, q, :, :],
                                        start=True, stop=True)
                elif kind == "bT":
                    if i == 0:
                        pe.wait_ge(brows_in, 128)
                    for j in range(4):
                        ins = pe.transpose(b[:, j * P:(j + 1) * P], b_rows[:, 4 * i + j, :], ident[:, :])
                elif kind == "betaT":
                    ins = pe.transpose(b[:, 0:HEADS], beta_rows[:, :], ident[0:HEADS, 0:HEADS])
                else:
                    for j in range(4):
                        q = 4 * i + j
                        ins = pe.transpose(b[:, j * P:(j + 1) * P], wo_rows[:, q * P:(q + 1) * P], ident[:, :])
                ins.then_inc(w_bank_full, 1)


def linear_attention(K, C, A):
    nc = K.nc
    x = C["x"]
    with ExitStack() as ctx:
        xn = K.sb(ctx, "a_xn", [P, NT, DIM])
        xnT = K.sb(ctx, "a_xnT", [P, SEQ])
        phik = K.sb(ctx, "phik", [P, NT, HD])
        phik_sum = K.sb(ctx, "phik_sum", [P, HD])
        phiq = K.sb(ctx, "phiq", [P, NT, HD])
        phiqT = K.sb(ctx, "phiqT", [P, 2, PAIRS, P])
        kxT = K.sb(ctx, "kxT", [P, HD])
        kv = K.sb(ctx, "kv", [P, PAIRS, DIM])
        ksum = K.sb(ctx, "ksum", [P, HD])
        prod = K.sb(ctx, "a_prod", [P, HD])
        norm = K.sb(ctx, "a_norm", [P, HEADS])
        rnorm = K.sb(ctx, "a_rnorm", [P, 2, HEADS])
        ln = LayerNorm(K, ctx, "a_ln", NT)
        ring = [K.pb(ctx, f"a_ring{i}") for i in range(4)]
        kx_bank = [K.pb(ctx, f"a_kx{i}") for i in range(2)]
        y_bank = K.pb(ctx, "a_y")
        t_bank = K.pb(ctx, "a_t")

        xn_ready = K.sem("a_xn_ready")
        xnT_done = K.sem("a_xnT_done")
        xnT_ready = K.sem("a_xnT_ready")
        ring_full = K.sem("a_ring_full")
        act_read = K.sem("a_act_read")
        dve_read = K.sem("a_dve_read")
        presum_step = K.sem("a_presum_step")
        kx_done = K.sem("a_kx_done")
        kxT_ready = K.sem("a_kxT_ready")
        norm_step = K.sem("a_norm_step")
        rnorm_ready = K.sem("a_rnorm_ready")
        phiq_scaled = K.sem("a_phiq_scaled")
        bias_added = K.sem("a_bias_added")
        y_done = K.sem("a_y_done")
        y_added = K.sem("a_y_added")
        block = ctx.enter_context(nc.Block())

        KSUM, KV, PHIQT, FILLS = 16, 18, 20, 28
        ACT_READS, DVE_READS = 24, 4

        def tiles(t):
            return [x[:, t * NT + n, :] if isinstance(t, int) else
                    x[:, bass.ds(t * NT + n, 1), :].rearrange("p a c -> p (a c)") for n in range(NT)]

        def x_of(t):
            return x[:, t * NT:(t + 1) * NT, :] if isinstance(t, int) else x[:, bass.ds(t * NT, NT), :]

        xn_tiles = [xn[:, n, :] for n in range(NT)]

        @block.tensor
        def _(pe):
            def transposes(t):
                pe.wait_ge(xn_ready, t + 1)
                for n in range(NT):
                    ins = pe.transpose(t_bank[:, n * P:(n + 1) * P], xn[:, n, :], C["ident"][:, :])
                ins.then_inc(xnT_done, 1)

            def body(t, more):
                pe.wait_ge(xnT_ready, t + 1)
                for k in range(16):
                    if k >= 4:
                        pe.wait_ge(act_read, t * ACT_READS + k - 3)
                    n, half = k % 8 // 2, k % 2
                    w = A["feat_k"] if k < 8 else A["feat_q"]
                    pe.matmul(ring[k % 4][:, :], xnT[:, n * P:(n + 1) * P], w[:, half * 512:half * 512 + 512],
                              start=True, stop=True).then_inc(ring_full, 1)
                pe.wait_ge(presum_step, 3 * t + 3)
                for half in range(2):
                    pe.wait_ge(act_read, t * ACT_READS + 13 + half)
                    pe.matmul(ring[half][:, :], A["ones"][:, :], phik_sum[:, half * 512:half * 512 + 512],
                              start=True, stop=True).then_inc(ring_full, 1)
                for half in range(2):
                    for n in range(NT):
                        ins = pe.matmul(kx_bank[half][:, :], xn[:, n, :], phik[:, n, half * 512:half * 512 + 512],
                                        start=(n == 0), stop=(n == NT - 1))
                    ins.then_inc(kx_done, 1)
                pe.wait_ge(kxT_ready, 2 * t + 2)
                for q in range(2):
                    pe.wait_ge(act_read, t * ACT_READS + 15 + q)
                    for j in range(4):
                        for hh in range(2):
                            h = 2 * (4 * q + j) + hh
                            ins = pe.matmul(ring[2 + q][hh * DH:(hh + 1) * DH, j * P:(j + 1) * P],
                                            kxT[:, h * DH:(h + 1) * DH], A["vo"][:, h, :], start=True, stop=True)
                    ins.then_inc(ring_full, 1)

                def turn_phiq(n):
                    pe.wait_ge(phiq_scaled, t * NT + n + 1)
                    for q in range(2):
                        if n < 2:
                            pe.wait_ge(dve_read, t * DVE_READS + 2 * n + q + 1)
                        else:
                            pe.wait_ge(act_read, t * ACT_READS + 16 + 2 * (n - 2) + q + 1)
                        for j in range(4):
                            p = 4 * q + j
                            ins = pe.transpose(ring[(2 * n + q) % 4][:, j * P:(j + 1) * P], phiq[:, n, p * P:(p + 1) * P],
                                               C["ident"][:, :])
                        ins.then_inc(ring_full, 1)

                def output(n):
                    pe.wait_ge(act_read, t * ACT_READS + 16 + 2 * n + 2)
                    pe.wait_ge(dve_read, t * DVE_READS + 4)
                    for p in range(PAIRS):
                        ins = pe.matmul(y_bank[:, n * P:(n + 1) * P], phiqT[:, n % 2, p, :], kv[:, p, :],
                                        start=(p == 0), stop=(p == PAIRS - 1))
                    ins.then_inc(y_done, 1)

                turn_phiq(0)
                for n in range(NT):
                    if n + 1 < NT:
                        turn_phiq(n + 1)
                    elif more:
                        transposes(t + 1)
                    output(n)

            transposes(0)
            with pe.Fori(0, BATCH - 1) as t:
                body(t, True)
            body(BATCH - 1, False)

        @block.scalar
        def _(act):
            def copy_xnT(t):
                act.wait_ge(xnT_done, t + 1)
                act.copy(xnT[:, :], t_bank[:, :]).then_inc(xnT_ready, 1)

            def body(t, more):
                for k in range(16):
                    act.wait_ge(ring_full, t * FILLS + k + 1)
                    dst = phik if k < 8 else phiq
                    act.activation(dst[:, k % 8 // 2, (k % 2) * 512:(k % 2) * 512 + 512], ring[k % 4][:, :], ACT.Relu)\
                        .then_inc(act_read, 1)
                for n in range(NT):
                    for q in range(2):
                        act.wait_ge(ring_full, t * FILLS + PHIQT + 2 * n + q + 1)
                        if n >= 2 and q == 0:
                            act.wait_ge(y_done, t * NT + n - 1)
                        act.copy(phiqT[:, n % 2, 4 * q:4 * q + 4, :],
                                 ring[(2 * n + q) % 4][:, :].rearrange("p (a c) -> p a c", a=4)).then_inc(act_read, 1)
                if more:
                    copy_xnT(t + 1)

            copy_xnT(0)
            with act.Fori(0, BATCH - 1) as t:
                body(t, True)
            body(BATCH - 1, False)

        @block.gpsimd
        def _(pool):
            def body(t, more):
                pool.wait_ge(act_read, t * ACT_READS + 4)
                pool.tensor_tensor(phik_sum[:, :], phik[:, 0, :], phik[:, 1, :], ALU.add).then_inc(presum_step, 1)
                for n in range(2, NT):
                    pool.wait_ge(act_read, t * ACT_READS + 2 * n + 2)
                    pool.wait_ge(presum_step, 3 * t + n - 1)
                    pool.tensor_tensor(phik_sum[:, :], phik_sum[:, :], phik[:, n, :], ALU.add).then_inc(presum_step, 1)
                pool.wait_ge(xn_ready, t + 1)
                pool.tensor_tensor(x_of(t), x_of(t), C["b_out"][:, :].unsqueeze(1).to_broadcast([P, NT, DIM]), ALU.add)\
                    .then_inc(bias_added, 1)
                for n in range(NT):
                    pool.wait_ge(rnorm_ready, t * NT + n + 1)
                    by_head = phiq[:, n, :].rearrange("p (h r) -> p h r", h=HEADS)
                    pool.tensor_tensor(by_head, by_head, rnorm[:, n % 2, :].unsqueeze(2).to_broadcast([P, HEADS, DH]),
                                       ALU.mult).then_inc(phiq_scaled, 1)
                    if more and n == 2:
                        ln.root(pool, C["minus_half"], t + 1)

            ln.root(pool, C["minus_half"], 0)
            with pool.Fori(0, BATCH - 1) as t:
                body(t, True)
            body(BATCH - 1, False)

        @block.vector
        def _(dve):
            def body(t, more):
                for half in range(2):
                    dve.wait_ge(ring_full, t * FILLS + KSUM + half + 1)
                    dve.tensor_copy(ksum[:, half * 512:half * 512 + 512], ring[half][:, :]).then_inc(dve_read, 1)
                dve.wait_ge(dve_read, t * DVE_READS + 2)

                def normalizer(n):
                    dve.wait_ge(act_read, t * ACT_READS + 8 + 2 * n + 2)
                    dve.tensor_tensor(prod[:, :], phiq[:, n, :], ksum[:, :], ALU.mult).then_inc(norm_step, 1)
                    dve.wait_ge(norm_step, (t * NT + n) * 3 + 1)
                    dve.tensor_reduce(norm[:, :], prod[:, :].rearrange("p (h r) -> p h r", h=HEADS), AX_X, ALU.add)\
                        .then_inc(norm_step, 1)
                    dve.wait_ge(norm_step, (t * NT + n) * 3 + 2)
                    dve.tensor_scalar(norm[:, :], norm[:, :], STAB, None, ALU.add).then_inc(norm_step, 1)
                    dve.wait_ge(norm_step, (t * NT + n) * 3 + 3)
                    if n >= 2:
                        dve.wait_ge(phiq_scaled, t * NT + n - 1)
                    dve.reciprocal(rnorm[:, n % 2, :], norm[:, :]).then_inc(rnorm_ready, 1)

                normalizer(0)
                normalizer(1)
                for half in range(2):
                    dve.wait_ge(kx_done, 2 * t + half + 1)
                    dve.tensor_copy(kxT[:, half * 512:half * 512 + 512], kx_bank[half][:, :]).then_inc(kxT_ready, 1)
                normalizer(2)
                for q in range(2):
                    dve.wait_ge(ring_full, t * FILLS + KV + q + 1)
                    dve.tensor_copy(kv[:, 4 * q:4 * q + 4, :], ring[2 + q][:, :].rearrange("p (a c) -> p a c", a=4))\
                        .then_inc(dve_read, 1)
                if more:
                    ln.statistics(dve, tiles(t + 1), t + 1)
                normalizer(3)
                if more:
                    ln.apply(dve, tiles(t + 1), xn_tiles, t + 1).then_inc(xn_ready, 1)
                dve.wait_ge(y_done, (t + 1) * NT)
                dve.wait_ge(bias_added, t + 1)
                dve.tensor_tensor(x_of(t), x_of(t), y_bank[:, :].rearrange("p (a c) -> p a c", a=NT), ALU.add)\
                    .then_inc(y_added, 1)

            ln.statistics(dve, tiles(0), 0)
            ln.apply(dve, tiles(0), xn_tiles, 0).then_inc(xn_ready, 1)
            with dve.Fori(0, BATCH - 1) as t:
                body(t, True)
            body(BATCH - 1, False)


def expert_ffn(K, C, tag, inp, out=None):
    nc = K.nc
    x = C["x"]
    with ExitStack() as ctx:
        w1 = K.sb(ctx, f"{tag}_w1", [P, EXPERTS, FF])
        w2 = K.sb(ctx, f"{tag}_w2", [P, EXPERTS, FC, DIM])
        xn = K.sb(ctx, f"{tag}_xn", [P, NT, DIM])
        xnT = K.sb(ctx, f"{tag}_xnT", [P, SEQ])
        hidT = K.sb(ctx, f"{tag}_hidT", [P, 2, FC, SEQ])
        logits = K.sb(ctx, f"{tag}_logits", [P, NT, EXPERTS])
        best = K.sb(ctx, f"{tag}_best", [P, NT, 8])
        best_id = K.sb(ctx, f"{tag}_best_id", [P, NT, 8], U32)
        best_idf = K.sb(ctx, f"{tag}_best_idf", [P, NT, 2])
        gap = K.sb(ctx, f"{tag}_gap", [P, NT])
        ratio = K.sb(ctx, f"{tag}_ratio", [P, NT])
        denom = K.sb(ctx, f"{tag}_denom", [P, NT])
        weight = K.sb(ctx, f"{tag}_weight", [P, 2, NT])
        picked = K.sb(ctx, f"{tag}_picked", [P, 2, NT, EXPERTS])
        gates = K.sb(ctx, f"{tag}_gates", [P, BATCH * NT, EXPERTS])
        ln = LayerNorm(K, ctx, f"{tag}_ln", NT)
        hid_bank = [K.pb(ctx, f"{tag}_hid{i}") for i in range(FC)]
        y_bank = [K.pb(ctx, f"{tag}_y{i}") for i in range(2)]
        t_bank = K.pb(ctx, f"{tag}_t")
        l_bank = K.pb(ctx, f"{tag}_l")

        w_in = K.sem(f"{tag}_w_in")
        xn_ready = K.sem(f"{tag}_xn_ready")
        xnT_done = K.sem(f"{tag}_xnT_done")
        xnT_ready = K.sem(f"{tag}_xnT_ready")
        logits_done = K.sem(f"{tag}_logits_done")
        gap_ready = K.sem(f"{tag}_gap_ready")
        ratio_ready = K.sem(f"{tag}_ratio_ready")
        route_step = K.sem(f"{tag}_route_step")
        hid_done = K.sem(f"{tag}_hid_done")
        hid_ready = K.sem(f"{tag}_hid_ready")
        y_done = K.sem(f"{tag}_y_done")
        y_added = K.sem(f"{tag}_y_added")
        x_stored = K.sem(f"{tag}_x_stored")
        block = ctx.enter_context(nc.Block())

        def tiles(t):
            return [x[:, bass.ds(t * NT + n, 1), :].rearrange("p a c -> p (a c)") for n in range(NT)] \
                if not isinstance(t, int) else [x[:, t * NT + n, :] for n in range(NT)]

        def gates_of(t):
            return gates[:, t * NT:(t + 1) * NT, :] if isinstance(t, int) else gates[:, bass.ds(t * NT, NT), :]

        xn_tiles = [xn[:, n, :] for n in range(NT)]
        ROUTE = 9

        @block.sync
        def _(sp):
            for e in range(EXPERTS):
                sp.dma_start(w1[:, e, :], inp["W1"][e]).then_inc(w_in, 16)
                sp.dma_start(w2[:, e, :, :], inp["W2"][e].rearrange("(a p) c -> p a c", p=P)).then_inc(w_in, 16)
            if out is not None:
                for t in range(BATCH):
                    sp.wait_ge(y_added, (t + 1) * EXPERTS)
                    sp.dma_start(out[t].rearrange("(g p) c -> p g c", p=P), x[:, t * NT:(t + 1) * NT, :])\
                        .then_inc(x_stored, 16)
                sp.wait_ge(x_stored, 16 * BATCH)

        @block.gpsimd
        def _(pool):
            with pool.Fori(0, BATCH) as t:
                ln.root(pool, C["minus_half"], t)

        @block.tensor
        def _(pe):
            def transposes(t):
                pe.wait_ge(xn_ready, t + 1)
                for n in range(NT):
                    ins = pe.transpose(t_bank[:, n * P:(n + 1) * P], xn[:, n, :], C["ident"][:, :])
                ins.then_inc(xnT_done, 1)

            def router(t):
                pe.wait_ge(xnT_ready, t + 1)
                for n in range(NT):
                    ins = pe.matmul(l_bank[:, n * EXPERTS:(n + 1) * EXPERTS], xnT[:, n * P:(n + 1) * P], C["w_r"][:, :],
                                    start=True, stop=True)
                ins.then_inc(logits_done, 1)

            def hidden(t, e):
                for f in range(FC):
                    if e >= 1:
                        pe.wait_ge(hid_ready, (t * EXPERTS + e - 1) * FC + f + 1)
                    pe.matmul(hid_bank[f][:, :], w1[:, e, f * P:(f + 1) * P], xnT[:, :], start=True, stop=True)\
                        .then_inc(hid_done, 1)

            def expert_out(t, e):
                if e >= 2:
                    pe.wait_ge(y_added, t * EXPERTS + e - 1)
                pe.wait_ge(hid_ready, (t * EXPERTS + e + 1) * FC)
                for n in range(NT):
                    for f in range(FC):
                        ins = pe.matmul(y_bank[e % 2][:, n * P:(n + 1) * P], hidT[:, e % 2, f, n * P:(n + 1) * P],
                                        w2[:, e, f, :], start=(f == 0), stop=(f == FC - 1))
                ins.then_inc(y_done, 1)

            def body(t, more):
                hidden(t, 0)
                for e in range(EXPERTS):
                    if e + 1 < EXPERTS:
                        hidden(t, e + 1)
                    if more and e == EXPERTS - 2:
                        transposes(t + 1)
                    if more and e == EXPERTS - 1:
                        router(t + 1)
                    expert_out(t, e)
                pe.wait_ge(y_added, t * EXPERTS + EXPERTS)

            transposes(0)
            pe.wait_ge(w_in, 32 * EXPERTS)
            router(0)
            with pe.Fori(0, BATCH - 1) as t:
                body(t, True)
            body(BATCH - 1, False)

        @block.scalar
        def _(act):
            def copy_xnT(t):
                act.wait_ge(xnT_done, t + 1)
                act.copy(xnT[:, :], t_bank[:, :]).then_inc(xnT_ready, 1)

            def softmax_ratio(t):
                act.wait_ge(gap_ready, t + 1)
                act.activation(ratio[:, :], gap[:, :], ACT.Exp).then_inc(ratio_ready, 1)

            def body(t, more):
                for e in range(EXPERTS):
                    for f in range(FC):
                        act.wait_ge(hid_done, (t * EXPERTS + e) * FC + f + 1)
                        if e >= 2 and f == 0:
                            act.wait_ge(y_done, t * EXPERTS + e - 1)
                        act.activation(hidT[:, e % 2, f, :], hid_bank[f][:, :], ACT.Relu).then_inc(hid_ready, 1)
                if more:
                    copy_xnT(t + 1)
                    softmax_ratio(t + 1)

            copy_xnT(0)
            softmax_ratio(0)
            with act.Fori(0, BATCH - 1) as t:
                body(t, True)
            body(BATCH - 1, False)

        @block.vector
        def _(dve):
            def normalize(t):
                ln.statistics(dve, tiles(t), t)
                ln.apply(dve, tiles(t), xn_tiles, t).then_inc(xn_ready, 1)

            def route(t):
                step = [0]

                def then(ins):
                    step[0] += 1
                    ins.then_inc(route_step, 1)
                    dve.wait_ge(route_step, t * ROUTE + step[0])

                dve.wait_ge(logits_done, t + 1)
                then(dve.tensor_copy(logits[:, :, :], l_bank[:, 0:NT * EXPERTS].rearrange("p (a e) -> p a e", a=NT)))
                wait_apart(dve, route_step, t * ROUTE + 1, ln.passed)
                for n in range(NT):
                    ins = dve.max(best[:, n, :], logits[:, n, :])
                then(ins)
                wait_apart(dve, route_step, t * ROUTE + 2, ln.passed)
                for n in range(NT):
                    dve.max_index(best_id[:, n, :], best[:, n, :], logits[:, n, :])
                ins = dve.tensor_tensor(gap[:, :], best[:, :, 1], best[:, :, 0], ALU.subtract)
                ins.then_inc(gap_ready, 1)
                dve.wait_ge(gap_ready, t + 1)
                then(dve.tensor_copy(best_idf[:, :, :], best_id[:, :, 0:2]))
                dve.wait_ge(ratio_ready, t + 1)
                then(dve.tensor_scalar(denom[:, :], ratio[:, :], 1.0, None, ALU.add))
                then(dve.reciprocal(weight[:, 0, :], denom[:, :]))
                then(dve.tensor_tensor(weight[:, 1, :], weight[:, 0, :], ratio[:, :], ALU.mult))
                for k in range(2):
                    ins = dve.tensor_tensor(picked[:, k, :, :],
                                            C["expert_ids"][:, :].unsqueeze(1).to_broadcast([P, NT, EXPERTS]),
                                            best_idf[:, :, k:k + 1].to_broadcast([P, NT, EXPERTS]), ALU.is_equal)
                then(ins)
                for k in range(2):
                    ins = dve.tensor_tensor(picked[:, k, :, :], picked[:, k, :, :],
                                            weight[:, k, :].unsqueeze(2).to_broadcast([P, NT, EXPERTS]), ALU.mult)
                then(ins)
                then(dve.tensor_tensor(gates_of(t), picked[:, 0, :, :], picked[:, 1, :, :], ALU.add))
                assert step[0] == ROUTE

            def body(t, more):
                for e in range(EXPERTS):
                    if more and e == 5:
                        normalize(t + 1)
                    dve.wait_ge(y_done, t * EXPERTS + e + 1)
                    for n in range(NT):
                        xt = tiles(t)[n]
                        gate = gates[:, t * NT + n, e:e + 1] if isinstance(t, int) else \
                            gates[:, bass.ds(t * NT + n, 1), e:e + 1].rearrange("p a c -> p (a c)")
                        ins = dve.scalar_tensor_tensor(out=xt, in0=y_bank[e % 2][:, n * P:(n + 1) * P], scalar=gate,
                                                       in1=xt, op0=ALU.mult, op1=ALU.add)
                    ins.then_inc(y_added, 1)
                    dve.wait_ge(y_added, t * EXPERTS + e + 1)
                if more:
                    route(t + 1)

            normalize(0)
            route(0)
            with dve.Fori(0, BATCH - 1) as t:
                body(t, True)
            body(BATCH - 1, False)


def delta_memory(K, C, cd, gd):
    nc = K.nc
    x = C["x"]
    with ExitStack() as ctx:
        h = K.sb(ctx, "b_h", [P, T, DIM])
        hT = K.sb(ctx, "b_hT", [P, TOK])
        pos_exp = K.sb(ctx, "b_exp", [P, 2, 512])
        pos_rel = K.sb(ctx, "b_rel", [P, 2, 512])
        kq = K.sb(ctx, "b_kq", [P, 2, 2, TOK])
        gram = K.sb(ctx, "b_gram", [P, NTAU, 32, 2, HEADS])
        outT = gram[:, :, :, :, :].rearrange("p a b c d -> p (a b c d)").rearrange("p (a n) -> p a n", a=PAIRS)
        v = K.sb(ctx, "b_v", [P, NTAU, HD])
        coef = K.sb(ctx, "b_coef", [P, T, T, 2, HEADS])
        sums_raw = K.sb(ctx, "b_sums_raw", [P, 2, T, 32])
        sums = K.sb(ctx, "b_sums", [P, 2, T, 2, HEADS])
        rsum = K.sb(ctx, "b_rsum", [P, T, 2, HEADS])
        den = K.sb(ctx, "b_den", [P, T, 2, HEADS])
        rden = K.sb(ctx, "b_rden", [P, T, 2, HEADS])
        beta = K.sb(ctx, "b_beta", [P, T, HEADS])
        gamma = K.sb(ctx, "b_gamma", [P, T, HEADS])
        alpha = K.sb(ctx, "b_alpha", [P, T, HEADS])
        inv = K.sb(ctx, "b_inv", [P, T, T, HEADS])
        prod = K.sb(ctx, "b_prod", [P, T, T, HEADS])
        mix = K.sb(ctx, "b_mix", [P, T, T, HEADS])
        spread = K.sb(ctx, "b_spread", [P, NTAU // 2, BL * T, HEADS])
        ln = LayerNorm(K, ctx, "b_ln", T)
        ring = [K.pb(ctx, f"b_ring{i}") for i in range(4)]
        g_bank = [K.pb(ctx, f"b_g{i}") for i in range(2)]
        s_bank = K.pb(ctx, "b_s")

        names = ["h_ready", "ring_full", "act_read", "dve_read", "exp_read", "rel_read", "hT_ready", "v_ready",
                 "kq_ready", "gram_done", "gram_read0", "gram_read1", "sums_done", "beta_exp", "beta_logit", "solve_step",
                 "gram_stored", "coef_loaded", "mix_stored", "spread_loaded", "spread_zero",
                 "outT_ready", "resid_step", "x_ready", "pe_passed"]
        S = {n: K.sem(f"b_{n}") for n in names}
        block = ctx.enter_context(nc.Block())

        HT, V, KQ, MIXED, ATT = 0, 2, 18, 50, 66
        FILLS = 68
        HALVES = 2
        STEPS = 50

        def x_tile(g, t):
            return x[:, bass.ds(g + t * NG, 1), :].rearrange("p a c -> p (a c)")

        @block.sync
        def _(sp):
            with sp.Fori(0, NG) as g:
                sp.wait_ge(S["gram_read0"], g * PAIRS + PAIRS)
                sp.wait_ge(S["gram_read1"], g * PAIRS + PAIRS)
                for b in range(BL):
                    sp.dma_start(gd.rearrange("(a b) s n -> b s a n", b=BL)[b],
                                 gram[b * T:(b + 1) * T, :, (b % 4) * T:(b % 4 + 1) * T, :, :]
                                 .rearrange("p a t k h -> p a (t k h)")).then_inc(S["gram_stored"], 16)
                sp.wait_ge(S["gram_stored"], (g + 1) * 16 * BL)
                sp.dma_start(coef[:, :, :, :, :].rearrange("p s t k h -> p (s t k h)"), gd.rearrange("b s n -> b (s n)"))\
                    .then_inc(S["coef_loaded"], 16)
                sp.wait_ge(S["solve_step"], (g + 1) * STEPS)
                sp.dma_start(cd.rearrange("b u n -> b (u n)"), mix[:, :, :, :].rearrange("p u t h -> p (u t h)"))\
                    .then_inc(S["mix_stored"], 16)
                sp.wait_ge(S["mix_stored"], (g + 1) * 16)
                for q in range(HALVES):
                    if q == 1:
                        sp.wait_ge(S["outT_ready"], g * 16 + 8)
                    for b in range(BL):
                        sp.dma_start(spread[b * T:(b + 1) * T, :, b * T:(b + 1) * T, :].rearrange("p a t h -> p a (t h)"),
                                     cd.rearrange("(q a b) u n -> q b u a n", q=HALVES, b=BL)[q, b])\
                            .then_inc(S["spread_loaded"], 16)

        @block.gpsimd
        def _(pool):
            with pool.Fori(0, 2 * NG) as k:
                ln.root(pool, C["minus_half"], k)

        @block.tensor
        def _(pe):
            with pe.Fori(0, NG) as g:
                pe.wait_ge(S["h_ready"], g + 1)
                for q in range(2):
                    for j in range(4):
                        ins = pe.transpose(ring[q][:, j * P:(j + 1) * P], h[:, 4 * q + j, :], C["ident"][:, :])
                    ins.then_inc(S["ring_full"], 1)
                pe.wait_ge(S["hT_ready"], 2 * g + 2)
                for j in range(4):
                    pe.matmul(s_bank[32 * j:32 * j + 32, 256:512], C["b_betaT"][:, :], hT[:, 256 * j:256 * j + 256],
                              start=True, stop=True)
                for k in range(16):
                    if k >= 4:
                        pe.wait_ge(S["v_ready"], 16 * g + k - 3)
                    pe.matmul(ring[(V + k) % 4][:, :], hT[:, (k // 2) * P:(k // 2 + 1) * P],
                              C["b_vT"][:, (k % 2) * 512:(k % 2) * 512 + 512], start=True, stop=True)\
                        .then_inc(S["ring_full"], 1)

                def project(p):
                    for k in range(4):
                        n = 4 * p + k
                        if n < 4:
                            pe.wait_ge(S["v_ready"], 16 * g + 13 + n)
                        else:
                            pe.wait_ge(S["rel_read"], 32 * g + n - 3)
                        kind, half = k // 2, k % 2
                        w = C["b_qkT"][:, (1 - kind) * HD + p * P:(1 - kind) * HD + (p + 1) * P]
                        pe.matmul(ring[(KQ + n) % 4][:, :], w, hT[:, half * 512:half * 512 + 512], start=True, stop=True)\
                            .then_inc(S["ring_full"], 1)

                def products(p):
                    pe.wait_ge(S["kq_ready"], 32 * g + 4 * p + 4)
                    for kind in range(2):
                        for j in range(4):
                            pe.matmul(s_bank[32 * j:32 * j + 32, 0:256], C["head_ind"][:, kind, p, :],
                                      kq[:, p % 2, kind, 256 * j:256 * j + 256], start=(p == 0 and kind == 0),
                                      stop=(p == PAIRS - 1 and kind == 1), skip_group_check=True)
                    if p >= 1:
                        pe.wait_ge(S["gram_read0"], PAIRS * g + p)
                        pe.wait_ge(S["gram_read1"], PAIRS * g + p)
                    wait_apart(pe, S["kq_ready"], 32 * g + 4 * p + 4, S["pe_passed"])
                    for a in range(NTAU):
                        for j in range(4):
                            c = (4 * a + j) * 32
                            for hh in range(2):
                                r = slice(hh * DH, (hh + 1) * DH)
                                ins = pe.matmul(g_bank[hh][32 * j:32 * j + 32, a * 64:(a + 1) * 64],
                                                kq[r, p % 2, 0, c:c + 32], kq[r, p % 2, :, c:c + 32], start=True, stop=True)
                    ins.then_inc(S["gram_done"], 1)

                project(0)
                for p in range(PAIRS):
                    if p + 1 < PAIRS:
                        project(p + 1)
                    products(p)

                for q in range(HALVES):
                    pe.wait_ge(S["spread_loaded"], (g * HALVES + q + 1) * 16 * BL)
                    for p in range(PAIRS):
                        n = q * PAIRS + p
                        if n < 4:
                            pe.wait_ge(S["rel_read"], 32 * g + 32)
                        else:
                            pe.wait_ge(S["outT_ready"], 16 * g + n - 3)
                        for a in range(NTAU // 2):
                            for hh in range(2):
                                hd = (2 * p + hh) * DH
                                ins = pe.matmul(ring[(MIXED + n) % 4][hh * DH:(hh + 1) * DH, a * P:(a + 1) * P],
                                                v[:, q * 4 + a, hd:hd + DH], spread[:, a, :, 2 * p + hh],
                                                start=True, stop=True)
                        ins.then_inc(S["ring_full"], 1)
                pe.wait_ge(S["outT_ready"], 16 * g + 16)
                for q in range(2):
                    for j in range(4):
                        t = 4 * q + j
                        for p in range(PAIRS):
                            ins = pe.matmul(ring[(ATT + q) % 4][:, j * P:(j + 1) * P], outT[:, p, t::T], C["b_oT"][:, p, :],
                                            start=(p == 0), stop=(p == PAIRS - 1))
                    ins.then_inc(S["ring_full"], 1)

        @block.scalar
        def _(act):
            with act.Fori(0, NG) as g:
                for q in range(2):
                    act.wait_ge(S["ring_full"], g * FILLS + q + 1)
                    act.copy(hT[:, :].rearrange("c (b t) -> c t b", t=T)[:, 4 * q:4 * q + 4, :],
                             ring[q][:, :].rearrange("c (t b) -> c t b", t=4)).then_inc(S["hT_ready"], 1)
                for k in range(16):
                    act.wait_ge(S["ring_full"], g * FILLS + V + k + 1)
                    act.copy(v[:, k // 2, (k % 2) * 512:(k % 2) * 512 + 512], ring[(V + k) % 4][:, :]).then_inc(S["v_ready"], 1)

                def gram_copy(p):
                    act.wait_ge(S["gram_done"], g * PAIRS + p + 1)
                    act.copy(gram[:, :, :, :, 2 * p].rearrange("p a b k -> p a k b"),
                             g_bank[0][:, :].rearrange("p (a k b) -> p a k b", a=NTAU, k=2)).then_inc(S["gram_read0"], 1)

                for n in range(32):
                    act.wait_ge(S["ring_full"], g * FILLS + KQ + n + 1)
                    if n >= 2:
                        act.wait_ge(S["kq_ready"], g * 32 + n - 1)
                    act.activation(pos_exp[:, n % 2, :], ring[(KQ + n) % 4][:, :], ACT.Exp).then_inc(S["exp_read"], 1)
                    act.activation(pos_rel[:, n % 2, :], ring[(KQ + n) % 4][:, :], ACT.Relu).then_inc(S["rel_read"], 1)
                    if n % 4 == 3 and n > 4:
                        gram_copy(n // 4 - 1)
                gram_copy(PAIRS - 1)
                act.wait_ge(S["beta_logit"], g + 1)
                act.activation(beta[:, :, :], sums[:, 1, :, 0, :], ACT.Exp, scale=-1.0).then_inc(S["beta_exp"], 1)
                for n in range(16):
                    act.wait_ge(S["ring_full"], g * FILLS + MIXED + n + 1)
                    q, p = n // PAIRS, n % PAIRS
                    act.copy(outT[:, p, q * 512:(q + 1) * 512], ring[(MIXED + n) % 4][:, :]).then_inc(S["outT_ready"], 1)

        @block.vector
        def _(dve):
            dve.memset(spread[:, :, :, :], 0.0)
            dve.memset(inv[:, :, :, :], 0.0)
            dve.memset(mix[:, :, :, :], 0.0).then_inc(S["spread_zero"], 1)
            with dve.Fori(0, NG) as g:
                x_tiles = [x_tile(g, t) for t in range(T)]
                h_tiles = [h[:, t, :] for t in range(T)]
                ln.statistics(dve, x_tiles, 2 * g)
                ln.apply(dve, x_tiles, h_tiles, 2 * g).then_inc(S["h_ready"], 1)

                def gram_copy(p):
                    dve.wait_ge(S["gram_done"], g * PAIRS + p + 1)
                    dve.tensor_copy(gram[:, :, :, :, 2 * p + 1].rearrange("p a b k -> p a k b"),
                                    g_bank[1][:, :].rearrange("p (a k b) -> p a k b", a=NTAU, k=2))\
                        .then_inc(S["gram_read1"], 1)

                for n in range(32):
                    dve.wait_ge(S["rel_read"], g * 32 + n + 1)
                    p, k = n // 4, n % 4
                    if p >= 2 and k == 0:
                        dve.wait_ge(S["gram_done"], g * PAIRS + p - 1)
                    dve.scalar_tensor_tensor(out=kq[:, p % 2, k // 2, (k % 2) * 512:(k % 2) * 512 + 512],
                                             in0=pos_exp[:, n % 2, :], scalar=1.0, in1=pos_rel[:, n % 2, :],
                                             op0=ALU.min, op1=ALU.add).then_inc(S["kq_ready"], 1)
                    if k == 3 and p >= 1:
                        gram_copy(p - 1)
                gram_copy(PAIRS - 1)

                step = [0]

                def then(ins):
                    step[0] += 1
                    ins.then_inc(S["solve_step"], 1)
                    dve.wait_ge(S["solve_step"], g * STEPS + step[0])

                then(dve.tensor_copy(sums_raw[:, :, :, :], s_bank[:, :].rearrange("p (a b t) -> p a t b", a=2, t=T)))
                ins = dve.transpose(sums[:, :, :, :, :].rearrange("p a t k h -> p (a t k h)"),
                                    sums_raw[:, :, :, :].rearrange("p a t b -> p (a t b)"))
                ins.then_inc(S["beta_logit"], 1)
                dve.wait_ge(S["beta_logit"], g + 1)
                then(dve.reciprocal(rsum[:, :, :, :], sums[:, 0, :, :, :]))
                dve.wait_ge(S["coef_loaded"], (g + 1) * 16)
                by_s = coef[:, :, :, :, :].rearrange("p s t k h -> p s (t k h)")
                then(dve.tensor_tensor(by_s, by_s, rsum[:, :, :, :].rearrange("p t k h -> p (t k h)").unsqueeze(1)
                                       .to_broadcast([P, T, T * 2 * HEADS]), ALU.mult))
                by_tk = coef[:, :, :, :, :].rearrange("p s t k h -> p s (t k) h")
                then(dve.tensor_tensor(by_tk, by_tk, rsum[:, :, 0, :].unsqueeze(2).to_broadcast([P, T, 2 * T, HEADS]), ALU.mult))
                dve.memset(den[:, 0, 0, :], 1.0)
                dve.tensor_copy(den[:, 0, 1, :], coef[:, 0, 0, 1, :])
                then(dve.tensor_copy(den[:, 1:T, :, :], coef[:, 0, 1:T, :, :]))
                for s in range(1, T - 1):
                    then(dve.tensor_tensor(den[:, s + 1:T, :, :], den[:, s + 1:T, :, :], coef[:, s, s + 1:T, :, :], ALU.add))
                diag = coef[:, :, :, 1, :].rearrange("p s t h -> p (s t) h")[:, T + 1::T + 1, :]
                then(dve.tensor_tensor(den[:, 1:T, 1, :], den[:, 1:T, 1, :], diag, ALU.add))
                then(dve.tensor_scalar(rden[:, :, :, :], den[:, :, :, :], EPS, None, ALU.add))
                then(dve.reciprocal(rden[:, :, :, :], rden[:, :, :, :]))
                dve.wait_ge(S["beta_exp"], g + 1)
                then(dve.tensor_scalar(beta[:, :, :], beta[:, :, :], 1.0, None, ALU.add))
                then(dve.reciprocal(beta[:, :, :], beta[:, :, :]))
                then(dve.tensor_tensor(gamma[:, :, :], beta[:, :, :], den[:, :, 0, :], ALU.mult))
                then(dve.tensor_tensor(gamma[:, :, :], gamma[:, :, :], rden[:, :, 0, :], ALU.mult))
                dve.tensor_copy(inv[:, :, :, :].rearrange("p t u h -> p (t u) h")[:, ::T + 1, :], gamma[:, :, :])
                dve.tensor_scalar(rden[:, :, 1, :], rden[:, :, 1, :], SCALE, None, ALU.mult)
                then(dve.scalar_tensor_tensor(out=alpha[:, :, :], in0=gamma[:, :, :], scalar=-1.0, in1=rden[:, :, 0, :],
                                              op0=ALU.mult, op1=ALU.mult))
                dve.tensor_tensor(coef[:, :, :, 0, :], coef[:, :, :, 0, :], alpha[:, :, :].unsqueeze(1)
                                  .to_broadcast([P, T, T, HEADS]), ALU.mult)
                then(dve.tensor_tensor(coef[:, :, :, 1, :], coef[:, :, :, 1, :], rden[:, :, 1, :].unsqueeze(1)
                                       .to_broadcast([P, T, T, HEADS]), ALU.mult))
                for t in range(1, T):
                    then(dve.tensor_tensor(prod[:, 0:t, 0:t, :], inv[:, 0:t, 0:t, :],
                                           coef[:, 0:t, t, 0, :].unsqueeze(2).to_broadcast([P, t, t, HEADS]), ALU.mult))
                    then(dve.tensor_reduce(inv[:, t, 0:t, :], prod[:, 0:t, 0:t, :].rearrange("p s u h -> p u h s"),
                                           AX_X, ALU.add))
                for t in range(T):
                    n = t + 1
                    then(dve.tensor_tensor(prod[:, 0:n, 0:n, :], inv[:, 0:n, 0:n, :],
                                           coef[:, 0:n, t, 1, :].unsqueeze(2).to_broadcast([P, n, n, HEADS]), ALU.mult))
                    then(dve.tensor_reduce(mix[:, 0:n, t, :], prod[:, 0:n, 0:n, :].rearrange("p s u h -> p u h s"),
                                           AX_X, ALU.add))
                assert step[0] == STEPS

                for q in range(2):
                    dve.wait_ge(S["ring_full"], g * FILLS + ATT + q + 1)
                    ins = dve.tensor_tensor(h[:, 4 * q:4 * q + 4, :], h[:, 4 * q:4 * q + 4, :],
                                            ring[(ATT + q) % 4][:, :].rearrange("p (t c) -> p t c", t=4), ALU.add)
                ins.then_inc(S["resid_step"], 1)
                dve.wait_ge(S["resid_step"], 4 * g + 1)
                ln.statistics(dve, h_tiles, 2 * g + 1)
                ln.apply(dve, h_tiles, h_tiles, 2 * g + 1).then_inc(S["resid_step"], 1)
                dve.wait_ge(S["resid_step"], 4 * g + 2)
                dve.tensor_tensor(h[:, :, :], h[:, :, :], C["ln_g"][:, :].unsqueeze(1).to_broadcast([P, T, DIM]), ALU.mult)\
                    .then_inc(S["resid_step"], 1)
                dve.wait_ge(S["resid_step"], 4 * g + 3)
                dve.tensor_tensor(h[:, :, :], h[:, :, :], C["ln_b"][:, :].unsqueeze(1).to_broadcast([P, T, DIM]), ALU.add)\
                    .then_inc(S["resid_step"], 1)
                dve.wait_ge(S["resid_step"], 4 * g + 4)
                for t in range(T):
                    ins = dve.tensor_tensor(x_tiles[t], x_tiles[t], h[:, t, :], ALU.add)
                ins.then_inc(S["x_ready"], 1)


def build(nc, a):
    inp = {"x": a["L0_attn_a_x"], "W_qkv": a["L0_attn_a_W_qkv"], "RF": a["L0_attn_a_RF"], "W_out": a["L0_attn_a_W_out"],
           "b_out": a["L0_attn_a_b_out"], "w_qkvb": a["L0_attn_b_w_qkvb"], "w_o": a["L0_attn_b_w_o"],
           "ln_g": a["L0_attn_b_ln_g"], "ln_b": a["L0_attn_b_ln_b"], "Wr": a["L0_ffn_Wr"], "W1": a["L0_ffn_W1"],
           "W2": a["L0_ffn_W2"]}
    gd = nc.dram_tensor("gram_compact", [P, T, T * 2 * HEADS], F32, kind="Internal").ap()
    cd = nc.dram_tensor("mix_compact", [P, T, T * HEADS], F32, kind="Internal").ap()
    with ExitStack() as ctx:
        K = Kernel(nc, ctx)
        C = {
            "x": K.sb(ctx, "x", [P, BATCH * NT, DIM]),
            "ident": K.sb(ctx, "ident", [P, P]),
            "b_out": K.sb(ctx, "b_out", [P, DIM]),
            "ln_g": K.sb(ctx, "ln_g", [P, DIM]),
            "ln_b": K.sb(ctx, "ln_b", [P, DIM]),
            "w_r": K.sb(ctx, "w_r", [P, EXPERTS]),
            "minus_half": K.sb(ctx, "minus_half", [P, T]),
            "expert_ids": K.sb(ctx, "expert_ids", [P, EXPERTS]),
            "head_ind": K.sb(ctx, "head_ind", [P, 2, PAIRS, 32]),
            "b_qkT": K.sb(ctx, "b_qkT", [P, 2 * HD]),
            "b_vT": K.sb(ctx, "b_vT", [P, HD]),
            "b_betaT": K.sb(ctx, "b_betaT", [P, 32]),
            "b_oT": K.sb(ctx, "b_oT", [P, PAIRS, DIM]),
        }
        with ExitStack() as actx:
            A = {
                "feat_q": K.sb(actx, "feat_q", [P, HD]),
                "feat_k": K.sb(actx, "feat_k", [P, HD]),
                "vo": K.sb(actx, "vo", [P, HEADS, DIM]),
                "ones": K.sb(actx, "ones", [P, P]),
            }
            load_and_fold_weights(K, C, A, inp)
            linear_attention(K, C, A)
        expert_ffn(K, C, "f", inp)
        delta_memory(K, C, cd, gd)
        expert_ffn(K, C, "g", inp, out=a["out"])


_INS = ["L0_attn_a_x", "L0_attn_a_W_qkv", "L0_attn_a_RF", "L0_attn_a_W_out", "L0_attn_a_b_out", "L0_attn_b_w_qkvb",
        "L0_attn_b_w_o", "L0_attn_b_ln_g", "L0_attn_b_ln_b", "L0_ffn_Wr", "L0_ffn_W1", "L0_ffn_W2"]


def kernel(**inputs):
    import numpy as np
    import concourse.bacc as bacc
    from concourse.bass_utils import run_bass_kernel_spmd

    nc = bacc.Bacc("TRN2", target_bir_lowering=False, num_devices=1)
    arrays, args = {}, {}
    for name in _INS:
        arr = np.ascontiguousarray(inputs[name])
        arrays[f"in_{name}"] = arr
        args[name] = nc.dram_tensor(f"in_{name}", arr.shape, mybir.dt.from_np(arr.dtype), kind="ExternalInput").ap()
    args["out"] = nc.dram_tensor("out_x", (BATCH, SEQ, DIM), F32, kind="ExternalOutput").ap()
    build(nc, args)
    r = run_bass_kernel_spmd(nc, [arrays], core_ids=[0])
    return r.results[0]["out_x"]
```

```python
from contextlib import ExitStack

import concourse.bass as bass
from concourse import mybir

F32 = mybir.dt.float32
U32 = mybir.dt.uint32
ALU = mybir.AluOpType
ACT = mybir.ActivationFunctionType
AX_X = mybir.AxisListType.X

P = 128
BATCH, SEQ, DIM = 8, 512, 128
NT = SEQ // P
HEADS, DH = 16, 64
PAIRS = HEADS // 2
HD = HEADS * DH
STAB = 1e-6
LN_EPS = 1e-5
EPS = 1e-5
EXPERTS, FF = 8, 512
FC = FF // P
TOKENS = BATCH * SEQ
UNROLL = 4
BLOCKS = -(-(2 * TOKENS // P + EXPERTS - 1) // UNROLL) * UNROLL
REGION = TOKENS + P
UNUSED = EXPERTS * REGION
ROW = DIM + 2
NOWHERE = 2 * TOKENS
T = BATCH
NG = SEQ // P
TOK = P * T
BL = P // T
NTAU = P // BL
SCALE = float(DH) ** -0.5


class Kernel:

    def __init__(self, nc, ctx):
        self.nc, self.ctx = nc, ctx

    def sem(self, name):
        return self.ctx.enter_context(self.nc.semaphore(name))

    def sb(self, ctx, name, shape, dt=F32):
        return ctx.enter_context(self.nc.sbuf_tensor(name, shape, dt))

    def pb(self, ctx, name, shape=(P, 512), dt=F32):
        return ctx.enter_context(self.nc.psum_tensor(name, list(shape), dt))


def wait_apart(eng, sem, value, passed):
    eng.wait_ge(sem, value)
    eng.sem_inc(passed, 1)


class LayerNorm:

    def __init__(self, K, ctx, tag, n):
        self.n = n
        self.stats = K.sb(ctx, f"{tag}_stats", [P, n, 6])
        self.meanvar = K.sb(ctx, f"{tag}_meanvar", [P, n, 2])
        self.var_eps = K.sb(ctx, f"{tag}_var_eps", [P, n])
        self.rstd = K.sb(ctx, f"{tag}_rstd", [P, n])
        self.stats_step = K.sem(f"{tag}_stats_step")
        self.passed = K.sem(f"{tag}_passed")
        self.var_ready = K.sem(f"{tag}_var_ready")
        self.rstd_ready = K.sem(f"{tag}_rstd_ready")

    def statistics(self, dve, tiles, k, eps=LN_EPS):
        for n, x in enumerate(tiles):
            ins = dve.bn_stats(self.stats[:, n, :], x)
        ins.then_inc(self.stats_step, 1)
        wait_apart(dve, self.stats_step, 2 * k + 1, self.passed)
        for n in range(self.n):
            ins = dve.bn_aggr(self.meanvar[:, n, :], self.stats[:, n, :])
        ins.then_inc(self.stats_step, 1)
        dve.wait_ge(self.stats_step, 2 * k + 2)
        dve.tensor_scalar(self.var_eps[:, :], self.meanvar[:, :, 1], eps, None, ALU.add).then_inc(self.var_ready, 1)

    def root(self, pool, minus_half, k):
        pool.wait_ge(self.var_ready, k + 1)
        pool.tensor_tensor(self.rstd[:, :], self.var_eps[:, :], minus_half[:, 0:self.n], ALU.pow).then_inc(self.rstd_ready, 1)

    def apply(self, dve, tiles, outs, k):
        dve.wait_ge(self.rstd_ready, k + 1)
        for n, (x, o) in enumerate(zip(tiles, outs)):
            ins = dve.tensor_scalar(o, x, self.meanvar[:, n, 0:1], self.rstd[:, n:n + 1], ALU.subtract, ALU.mult)
        return ins


def load_and_fold_weights(K, C, A, inp):
    nc = K.nc
    with ExitStack() as ctx:
        w_qkv = K.sb(ctx, "w_qkv", [P, 3 * HD])
        w_qkvT = K.sb(ctx, "w_qkvT", [P, 3 * PAIRS, P])
        rf_blk = K.sb(ctx, "rf_blk", [P, PAIRS, 2, DH])
        wout_blk = K.sb(ctx, "wout_blk", [P, PAIRS, 2, DIM])
        b_rows = K.sb(ctx, "b_rows", [P, 3 * PAIRS, DIM])
        beta_rows = K.sb(ctx, "beta_rows", [HEADS, DIM])
        wo_rows = K.sb(ctx, "wo_rows", [P, HD])
        banks = [K.pb(ctx, f"w_bank{i}") for i in range(8)]

        x_in = K.sem("x_in")
        wqkv_in = K.sem("wqkv_in")
        blk_zero = K.sem("blk_zero")
        blk_in = K.sem("blk_in")
        brows_in = K.sem("brows_in")
        ident_step = K.sem("ident_step")
        masks_ready = K.sem("masks_ready")
        w_bank_full = K.sem("w_bank_full")
        w_bank_read = K.sem("w_bank_read")
        block = ctx.enter_context(nc.Block())

        fills = [("qkvT", i) for i in range(6)] + [("feat", i) for i in range(4)] + [("vo", i) for i in range(4)] \
            + [("bT", i) for i in range(6)] + [("betaT", 0)] + [("woT", i) for i in range(2)]

        @block.sync
        def _(sp):
            sp.dma_start(w_qkv[:, :], inp["W_qkv"]).then_inc(wqkv_in, 16)
            for t in range(BATCH):
                sp.dma_start(C["x"][:, t * NT:(t + 1) * NT, :],
                             inp["x"][t].rearrange("(g p) c -> p g c", p=P)).then_inc(x_in, 16)
            sp.dma_start(C["b_out"][:, :], inp["b_out"].partition_broadcast(P)).then_inc(x_in, 16)
            sp.dma_start(C["ln_g"][:, :], inp["ln_g"].partition_broadcast(P)).then_inc(x_in, 16)
            sp.dma_start(C["ln_b"][:, :], inp["ln_b"].partition_broadcast(P)).then_inc(x_in, 16)
            sp.dma_start(C["w_r"][:, :], inp["Wr"]).then_inc(x_in, 16)
            sp.wait_ge(x_in, 16 * (BATCH + 4))

        @block.scalar
        def _(act):
            act.wait_ge(blk_zero, 2)
            for hh in range(2):
                rows = slice(hh * DH, (hh + 1) * DH)
                act.dma_start(rf_blk[rows, :, hh, :], inp["RF"].rearrange("(p e) d r -> e d p r", e=2)[hh]).then_inc(blk_in, 16)
                act.dma_start(wout_blk[rows, :, hh, :],
                              inp["W_out"].rearrange("(p e d) c -> e d p c", e=2, d=DH)[hh]).then_inc(blk_in, 16)
            qkvb = inp["w_qkvb"].rearrange("(p e r) c -> e r p c", e=2, r=3 * DH + 1)
            for kind in range(3):
                for hh in range(2):
                    act.dma_start(b_rows[hh * DH:(hh + 1) * DH, kind * PAIRS:(kind + 1) * PAIRS, :],
                                  qkvb[hh, kind * DH:(kind + 1) * DH]).then_inc(brows_in, 16)
            act.dma_start(beta_rows[:, :], inp["w_qkvb"].rearrange("(h r) c -> h r c", h=HEADS)[:, 3 * DH, :]).then_inc(brows_in, 16)
            act.dma_start(wo_rows[:, :], inp["w_o"]).then_inc(brows_in, 16)
            for n, (kind, i) in enumerate(fills):
                act.wait_ge(w_bank_full, n + 1)
                b = banks[n % 8]
                if kind == "qkvT":
                    ins = act.copy(w_qkvT[:, 4 * i:4 * i + 4, :], b[:, :])
                elif kind == "feat":
                    dst = A["feat_q"] if i < 2 else A["feat_k"]
                    ins = act.copy(dst[:, (i % 2) * 512:(i % 2) * 512 + 512], b[:, :])
                elif kind == "vo":
                    ins = act.copy(A["vo"][:, 4 * i:4 * i + 4, :], b[:, :])
                elif kind == "bT":
                    dst, o = (C["b_qkT"], i) if i < 4 else (C["b_vT"], i - 4)
                    ins = act.copy(dst[:, o * 512:o * 512 + 512], b[:, :])
                elif kind == "betaT":
                    act.wait_ge(masks_ready, 1)
                    ins = act.copy(C["b_betaT"][:, 0:HEADS], b[:, 0:HEADS])
                else:
                    ins = act.copy(C["b_oT"][:, 4 * i:4 * i + 4, :], b[:, :])
                ins.then_inc(w_bank_read, 1)

        @block.gpsimd
        def _(pool):
            pool.memset(rf_blk[:, :, :, :], 0.0).then_inc(blk_zero, 1)
            pool.memset(wout_blk[:, :, :, :], 0.0).then_inc(blk_zero, 1)
            pool.memset(C["ident"][:, :], 0.0).then_inc(ident_step, 1)
            pool.wait_ge(ident_step, 1)
            pool.affine_select(out=C["ident"][:, :], in_=C["ident"][:, :], compare_op=ALU.not_equal, fill=1.0, base=0,
                               pattern=[[-1, P]], channel_multiplier=1).then_inc(ident_step, 1)
            pool.wait_ge(masks_ready, 3)
            pool.affine_select(out=C["earlier"][:, :], in_=C["ones"][:, :], compare_op=ALU.is_gt, fill=0.0, base=0,
                               pattern=[[1, P]], channel_multiplier=-1).then_inc(ident_step, 1)
            pool.iota(C["part_ids"][:, :, :], [[P, BATCH * NT], [TOKENS, 2]], base=0, channel_multiplier=1)

        @block.vector
        def _(dve):
            dve.memset(C["b_betaT"][:, :], 0.0).then_inc(masks_ready, 1)
            dve.memset(C["head_ind"][:, :, :, :], 0.0).then_inc(masks_ready, 1)
            dve.memset(C["ones"][:, :], 1.0).then_inc(masks_ready, 1)
            dve.memset(C["filler"][:, 0:DIM + 1], 0.0)
            dve.memset(C["x"][:, BATCH * NT, :], 0.0)
            dve.memset(C["filler"][:, DIM + 1:ROW].bitcast(U32), NOWHERE)
            for j in range(BLOCKS):
                dve.memset(C["block_rows"][:, j:j + 1], float(P * j))
            for e in range(EXPERTS):
                dve.memset(C["regions"][:, e:e + 1], float(e * REGION))
            dve.memset(C["minus_half"][:, :], -0.5)
            for e in range(EXPERTS):
                dve.memset(C["expert_ids"][:, e:e + 1], float(e))
            dve.wait_ge(masks_ready, 2)
            for kind in range(2):
                for p in range(PAIRS):
                    for hh in range(2):
                        col = HEADS * kind + 2 * p + hh
                        dve.memset(C["head_ind"][hh * DH:(hh + 1) * DH, kind, p, col:col + 1], 1.0)

        @block.tensor
        def _(pe):
            pe.wait_ge(ident_step, 2)
            ident = C["ident"]
            for n, (kind, i) in enumerate(fills):
                b = banks[n % 8]
                if n >= 8:
                    pe.wait_ge(w_bank_read, n - 7)
                if kind == "qkvT":
                    if i == 0:
                        pe.wait_ge(wqkv_in, 16)
                    for j in range(4):
                        q = 4 * i + j
                        ins = pe.transpose(b[:, j * P:(j + 1) * P], w_qkv[:, q * P:(q + 1) * P], ident[:, :])
                elif kind == "feat":
                    if i == 0:
                        pe.wait_ge(blk_in, 64)
                    pe.wait_ge(w_bank_read, 6)
                    for j in range(4):
                        q = 4 * i + j
                        ins = pe.matmul(b[:, j * P:(j + 1) * P], w_qkvT[:, q, :], rf_blk[:, q % PAIRS, :, :],
                                        start=True, stop=True)
                elif kind == "vo":
                    for j in range(2):
                        q = 2 * i + j
                        ins = pe.matmul(b[:, j * 256:(j + 1) * 256], w_qkvT[:, 2 * PAIRS + q, :], wout_blk[:, q, :, :],
                                        start=True, stop=True)
                elif kind == "bT":
                    if i == 0:
                        pe.wait_ge(brows_in, 128)
                    for j in range(4):
                        ins = pe.transpose(b[:, j * P:(j + 1) * P], b_rows[:, 4 * i + j, :], ident[:, :])
                elif kind == "betaT":
                    ins = pe.transpose(b[:, 0:HEADS], beta_rows[:, :], ident[0:HEADS, 0:HEADS])
                else:
                    for j in range(4):
                        q = 4 * i + j
                        ins = pe.transpose(b[:, j * P:(j + 1) * P], wo_rows[:, q * P:(q + 1) * P], ident[:, :])
                ins.then_inc(w_bank_full, 1)


def linear_attention(K, C, A):
    nc = K.nc
    x = C["x"]
    with ExitStack() as ctx:
        xn = K.sb(ctx, "a_xn", [P, NT, DIM])
        xnT = K.sb(ctx, "a_xnT", [P, SEQ])
        phik = K.sb(ctx, "phik", [P, NT, HD])
        phik_sum = K.sb(ctx, "phik_sum", [P, HD])
        phiq = K.sb(ctx, "phiq", [P, NT, HD])
        phiqT = K.sb(ctx, "phiqT", [P, 2, PAIRS, P])
        kxT = K.sb(ctx, "kxT", [P, HD])
        kv = K.sb(ctx, "kv", [P, PAIRS, DIM])
        ksum = K.sb(ctx, "ksum", [P, HD])
        prod = K.sb(ctx, "a_prod", [P, HD])
        norm = K.sb(ctx, "a_norm", [P, HEADS])
        rnorm = K.sb(ctx, "a_rnorm", [P, 2, HEADS])
        ln = LayerNorm(K, ctx, "a_ln", NT)
        ring = [K.pb(ctx, f"a_ring{i}") for i in range(4)]
        kx_bank = [K.pb(ctx, f"a_kx{i}") for i in range(2)]
        y_bank = K.pb(ctx, "a_y")
        t_bank = K.pb(ctx, "a_t")

        xn_ready = K.sem("a_xn_ready")
        xnT_done = K.sem("a_xnT_done")
        xnT_ready = K.sem("a_xnT_ready")
        ring_full = K.sem("a_ring_full")
        act_read = K.sem("a_act_read")
        dve_read = K.sem("a_dve_read")
        presum_step = K.sem("a_presum_step")
        kx_done = K.sem("a_kx_done")
        kxT_ready = K.sem("a_kxT_ready")
        norm_step = K.sem("a_norm_step")
        rnorm_ready = K.sem("a_rnorm_ready")
        phiq_scaled = K.sem("a_phiq_scaled")
        bias_added = K.sem("a_bias_added")
        y_done = K.sem("a_y_done")
        y_added = K.sem("a_y_added")
        block = ctx.enter_context(nc.Block())

        KSUM, KV, PHIQT, FILLS = 16, 18, 20, 28
        ACT_READS, DVE_READS = 24, 4

        def tiles(t):
            return [x[:, t * NT + n, :] if isinstance(t, int) else
                    x[:, bass.ds(t * NT + n, 1), :].rearrange("p a c -> p (a c)") for n in range(NT)]

        def x_of(t):
            return x[:, t * NT:(t + 1) * NT, :] if isinstance(t, int) else x[:, bass.ds(t * NT, NT), :]

        xn_tiles = [xn[:, n, :] for n in range(NT)]

        @block.tensor
        def _(pe):
            def transposes(t):
                pe.wait_ge(xn_ready, t + 1)
                for n in range(NT):
                    ins = pe.transpose(t_bank[:, n * P:(n + 1) * P], xn[:, n, :], C["ident"][:, :])
                ins.then_inc(xnT_done, 1)

            def body(t, more):
                pe.wait_ge(xnT_ready, t + 1)
                for k in range(16):
                    if k >= 4:
                        pe.wait_ge(act_read, t * ACT_READS + k - 3)
                    n, half = k % 8 // 2, k % 2
                    w = A["feat_k"] if k < 8 else A["feat_q"]
                    pe.matmul(ring[k % 4][:, :], xnT[:, n * P:(n + 1) * P], w[:, half * 512:half * 512 + 512],
                              start=True, stop=True).then_inc(ring_full, 1)
                pe.wait_ge(presum_step, 3 * t + 3)
                for half in range(2):
                    pe.wait_ge(act_read, t * ACT_READS + 13 + half)
                    pe.matmul(ring[half][:, :], C["ones"][:, :], phik_sum[:, half * 512:half * 512 + 512],
                              start=True, stop=True).then_inc(ring_full, 1)
                for half in range(2):
                    for n in range(NT):
                        ins = pe.matmul(kx_bank[half][:, :], xn[:, n, :], phik[:, n, half * 512:half * 512 + 512],
                                        start=(n == 0), stop=(n == NT - 1))
                    ins.then_inc(kx_done, 1)
                pe.wait_ge(kxT_ready, 2 * t + 2)
                for q in range(2):
                    pe.wait_ge(act_read, t * ACT_READS + 15 + q)
                    for j in range(4):
                        for hh in range(2):
                            h = 2 * (4 * q + j) + hh
                            ins = pe.matmul(ring[2 + q][hh * DH:(hh + 1) * DH, j * P:(j + 1) * P],
                                            kxT[:, h * DH:(h + 1) * DH], A["vo"][:, h, :], start=True, stop=True)
                    ins.then_inc(ring_full, 1)

                def turn_phiq(n):
                    pe.wait_ge(phiq_scaled, t * NT + n + 1)
                    for q in range(2):
                        if n < 2:
                            pe.wait_ge(dve_read, t * DVE_READS + 2 * n + q + 1)
                        else:
                            pe.wait_ge(act_read, t * ACT_READS + 16 + 2 * (n - 2) + q + 1)
                        for j in range(4):
                            p = 4 * q + j
                            ins = pe.transpose(ring[(2 * n + q) % 4][:, j * P:(j + 1) * P], phiq[:, n, p * P:(p + 1) * P],
                                               C["ident"][:, :])
                        ins.then_inc(ring_full, 1)

                def output(n):
                    pe.wait_ge(act_read, t * ACT_READS + 16 + 2 * n + 2)
                    pe.wait_ge(dve_read, t * DVE_READS + 4)
                    for p in range(PAIRS):
                        ins = pe.matmul(y_bank[:, n * P:(n + 1) * P], phiqT[:, n % 2, p, :], kv[:, p, :],
                                        start=(p == 0), stop=(p == PAIRS - 1))
                    ins.then_inc(y_done, 1)

                turn_phiq(0)
                for n in range(NT):
                    if n + 1 < NT:
                        turn_phiq(n + 1)
                    elif more:
                        transposes(t + 1)
                    output(n)

            transposes(0)
            with pe.Fori(0, BATCH - 1) as t:
                body(t, True)
            body(BATCH - 1, False)

        @block.scalar
        def _(act):
            def copy_xnT(t):
                act.wait_ge(xnT_done, t + 1)
                act.copy(xnT[:, :], t_bank[:, :]).then_inc(xnT_ready, 1)

            def body(t, more):
                for k in range(16):
                    act.wait_ge(ring_full, t * FILLS + k + 1)
                    dst = phik if k < 8 else phiq
                    act.activation(dst[:, k % 8 // 2, (k % 2) * 512:(k % 2) * 512 + 512], ring[k % 4][:, :], ACT.Relu)\
                        .then_inc(act_read, 1)
                for n in range(NT):
                    for q in range(2):
                        act.wait_ge(ring_full, t * FILLS + PHIQT + 2 * n + q + 1)
                        if n >= 2 and q == 0:
                            act.wait_ge(y_done, t * NT + n - 1)
                        act.copy(phiqT[:, n % 2, 4 * q:4 * q + 4, :],
                                 ring[(2 * n + q) % 4][:, :].rearrange("p (a c) -> p a c", a=4)).then_inc(act_read, 1)
                if more:
                    copy_xnT(t + 1)

            copy_xnT(0)
            with act.Fori(0, BATCH - 1) as t:
                body(t, True)
            body(BATCH - 1, False)

        @block.gpsimd
        def _(pool):
            def body(t, more):
                pool.wait_ge(act_read, t * ACT_READS + 4)
                pool.tensor_tensor(phik_sum[:, :], phik[:, 0, :], phik[:, 1, :], ALU.add).then_inc(presum_step, 1)
                for n in range(2, NT):
                    pool.wait_ge(act_read, t * ACT_READS + 2 * n + 2)
                    pool.wait_ge(presum_step, 3 * t + n - 1)
                    pool.tensor_tensor(phik_sum[:, :], phik_sum[:, :], phik[:, n, :], ALU.add).then_inc(presum_step, 1)
                pool.wait_ge(xn_ready, t + 1)
                pool.tensor_tensor(x_of(t), x_of(t), C["b_out"][:, :].unsqueeze(1).to_broadcast([P, NT, DIM]), ALU.add)\
                    .then_inc(bias_added, 1)
                for n in range(NT):
                    pool.wait_ge(rnorm_ready, t * NT + n + 1)
                    by_head = phiq[:, n, :].rearrange("p (h r) -> p h r", h=HEADS)
                    pool.tensor_tensor(by_head, by_head, rnorm[:, n % 2, :].unsqueeze(2).to_broadcast([P, HEADS, DH]),
                                       ALU.mult).then_inc(phiq_scaled, 1)
                    if more and n == 2:
                        ln.root(pool, C["minus_half"], t + 1)

            ln.root(pool, C["minus_half"], 0)
            with pool.Fori(0, BATCH - 1) as t:
                body(t, True)
            body(BATCH - 1, False)

        @block.vector
        def _(dve):
            def body(t, more):
                for half in range(2):
                    dve.wait_ge(ring_full, t * FILLS + KSUM + half + 1)
                    dve.tensor_copy(ksum[:, half * 512:half * 512 + 512], ring[half][:, :]).then_inc(dve_read, 1)
                dve.wait_ge(dve_read, t * DVE_READS + 2)

                def normalizer(n):
                    dve.wait_ge(act_read, t * ACT_READS + 8 + 2 * n + 2)
                    dve.tensor_tensor(prod[:, :], phiq[:, n, :], ksum[:, :], ALU.mult).then_inc(norm_step, 1)
                    dve.wait_ge(norm_step, (t * NT + n) * 3 + 1)
                    dve.tensor_reduce(norm[:, :], prod[:, :].rearrange("p (h r) -> p h r", h=HEADS), AX_X, ALU.add)\
                        .then_inc(norm_step, 1)
                    dve.wait_ge(norm_step, (t * NT + n) * 3 + 2)
                    dve.tensor_scalar(norm[:, :], norm[:, :], STAB, None, ALU.add).then_inc(norm_step, 1)
                    dve.wait_ge(norm_step, (t * NT + n) * 3 + 3)
                    if n >= 2:
                        dve.wait_ge(phiq_scaled, t * NT + n - 1)
                    dve.reciprocal(rnorm[:, n % 2, :], norm[:, :]).then_inc(rnorm_ready, 1)

                normalizer(0)
                normalizer(1)
                for half in range(2):
                    dve.wait_ge(kx_done, 2 * t + half + 1)
                    dve.tensor_copy(kxT[:, half * 512:half * 512 + 512], kx_bank[half][:, :]).then_inc(kxT_ready, 1)
                normalizer(2)
                for q in range(2):
                    dve.wait_ge(ring_full, t * FILLS + KV + q + 1)
                    dve.tensor_copy(kv[:, 4 * q:4 * q + 4, :], ring[2 + q][:, :].rearrange("p (a c) -> p a c", a=4))\
                        .then_inc(dve_read, 1)
                if more:
                    ln.statistics(dve, tiles(t + 1), t + 1)
                normalizer(3)
                if more:
                    ln.apply(dve, tiles(t + 1), xn_tiles, t + 1).then_inc(xn_ready, 1)
                dve.wait_ge(y_done, (t + 1) * NT)
                dve.wait_ge(bias_added, t + 1)
                dve.tensor_tensor(x_of(t), x_of(t), y_bank[:, :].rearrange("p (a c) -> p a c", a=NT), ALU.add)\
                    .then_inc(y_added, 1)

            ln.statistics(dve, tiles(0), 0)
            ln.apply(dve, tiles(0), xn_tiles, 0).then_inc(xn_ready, 1)
            with dve.Fori(0, BATCH - 1) as t:
                body(t, True)
            body(BATCH - 1, False)


def expert_ffn(K, C, tag, inp, rows, parts, out=None):
    nc = K.nc
    x = C["x"]
    with ExitStack() as ctx:
        w1 = K.sb(ctx, f"{tag}_w1", [P, EXPERTS, FF])
        w2 = K.sb(ctx, f"{tag}_w2", [P, EXPERTS, FC, DIM])
        sent = K.sb(ctx, f"{tag}_sent", [P, 2, NT, 2, ROW])
        xnT = K.sb(ctx, f"{tag}_xnT", [P, 2, SEQ])
        logits = K.sb(ctx, f"{tag}_logits", [P, NT, EXPERTS])
        best = K.sb(ctx, f"{tag}_best", [P, NT, 8])
        best_id = K.sb(ctx, f"{tag}_best_id", [P, NT, 8], U32)
        best_idf = K.sb(ctx, f"{tag}_best_idf", [P, NT, 2])
        gap = K.sb(ctx, f"{tag}_gap", [P, NT])
        ratio = K.sb(ctx, f"{tag}_ratio", [P, NT])
        denom = K.sb(ctx, f"{tag}_denom", [P, NT])
        weight = K.sb(ctx, f"{tag}_weight", [P, 2, NT])
        picked = K.sb(ctx, f"{tag}_picked", [P, 2, NT, EXPERTS])
        member = K.sb(ctx, f"{tag}_member", [P, NT, EXPERTS])
        filled = K.sb(ctx, f"{tag}_filled", [P, EXPERTS])
        before = K.sb(ctx, f"{tag}_before", [P, NT, EXPERTS])
        place = K.sb(ctx, f"{tag}_place", [P, NT, EXPERTS])
        place_of = K.sb(ctx, f"{tag}_place_of", [P, 2, NT])
        place_id = K.sb(ctx, f"{tag}_place_id", [P, 2, 2, NT], U32)
        n_blocks = K.sb(ctx, f"{tag}_n_blocks", [P, EXPERTS])
        ends = K.sb(ctx, f"{tag}_ends", [P, EXPERTS + 1])
        shift = K.sb(ctx, f"{tag}_shift", [P, EXPERTS])
        past = K.sb(ctx, f"{tag}_past", [P, BLOCKS, EXPERTS + 1])
        inside = K.sb(ctx, f"{tag}_inside", [P, BLOCKS, EXPERTS])
        table_f = K.sb(ctx, f"{tag}_table_f", [P, 2, BLOCKS])
        table = K.sb(ctx, f"{tag}_table", [P, 2, BLOCKS], U32)
        tail = K.sb(ctx, f"{tag}_tail", [P, EXPERTS], U32)
        blk = K.sb(ctx, f"{tag}_blk", [P, UNROLL, ROW])
        meta = K.sb(ctx, f"{tag}_meta", [P, UNROLL, ROW - DIM])
        blkT = K.sb(ctx, f"{tag}_blkT", [P, UNROLL, P])
        w1_now = K.sb(ctx, f"{tag}_w1_now", [P, UNROLL, FF])
        hidT = K.sb(ctx, f"{tag}_hidT", [P, UNROLL, FC, P])
        y = K.sb(ctx, f"{tag}_y", [P, UNROLL, DIM])
        part = K.sb(ctx, f"{tag}_part", [P, 2, 2, NT, DIM])
        ln = LayerNorm(K, ctx, f"{tag}_ln", NT)
        t_bank = [K.pb(ctx, f"{tag}_t{i}") for i in range(2)]
        r_bank = [K.pb(ctx, f"{tag}_r{i}") for i in range(2)]
        hid_bank = [K.pb(ctx, f"{tag}_hid{i}") for i in range(2)]
        y_bank = [K.pb(ctx, f"{tag}_yb{i}") for i in range(2)]

        def sem(name):
            return K.sem(f"{tag}_{name}")

        w_in, filler_stored, tails_stored = sem("w_in"), sem("filler_stored"), sem("tails_stored")
        xn_ready, xnT_done, xnT_ready, logits_done = sem("xn_ready"), sem("xnT_done"), sem("xnT_ready"), sem("logits_done")
        gap_ready, ratio_ready, route_step = sem("gap_ready"), sem("ratio_ready"), sem("route_step")
        member_ready, rank_done, place_ready = sem("member_ready"), sem("rank_done"), sem("place_ready")
        sent_done = [sem(f"sent_done{i}") for i in range(2)]
        table_step, table_ready = sem("table_step"), sem("table_ready")
        blk_in = [sem(f"blk_in{i}") for i in range(UNROLL)]
        blkT_done, blkT_ready, meta_ready, w1_ready = sem("blkT_done"), sem("blkT_ready"), sem("meta_ready"), sem("w1_ready")
        hid_done, hid_ready, y_done, y_ready = sem("hid_done"), sem("hid_ready"), sem("y_done"), sem("y_ready")
        y_stored = [sem(f"y_stored{i}") for i in range(UNROLL)]
        part_in = [sem(f"part_in{i}") for i in range(2)]
        sum_step, x_stored, pool_passed = sem("sum_step"), sem("x_stored"), sem("pool_passed")
        block = ctx.enter_context(nc.Block())

        def tiles(t):
            return [x[:, bass.ds(t * NT + n, 1), :].rearrange("p a c -> p (a c)") for n in range(NT)] \
                if not isinstance(t, int) else [x[:, t * NT + n, :] for n in range(NT)]

        def x_of(t):
            return x[:, bass.ds(t * NT, NT), :]

        ROUTE = 16

        @block.sync
        def _(sp):
            for e in range(EXPERTS):
                sp.dma_start(w1[:, e, :], inp["W1"][e]).then_inc(w_in, 16)
                sp.dma_start(w2[:, e, :, :], inp["W2"][e].rearrange("(a p) c -> p a c", p=P)).then_inc(w_in, 16)
            sp.dma_start(rows[UNUSED:UNUSED + P, :], C["filler"][:, :]).then_inc(filler_stored, 16)
            sp.wait_ge(filler_stored, 16)
            sp.wait_ge(table_ready, 1)
            for e in range(EXPERTS):
                end = sp.value_load(tail[0:1, e:e + 1], min_val=e * REGION, max_val=e * REGION + TOKENS)
                sp.dma_start(rows[bass.ds(end, P), :], C["filler"][:, :]).then_inc(tails_stored, 16)
            sp.wait_ge(tails_stored, 16 * EXPERTS)
            for i in range(2):
                sp.wait_ge(sent_done[i], BATCH // 2 * 2 * NT * 16)
            with sp.Fori(0, BLOCKS // UNROLL) as i:
                for u in range(UNROLL):
                    first = sp.value_load(table[0:1, 0, bass.ds(i * UNROLL + u, 1)], min_val=0, max_val=UNUSED)
                    sp.wait_ge(blkT_done, i * UNROLL + u + 1)
                    sp.wait_ge(meta_ready, i * UNROLL + u + 1)
                    sp.dma_start(blk[:, u, :], rows[bass.ds(first, P), :]).then_inc(blk_in[u], 16)
            for u in range(UNROLL):
                sp.wait_ge(y_stored[u], BLOCKS // UNROLL * 16)
            with sp.Fori(0, BATCH // 2) as i:
                for u in range(2):
                    t = i * 2 + u
                    sp.wait_ge(sum_step, 2 * t + 2)
                    for k in range(2):
                        sp.dma_start(part[:, u, k, :, :], parts.rearrange("(k t g p) c -> k t p g c", k=2, t=BATCH, p=P)
                                     [k, bass.ds(t, 1)].rearrange("a p g c -> (a p) g c")).then_inc(part_in[u], 16)
            if out is not None:
                with sp.Fori(0, BATCH) as t:
                    sp.wait_ge(sum_step, 2 * t + 6)
                    sp.dma_start(out[bass.ds(t, 1)].rearrange("a (g p) c -> p (a g) c", p=P), x_of(t)).then_inc(x_stored, 16)
                sp.wait_ge(x_stored, 16 * BATCH)

        @block.gpsimd
        def _(pool):
            with pool.Fori(0, BATCH // 2) as i:
                for u in range(2):
                    t = i * 2 + u
                    ln.root(pool, C["minus_half"], t)
                    wait_apart(pool, place_ready, t + 1, pool_passed)
                    for n in range(NT):
                        for k in range(2):
                            pool.indirect_dma_start(rows, bass.IndirectOffsetOnAxis(place_id[:, u, k, n:n + 1], 0),
                                                    sent[:, u, n, k, :], None).then_inc(sent_done[u], 16)
            with pool.Fori(0, BLOCKS // UNROLL) as i:
                for u in range(UNROLL):
                    wait_apart(pool, y_ready, i * UNROLL + u + 1, pool_passed)
                    pool.indirect_dma_start(parts, bass.IndirectOffsetOnAxis(meta[:, u, 1:2].bitcast(U32), 0), y[:, u, :], None,
                                            bounds_check=2 * TOKENS - 1, oob_is_err=False).then_inc(y_stored[u], 16)

        @block.tensor
        def _(pe):
            pe.sem_inc(blkT_done, UNROLL)
            with pe.Fori(0, BATCH // 2) as i:
                for u in range(2):
                    t = i * 2 + u
                    pe.wait_ge(xn_ready, t + 1)
                    for n in range(NT):
                        ins = pe.transpose(t_bank[u][:, n * P:(n + 1) * P], sent[:, u, n, 0, 0:DIM], C["ident"][:, :])
                    ins.then_inc(xnT_done, 1)
                    pe.wait_ge(xnT_ready, t + 1)
                    for n in range(NT):
                        ins = pe.matmul(r_bank[0][:, n * EXPERTS:(n + 1) * EXPERTS], xnT[:, u, n * P:(n + 1) * P],
                                        C["w_r"][:, :], start=True, stop=True)
                    ins.then_inc(logits_done, 1)
                    pe.wait_ge(member_ready, t + 1)
                    pe.matmul(r_bank[1][:, 0:32], C["earlier"][:, :], member[:, :, :], start=True, stop=True)
                    pe.matmul(r_bank[1][:, 32:64], C["ones"][:, :], member[:, :, :], start=True, stop=True)\
                        .then_inc(rank_done, 1)
            pe.wait_ge(w_in, 32 * EXPERTS)
            pe.wait_ge(table_ready, 1)

            def turn(i, u, done):
                pe.wait_ge(blk_in[u], 16 * (i + 1))
                if done is not None:
                    pe.wait_ge(blkT_ready, done - 1)
                pe.transpose(t_bank[u % 2][:, 0:P], blk[:, u, 0:DIM], C["ident"][:, :]).then_inc(blkT_done, 1)

            def hidden(i, u, j):
                pe.wait_ge(blkT_ready, j + 1)
                pe.wait_ge(w1_ready, j + 1)
                if not (isinstance(j, int) and j < 2):
                    pe.wait_ge(hid_ready, j - 1)
                for f in range(FC):
                    ins = pe.matmul(hid_bank[u % 2][:, f * P:(f + 1) * P], w1_now[:, u, f * P:(f + 1) * P], blkT[:, u, :],
                                    start=True, stop=True)
                ins.then_inc(hid_done, 1)

            def output(i, u, j, first):
                e = pe.value_load(table[0:1, 1, bass.ds(i * UNROLL + u, 1)], min_val=0, max_val=EXPERTS - 1)
                pe.wait_ge(hid_ready, j + 1)
                if not first:
                    pe.wait_ge(y_ready, j - 1)
                for f in range(FC):
                    ins = pe.matmul(y_bank[u % 2][:, 0:P], hidT[:, u, f, :],
                                    w2[:, bass.ds(e, 1), f, :].rearrange("p a c -> p (a c)"),
                                    start=(f == 0), stop=(f == FC - 1))
                ins.then_inc(y_done, 1)

            turn(0, 0, None)
            turn(0, 1, None)
            hidden(0, 0, 0)

            def body(i, lead, tail_end):
                for u in range(UNROLL):
                    j = i * UNROLL + u
                    if not (tail_end and u + 2 >= UNROLL):
                        turn(i + (u + 2) // UNROLL, (u + 2) % UNROLL, j + 2)
                    if not (tail_end and u + 1 >= UNROLL):
                        hidden(i + (u + 1) // UNROLL, (u + 1) % UNROLL, j + 1)
                    output(i, u, j, lead and u < 2)

            body(0, True, False)
            with pe.Fori(1, BLOCKS // UNROLL - 1) as i:
                body(i, False, False)
            body(BLOCKS // UNROLL - 1, False, True)

        @block.scalar
        def _(act):
            with act.Fori(0, BATCH // 2) as i:
                for u in range(2):
                    t = i * 2 + u
                    act.wait_ge(xnT_done, t + 1)
                    act.copy(xnT[:, u, :], t_bank[u][:, :]).then_inc(xnT_ready, 1)
                    act.wait_ge(gap_ready, t + 1)
                    act.activation(ratio[:, :], gap[:, :], ACT.Exp).then_inc(ratio_ready, 1)

            def turned(i, u):
                j = i * UNROLL + u
                act.wait_ge(blkT_done, UNROLL + j + 1)
                act.copy(blkT[:, u, :], t_bank[u % 2][:, 0:P]).then_inc(blkT_ready, 1)

            turned(0, 0)
            turned(0, 1)

            def body(i, tail_end):
                for u in range(UNROLL):
                    j = i * UNROLL + u
                    act.wait_ge(hid_done, j + 1)
                    act.activation(hidT[:, u, :, :], hid_bank[u % 2][:, :].rearrange("p (f n) -> p f n", f=FC), ACT.Relu)\
                        .then_inc(hid_ready, 1)
                    if not (tail_end and u + 2 >= UNROLL):
                        turned(i + (u + 2) // UNROLL, (u + 2) % UNROLL)

            with act.Fori(0, BLOCKS // UNROLL - 1) as i:
                body(i, False)
            body(BLOCKS // UNROLL - 1, True)

        @block.vector
        def _(dve):
            dve.sem_inc(meta_ready, UNROLL)
            dve.sem_inc(sum_step, 4)
            dve.tensor_copy(filled[:, :], C["regions"][:, :]).then_inc(table_step, 1)
            dve.wait_ge(table_step, 1)

            def route(t, u, first):
                step = [0]

                def then(ins):
                    step[0] += 1
                    ins.then_inc(route_step, 1)
                    dve.wait_ge(route_step, t * ROUTE + step[0])

                if not first:
                    dve.wait_ge(sent_done[u], (t - u) * NT * 16)
                ln.statistics(dve, tiles(t), t)
                ln.apply(dve, tiles(t), [sent[:, u, n, 0, 0:DIM] for n in range(NT)], t).then_inc(xn_ready, 1)
                dve.wait_ge(xn_ready, t + 1)
                dve.tensor_copy(sent[:, u, :, 1, 0:DIM], sent[:, u, :, 0, 0:DIM])
                dve.tensor_copy(sent[:, u, :, :, DIM + 1].bitcast(U32), C["part_ids"][:, bass.ds(t * NT, NT), :])
                dve.wait_ge(logits_done, t + 1)
                then(dve.tensor_copy(logits[:, :, :], r_bank[0][:, 0:NT * EXPERTS].rearrange("p (a e) -> p a e", a=NT)))
                wait_apart(dve, route_step, t * ROUTE + 1, ln.passed)
                for n in range(NT):
                    ins = dve.max(best[:, n, :], logits[:, n, :])
                then(ins)
                wait_apart(dve, route_step, t * ROUTE + 2, ln.passed)
                for n in range(NT):
                    dve.max_index(best_id[:, n, :], best[:, n, :], logits[:, n, :])
                dve.tensor_tensor(gap[:, :], best[:, :, 1], best[:, :, 0], ALU.subtract).then_inc(gap_ready, 1)
                dve.wait_ge(gap_ready, t + 1)
                then(dve.tensor_copy(best_idf[:, :, :], best_id[:, :, 0:2]))
                for k in range(2):
                    ins = dve.tensor_tensor(picked[:, k, :, :],
                                            C["expert_ids"][:, :].unsqueeze(1).to_broadcast([P, NT, EXPERTS]),
                                            best_idf[:, :, k:k + 1].to_broadcast([P, NT, EXPERTS]), ALU.is_equal)
                then(ins)
                dve.tensor_tensor(member[:, :, :], picked[:, 0, :, :], picked[:, 1, :, :], ALU.add).then_inc(member_ready, 1)
                dve.wait_ge(ratio_ready, t + 1)
                then(dve.tensor_scalar(denom[:, :], ratio[:, :], 1.0, None, ALU.add))
                then(dve.reciprocal(weight[:, 0, :], denom[:, :]))
                then(dve.tensor_tensor(weight[:, 1, :], weight[:, 0, :], ratio[:, :], ALU.mult))
                for k in range(2):
                    ins = dve.tensor_copy(sent[:, u, :, k, DIM], weight[:, k, :])
                then(ins)
                dve.wait_ge(rank_done, t + 1)
                total = r_bank[1][:, 32:64].rearrange("p (a e) -> p a e", a=NT)
                then(dve.tensor_copy(before[:, 0, :], filled[:, :]))
                for n in range(1, NT):
                    then(dve.tensor_tensor(before[:, n, :], before[:, n - 1, :], total[:, n - 1, :], ALU.add))
                then(dve.tensor_tensor(filled[:, :], before[:, NT - 1, :], total[:, NT - 1, :], ALU.add))
                then(dve.tensor_tensor(place[:, :, :], before[:, :, :],
                                       r_bank[1][:, 0:32].rearrange("p (a e) -> p a e", a=NT), ALU.add))
                for k in range(2):
                    ins = dve.tensor_tensor(picked[:, k, :, :], picked[:, k, :, :], place[:, :, :], ALU.mult)
                then(ins)
                then(dve.tensor_reduce(place_of[:, :, :], picked[:, :, :, :], AX_X, ALU.add))
                dve.tensor_copy(place_id[:, u, :, :], place_of[:, :, :]).then_inc(place_ready, 1)
                assert step[0] == ROUTE, step

            route(0, 0, True)
            route(1, 1, True)
            with dve.Fori(1, BATCH // 2) as i:
                for u in range(2):
                    route(i * 2 + u, u, False)

            step = [1]

            def then(ins):
                step[0] += 1
                ins.then_inc(table_step, 1)
                dve.wait_ge(table_step, step[0])

            then(dve.tensor_tensor(shift[:, :], filled[:, :], C["regions"][:, :], ALU.subtract))
            then(dve.tensor_tensor(past[:, 0:TOKENS // P, 0:EXPERTS],
                                   shift[:, :].unsqueeze(1).to_broadcast([P, TOKENS // P, EXPERTS]),
                                   C["block_rows"][:, 0:TOKENS // P].unsqueeze(2).to_broadcast([P, TOKENS // P, EXPERTS]),
                                   ALU.is_gt))
            then(dve.tensor_reduce(n_blocks[:, :], past[:, 0:TOKENS // P, 0:EXPERTS].rearrange("p b e -> p e b"), AX_X, ALU.add))
            then(dve.memset(ends[:, 0:1], 0.0))
            for e in range(EXPERTS):
                then(dve.scalar_tensor_tensor(out=ends[:, e + 1:e + 2], in0=n_blocks[:, e:e + 1], scalar=float(P),
                                              in1=ends[:, e:e + 1], op0=ALU.mult, op1=ALU.add))
            then(dve.tensor_tensor(past[:, :, :], C["block_rows"][:, :].unsqueeze(2).to_broadcast([P, BLOCKS, EXPERTS + 1]),
                                   ends[:, :].unsqueeze(1).to_broadcast([P, BLOCKS, EXPERTS + 1]), ALU.is_ge))
            then(dve.tensor_tensor(inside[:, :, :], past[:, :, 0:EXPERTS], past[:, :, 1:EXPERTS + 1], ALU.subtract))
            then(dve.tensor_tensor(shift[:, :], C["regions"][:, :], ends[:, 0:EXPERTS], ALU.subtract))
            then(dve.tensor_scalar(shift[:, :], shift[:, :], -float(UNUSED), None, ALU.add))
            then(dve.tensor_reduce(table_f[:, 1, :], past[:, :, 1:EXPERTS + 1], AX_X, ALU.add))
            then(dve.tensor_scalar(table_f[:, 1, :], table_f[:, 1, :], float(EXPERTS - 1), None, ALU.min))
            then(dve.tensor_tensor(past[:, :, 0:EXPERTS], C["block_rows"][:, :].unsqueeze(2).to_broadcast([P, BLOCKS, EXPERTS]),
                                   shift[:, :].unsqueeze(1).to_broadcast([P, BLOCKS, EXPERTS]), ALU.add))
            then(dve.tensor_tensor(inside[:, :, :], inside[:, :, :], past[:, :, 0:EXPERTS], ALU.mult))
            then(dve.tensor_reduce(table_f[:, 0, :], inside[:, :, :], AX_X, ALU.add))
            then(dve.tensor_scalar(table_f[:, 0, :], table_f[:, 0, :], float(UNUSED), None, ALU.add))
            dve.tensor_copy(tail[:, :], filled[:, :])
            dve.tensor_copy(table[:, :, :], table_f[:, :, :]).then_inc(table_ready, 1)
            dve.wait_ge(table_ready, 1)
            dve.wait_ge(w_in, 32 * EXPERTS)

            def take(i, u, j, first):
                e = dve.value_load(table[0:1, 1, bass.ds(i * UNROLL + u, 1)], min_val=0, max_val=EXPERTS - 1)
                dve.wait_ge(blk_in[u], 16 * (i + 1))
                if not first:
                    dve.wait_ge(hid_done, j - UNROLL + 1)
                    dve.wait_ge(y_stored[u], 16 * i)
                dve.tensor_copy(meta[:, u, :], blk[:, u, DIM:ROW]).then_inc(meta_ready, 1)
                dve.tensor_copy(w1_now[:, u, :], w1[:, bass.ds(e, 1), :].rearrange("p a f -> p (a f)")).then_inc(w1_ready, 1)

            def weigh(i, u, j):
                dve.wait_ge(y_done, j + 1)
                dve.wait_ge(meta_ready, UNROLL + j + 1)
                dve.tensor_scalar(y[:, u, :], y_bank[u % 2][:, 0:P], meta[:, u, 0:1], None, ALU.mult).then_inc(y_ready, 1)

            AHEAD = 2
            take(0, 0, 0, True)
            take(0, 1, 1, True)

            def body(i, lead, tail_end):
                for u in range(UNROLL):
                    j = i * UNROLL + u
                    if not (tail_end and u + AHEAD >= UNROLL):
                        take(i + (u + AHEAD) // UNROLL, (u + AHEAD) % UNROLL, j + AHEAD, lead and u + AHEAD < UNROLL)
                    weigh(i, u, j)

            body(0, True, False)
            with dve.Fori(1, BLOCKS // UNROLL - 1) as i:
                body(i, False, False)
            body(BLOCKS // UNROLL - 1, False, True)

            with dve.Fori(0, BATCH // 2) as i:
                for u in range(2):
                    t = i * 2 + u
                    dve.wait_ge(part_in[u], 32 * (i + 1))
                    for k in range(2):
                        if k:
                            dve.wait_ge(sum_step, 2 * t + 5)
                        dve.tensor_tensor(x_of(t), x_of(t), part[:, u, k, :, :], ALU.add).then_inc(sum_step, 1)


def delta_memory(K, C, cd, gd):
    nc = K.nc
    x = C["x"]
    QH = HEADS // 4
    with ExitStack() as ctx:
        h = K.sb(ctx, "b_h", [P, T, DIM])
        res = K.sb(ctx, "b_res", [P, T, DIM])
        hT = K.sb(ctx, "b_hT", [P, TOK])
        pos_exp = K.sb(ctx, "b_exp", [P, 2, 512])
        pos_rel = K.sb(ctx, "b_rel", [P, 2, 512])
        kq = K.sb(ctx, "b_kq", [P, 2, 2, TOK])
        gram = K.sb(ctx, "b_gram", [P, NTAU, 32, 2, HEADS])
        outT = K.sb(ctx, "b_outT", [P, 2, TOK])
        v = K.sb(ctx, "b_v", [P, NTAU, HD])
        coef = K.sb(ctx, "b_coef", [P, T, T, 2, HEADS])
        sums = K.sb(ctx, "b_sums", [P, 2, T, 2, HEADS])
        rsum = K.sb(ctx, "b_rsum", [P, T, 2, HEADS])
        den = K.sb(ctx, "b_den", [P, T, 2, HEADS])
        rden = K.sb(ctx, "b_rden", [P, T, 2, HEADS])
        beta = K.sb(ctx, "b_beta", [P, T, HEADS])
        gamma = K.sb(ctx, "b_gamma", [P, T, HEADS])
        alpha = K.sb(ctx, "b_alpha", [P, T, HEADS])
        inv = K.sb(ctx, "b_inv", [P, T, T, HEADS])
        prod = K.sb(ctx, "b_prod", [P, T, T, HEADS])
        mix = K.sb(ctx, "b_mix", [P, T, T, HEADS])
        spread = K.sb(ctx, "b_spread", [P, 2, NTAU, BL * T, QH])
        sums_raw = prod[:, 0:4, :, :].rearrange("p a t h -> p (a t h)").rearrange("p (a t b) -> p a t b", a=2, t=T)
        mix_q = prod[:, :, :, :].rearrange("p u t h -> p u (t h)").rearrange("p u (q t h) -> p u q t h", q=4, t=T)
        ln = LayerNorm(K, ctx, "b_ln", T)
        ring = [K.pb(ctx, f"b_ring{i}") for i in range(4)]
        g_bank = [K.pb(ctx, f"b_g{i}") for i in range(2)]
        s_bank = K.pb(ctx, "b_s")

        names = ["h_ready", "hT_full", "hT_ready", "v_full", "v_ready", "kq_full", "exp_read", "rel_read", "kq_ready",
                 "gram_done", "gram_read0", "gram_read1", "sums_read", "beta_logit", "beta_exp", "solve_step",
                 "gram_stored", "coef_loaded", "mix_stored", "spread_loaded0", "spread_loaded1", "spread_zero", "mixed_full", "outT_ready",
                 "att_done", "att_read", "resid_step", "sp_passed", "pe_passed"]
        S = {n: K.sem(f"b_{n}") for n in names}
        block = ctx.enter_context(nc.Block())
        STEPS = 50

        def x_tile(g, t):
            return x[:, bass.ds(g + t * NG, 1), :].rearrange("p a c -> p (a c)") if not isinstance(g, int) \
                else x[:, g + t * NG, :]

        @block.sync
        def _(sp):
            def compact(g):
                sp.wait_ge(S["gram_read0"], (g + 1) * PAIRS)
                wait_apart(sp, S["gram_read1"], (g + 1) * PAIRS, S["sp_passed"])
                if not isinstance(g, int):
                    sp.wait_ge(S["coef_loaded"], g * 16)
                for b in range(BL):
                    sp.dma_start(gd.rearrange("(a b) s n -> b s a n", b=BL)[b],
                                 gram[b * T:(b + 1) * T, :, (b % 4) * T:(b % 4 + 1) * T, :, :]
                                 .rearrange("p a t k h -> p a (t k h)")).then_inc(S["gram_stored"], 16)
                wait_apart(sp, S["gram_stored"], (g + 1) * 16 * BL, S["sp_passed"])
                if not isinstance(g, int):
                    sp.wait_ge(S["solve_step"], g * STEPS)
                sp.dma_start(coef[:, :, :, :, :].rearrange("p s t k h -> p (s t k h)"), gd.rearrange("b s n -> b (s n)"))\
                    .then_inc(S["coef_loaded"], 16)

            def store_mix(m):
                sp.wait_ge(S["solve_step"], (m + 1) * STEPS)
                sp.dma_start(cd.rearrange("b u q n -> b (u q n)"), prod[:, :, :, :].rearrange("p u t h -> p (u t h)"))\
                    .then_inc(S["mix_stored"], 16)
                wait_apart(sp, S["mix_stored"], (m + 1) * 16, S["sp_passed"])

            def load_spread(m, q):
                sp.wait_ge(S["outT_ready"], 16 * (m + 1) + 4 * (q - 1))
                for b in range(BL):
                    sp.dma_start(spread[b * T:(b + 1) * T, q % 2, :, b * T:(b + 1) * T, :].rearrange("p a t h -> p a (t h)"),
                                 cd.rearrange("(a b) u q n -> q b u a n", b=BL)[q, b])\
                        .then_inc(S[f"spread_loaded{q % 2}"], 16)

            sp.wait_ge(S["spread_zero"], 1)
            compact(0)
            with sp.Fori(1, NG) as g:
                m = g - 1
                store_mix(m)
                load_spread(m, 0)
                load_spread(m, 1)
                compact(g)
                load_spread(m, 2)
                load_spread(m, 3)
                for i in range(2):
                    wait_apart(sp, S[f"spread_loaded{i}"], (m + 1) * 2 * 16 * BL, S["sp_passed"])
            store_mix(NG - 1)
            for q in range(4):
                load_spread(NG - 1, q)

        @block.gpsimd
        def _(pool):
            with pool.Fori(0, 3 * NG + 1) as k:
                ln.root(pool, C["minus_half"], k)

        @block.tensor
        def _(pe):
            def values(m):
                pe.wait_ge(S["rel_read"], 32 * (m + 1))
                pe.wait_ge(S["outT_ready"], 16 * (m + 1))
                for k in range(16):
                    if k >= 4:
                        pe.wait_ge(S["v_ready"], 16 * m + k - 3)
                    pe.matmul(ring[k % 4][:, :], hT[:, (k // 2) * P:(k // 2 + 1) * P],
                              C["b_vT"][:, (k % 2) * 512:(k % 2) * 512 + 512], start=True, stop=True)\
                        .then_inc(S["v_full"], 1)

            def keys_and_queries(g):
                later = not isinstance(g, int)
                if later:
                    pe.wait_ge(S["v_ready"], 16 * g)
                pe.wait_ge(S["h_ready"], g + 1)
                for q in range(2):
                    for j in range(4):
                        ins = pe.transpose(ring[q][:, j * P:(j + 1) * P], h[:, 4 * q + j, :], C["ident"][:, :])
                    ins.then_inc(S["hT_full"], 1)
                pe.wait_ge(S["hT_ready"], 2 * g + 2)
                if later:
                    pe.wait_ge(S["sums_read"], g)
                for j in range(4):
                    pe.matmul(s_bank[32 * j:32 * j + 32, 256:512], C["b_betaT"][:, :], hT[:, 256 * j:256 * j + 256],
                              start=True, stop=True)

                def project(p):
                    for k in range(4):
                        n = 4 * p + k
                        if n >= 4:
                            pe.wait_ge(S["rel_read"], 32 * g + n - 3)
                        kind, half = k // 2, k % 2
                        w = C["b_qkT"][:, (1 - kind) * HD + p * P:(1 - kind) * HD + (p + 1) * P]
                        pe.matmul(ring[n % 4][:, :], w, hT[:, half * 512:half * 512 + 512], start=True, stop=True)\
                            .then_inc(S["kq_full"], 1)

                def products(p):
                    pe.wait_ge(S["kq_ready"], 32 * g + 4 * p + 4)
                    for kind in range(2):
                        for j in range(4):
                            pe.matmul(s_bank[32 * j:32 * j + 32, 0:256], C["head_ind"][:, kind, p, :],
                                      kq[:, p % 2, kind, 256 * j:256 * j + 256], start=(p == 0 and kind == 0),
                                      stop=(p == PAIRS - 1 and kind == 1), skip_group_check=True)
                    if p >= 1:
                        pe.wait_ge(S["gram_read0"], PAIRS * g + p)
                        pe.wait_ge(S["gram_read1"], PAIRS * g + p)
                    elif later:
                        pe.wait_ge(S["att_read"], g)
                    wait_apart(pe, S["kq_ready"], 32 * g + 4 * p + 4, S["pe_passed"])
                    for a in range(NTAU):
                        for j in range(4):
                            c = (4 * a + j) * 32
                            for hh in range(2):
                                r = slice(hh * DH, (hh + 1) * DH)
                                ins = pe.matmul(g_bank[hh][32 * j:32 * j + 32, a * 64:(a + 1) * 64],
                                                kq[r, p % 2, 0, c:c + 32], kq[r, p % 2, :, c:c + 32], start=True, stop=True)
                    ins.then_inc(S["gram_done"], 1)

                project(0)
                for p in range(PAIRS):
                    if p + 1 < PAIRS:
                        project(p + 1)
                    products(p)

            def mix_values(m, grams):
                pe.wait_ge(S["rel_read"], 32 * grams)
                pe.wait_ge(S["v_ready"], 16 * (m + 1))
                pe.wait_ge(S["gram_read0"], PAIRS * grams)
                pe.wait_ge(S["gram_read1"], PAIRS * grams)

                def project_out(p):
                    pe.wait_ge(S["outT_ready"], 16 * (m + 1) + 2 * p + 2)
                    for t in range(T):
                        ins = pe.matmul(g_bank[t // 4][:, (t % 4) * P:(t % 4 + 1) * P], outT[:, p % 2, t::T],
                                        C["b_oT"][:, p, :], start=(p == 0 and t % 4 == 0),
                                        stop=(p == PAIRS - 1 and t % 4 == 3), skip_group_check=True)
                    ins.then_inc(S["att_done"], 1)

                for p in range(PAIRS):
                    if p % 2 == 0:
                        pe.wait_ge(S[f"spread_loaded{p // 2 % 2}"], (m * 2 + p // 4 + 1) * 16 * BL)
                    for q in range(2):
                        n = 2 * p + q
                        if n >= 4:
                            pe.wait_ge(S["outT_ready"], 16 * (m + 1) + n - 3)
                        for a in range(NTAU // 2):
                            for hh in range(2):
                                hd = (2 * p + hh) * DH
                                ins = pe.matmul(ring[n % 4][hh * DH:(hh + 1) * DH, a * P:(a + 1) * P],
                                                v[:, q * 4 + a, hd:hd + DH],
                                                spread[:, (p // 2) % 2, q * 4 + a, :, (2 * p + hh) % QH],
                                                start=True, stop=True)
                        ins.then_inc(S["mixed_full"], 1)
                    if p >= 1:
                        project_out(p - 1)
                project_out(PAIRS - 1)

            keys_and_queries(0)
            with pe.Fori(1, NG) as g:
                values(g - 1)
                keys_and_queries(g)
                mix_values(g - 1, g + 1)
            values(NG - 1)
            mix_values(NG - 1, NG)

        @block.scalar
        def _(act):
            def values(m):
                for k in range(16):
                    act.wait_ge(S["v_full"], 16 * m + k + 1)
                    act.copy(v[:, k // 2, (k % 2) * 512:(k % 2) * 512 + 512], ring[k % 4][:, :]).then_inc(S["v_ready"], 1)

            def keys_and_queries(g):
                for q in range(2):
                    act.wait_ge(S["hT_full"], 2 * g + q + 1)
                    act.copy(hT[:, :].rearrange("c (b t) -> c t b", t=T)[:, 4 * q:4 * q + 4, :],
                             ring[q][:, :].rearrange("c (t b) -> c t b", t=4)).then_inc(S["hT_ready"], 1)

                def gram_copy(p):
                    act.wait_ge(S["gram_done"], g * PAIRS + p + 1)
                    if p == 0 and not isinstance(g, int):
                        act.wait_ge(S["gram_stored"], g * 16 * BL)
                    act.copy(gram[:, :, :, :, 2 * p].rearrange("p a b k -> p a k b"),
                             g_bank[0][:, :].rearrange("p (a k b) -> p a k b", a=NTAU, k=2)).then_inc(S["gram_read0"], 1)

                for n in range(32):
                    act.wait_ge(S["kq_full"], g * 32 + n + 1)
                    if n >= 2:
                        act.wait_ge(S["kq_ready"], g * 32 + n - 1)
                    act.activation(pos_exp[:, n % 2, :], ring[n % 4][:, :], ACT.Exp).then_inc(S["exp_read"], 1)
                    act.activation(pos_rel[:, n % 2, :], ring[n % 4][:, :], ACT.Relu).then_inc(S["rel_read"], 1)
                    if n % 4 == 3 and n > 4:
                        gram_copy(n // 4 - 1)
                gram_copy(PAIRS - 1)
                act.wait_ge(S["beta_logit"], g + 1)
                act.activation(beta[:, :, :], sums[:, 1, :, 0, :], ACT.Exp, scale=-1.0).then_inc(S["beta_exp"], 1)

            def mix_values(m):
                for n in range(16):
                    p, q = n // 2, n % 2
                    act.wait_ge(S["mixed_full"], 16 * m + n + 1)
                    if n % 2 == 0 and p >= 2:
                        act.wait_ge(S["att_done"], PAIRS * m + p - 1)
                    act.copy(outT[:, p % 2, q * 512:(q + 1) * 512], ring[n % 4][:, :]).then_inc(S["outT_ready"], 1)

            act.sem_inc(S["outT_ready"], 16)
            keys_and_queries(0)
            with act.Fori(1, NG) as g:
                values(g - 1)
                keys_and_queries(g)
                mix_values(g - 1)
            values(NG - 1)
            mix_values(NG - 1)

        @block.vector
        def _(dve):
            def normalize(g, k):
                tiles = [x_tile(g, t) for t in range(T)]
                ln.statistics(dve, tiles, k)
                if not (isinstance(g, int) and g == 0):
                    dve.wait_ge(S["hT_full"], 2 * g)
                ln.apply(dve, tiles, [h[:, t, :] for t in range(T)], k).then_inc(S["h_ready"], 1)

            def solver(m):
                step = [0]

                def then(ins):
                    step[0] += 1
                    ins.then_inc(S["solve_step"], 1)
                    dve.wait_ge(S["solve_step"], m * STEPS + step[0])

                def unit_sums():
                    then(dve.reciprocal(rsum[:, :, :, :], sums[:, 0, :, :, :]))
                    dve.wait_ge(S["coef_loaded"], (m + 1) * 16)
                    by_s = coef[:, :, :, :, :].rearrange("p s t k h -> p s (t k h)")
                    then(dve.tensor_tensor(by_s, by_s, rsum[:, :, :, :].rearrange("p t k h -> p (t k h)").unsqueeze(1)
                                           .to_broadcast([P, T, T * 2 * HEADS]), ALU.mult))

                def unit_sums_of_keys():
                    by_tk = coef[:, :, :, :, :].rearrange("p s t k h -> p s (t k) h")
                    then(dve.tensor_tensor(by_tk, by_tk, rsum[:, :, 0, :].unsqueeze(2).to_broadcast([P, T, 2 * T, HEADS]),
                                           ALU.mult))

                def denominators():
                    dve.memset(den[:, 0, 0, :], 1.0)
                    dve.tensor_copy(den[:, 0, 1, :], coef[:, 0, 0, 1, :])
                    then(dve.tensor_copy(den[:, 1:T, :, :], coef[:, 0, 1:T, :, :]))
                    for s in range(1, T - 1):
                        then(dve.tensor_tensor(den[:, s + 1:T, :, :], den[:, s + 1:T, :, :], coef[:, s, s + 1:T, :, :],
                                               ALU.add))
                    diag = coef[:, :, :, 1, :].rearrange("p s t h -> p (s t) h")[:, T + 1::T + 1, :]
                    then(dve.tensor_tensor(den[:, 1:T, 1, :], den[:, 1:T, 1, :], diag, ALU.add))

                def reciprocals():
                    then(dve.tensor_scalar(rden[:, :, :, :], den[:, :, :, :], EPS, None, ALU.add))
                    then(dve.reciprocal(rden[:, :, :, :], rden[:, :, :, :]))
                    dve.wait_ge(S["beta_exp"], m + 1)
                    then(dve.tensor_scalar(beta[:, :, :], beta[:, :, :], 1.0, None, ALU.add))
                    then(dve.reciprocal(beta[:, :, :], beta[:, :, :]))

                def factors():
                    then(dve.tensor_tensor(gamma[:, :, :], beta[:, :, :], den[:, :, 0, :], ALU.mult))
                    then(dve.tensor_tensor(gamma[:, :, :], gamma[:, :, :], rden[:, :, 0, :], ALU.mult))
                    dve.tensor_copy(inv[:, :, :, :].rearrange("p t u h -> p (t u) h")[:, ::T + 1, :], gamma[:, :, :])
                    dve.tensor_scalar(rden[:, :, 1, :], rden[:, :, 1, :], SCALE, None, ALU.mult)
                    then(dve.scalar_tensor_tensor(out=alpha[:, :, :], in0=gamma[:, :, :], scalar=-1.0, in1=rden[:, :, 0, :],
                                                  op0=ALU.mult, op1=ALU.mult))

                def apply_factors():
                    dve.tensor_tensor(coef[:, :, :, 0, :], coef[:, :, :, 0, :], alpha[:, :, :].unsqueeze(1)
                                      .to_broadcast([P, T, T, HEADS]), ALU.mult)
                    then(dve.tensor_tensor(coef[:, :, :, 1, :], coef[:, :, :, 1, :], rden[:, :, 1, :].unsqueeze(1)
                                           .to_broadcast([P, T, T, HEADS]), ALU.mult))

                def inverse_row(t):
                    then(dve.tensor_tensor(prod[:, 0:t, 0:t, :], inv[:, 0:t, 0:t, :],
                                           coef[:, 0:t, t, 0, :].unsqueeze(2).to_broadcast([P, t, t, HEADS]), ALU.mult))
                    then(dve.tensor_reduce(inv[:, t, 0:t, :], prod[:, 0:t, 0:t, :].rearrange("p s u h -> p u h s"),
                                           AX_X, ALU.add))

                def mix_column(t):
                    n = t + 1
                    then(dve.tensor_tensor(prod[:, 0:n, 0:n, :], inv[:, 0:n, 0:n, :],
                                           coef[:, 0:n, t, 1, :].unsqueeze(2).to_broadcast([P, n, n, HEADS]), ALU.mult))
                    then(dve.tensor_reduce(mix[:, 0:n, t, :], prod[:, 0:n, 0:n, :].rearrange("p s u h -> p u h s"),
                                           AX_X, ALU.add))

                def by_quarters():
                    for q in range(4):
                        ins = dve.tensor_copy(mix_q[:, :, q, :, :], mix[:, :, :, q * QH:(q + 1) * QH])
                    then(ins)
                    assert step[0] == STEPS, step

                def part(i):
                    if i < 6:
                        (unit_sums, unit_sums_of_keys, denominators, reciprocals, factors, apply_factors)[i]()
                    elif i < 6 + T - 1:
                        inverse_row(i - 5)
                    elif i < 6 + 2 * T - 1:
                        mix_column(i - 5 - T)
                    else:
                        by_quarters()

                return part

            SOLVE_PARTS = 6 + 2 * T

            def keys_and_queries(g):
                later = not isinstance(g, int)
                solve = solver(g - 1) if later else None

                def gram_copy(p):
                    dve.wait_ge(S["gram_done"], g * PAIRS + p + 1)
                    if p == 0 and later:
                        dve.wait_ge(S["gram_stored"], g * 16 * BL)
                    dve.tensor_copy(gram[:, :, :, :, 2 * p + 1].rearrange("p a b k -> p a k b"),
                                    g_bank[1][:, :].rearrange("p (a k b) -> p a k b", a=NTAU, k=2))\
                        .then_inc(S["gram_read1"], 1)

                for n in range(32):
                    dve.wait_ge(S["rel_read"], g * 32 + n + 1)
                    p, k = n // 4, n % 4
                    if p >= 2 and k == 0:
                        dve.wait_ge(S["gram_done"], g * PAIRS + p - 1)
                    dve.scalar_tensor_tensor(out=kq[:, p % 2, k // 2, (k % 2) * 512:(k % 2) * 512 + 512],
                                             in0=pos_exp[:, n % 2, :], scalar=1.0, in1=pos_rel[:, n % 2, :],
                                             op0=ALU.min, op1=ALU.add).then_inc(S["kq_ready"], 1)
                    if k == 3 and p >= 1:
                        gram_copy(p - 1)
                    if later and 2 <= n < 2 + SOLVE_PARTS:
                        solve(n - 2)
                gram_copy(PAIRS - 1)
                if later:
                    dve.wait_ge(S["mix_stored"], g * 16)
                dve.tensor_copy(sums_raw, s_bank[:, :].rearrange("p (a b t) -> p a t b", a=2, t=T)).then_inc(S["sums_read"], 1)
                dve.wait_ge(S["sums_read"], g + 1)
                dve.transpose(sums[:, :, :, :, :].rearrange("p a t k h -> p (a t k h)"),
                              sums_raw.rearrange("p a t b -> p (a t b)")).then_inc(S["beta_logit"], 1)
                dve.wait_ge(S["beta_logit"], g + 1)

            def add_output(m, k):
                tiles = [x_tile(m, t) for t in range(T)]
                res_tiles = [res[:, t, :] for t in range(T)]
                ln.statistics(dve, tiles, k)
                ln.apply(dve, tiles, res_tiles, k).then_inc(S["resid_step"], 1)
                dve.wait_ge(S["resid_step"], 5 * m + 1)
                dve.wait_ge(S["att_done"], PAIRS * (m + 1))
                for q in range(2):
                    ins = dve.tensor_tensor(res[:, 4 * q:4 * q + 4, :], res[:, 4 * q:4 * q + 4, :],
                                            g_bank[q][:, :].rearrange("p (t c) -> p t c", t=4), ALU.add)
                ins.then_inc(S["att_read"], 1)
                dve.wait_ge(S["att_read"], m + 2)
                ln.statistics(dve, res_tiles, k + 1)
                ln.apply(dve, res_tiles, res_tiles, k + 1).then_inc(S["resid_step"], 1)
                dve.wait_ge(S["resid_step"], 5 * m + 2)
                dve.tensor_tensor(res[:, :, :], res[:, :, :], C["ln_g"][:, :].unsqueeze(1).to_broadcast([P, T, DIM]), ALU.mult)\
                    .then_inc(S["resid_step"], 1)
                dve.wait_ge(S["resid_step"], 5 * m + 3)
                dve.tensor_tensor(res[:, :, :], res[:, :, :], C["ln_b"][:, :].unsqueeze(1).to_broadcast([P, T, DIM]), ALU.add)\
                    .then_inc(S["resid_step"], 1)
                dve.wait_ge(S["resid_step"], 5 * m + 4)
                for t in range(T):
                    ins = dve.tensor_tensor(tiles[t], tiles[t], res[:, t, :], ALU.add)
                ins.then_inc(S["resid_step"], 1)
                dve.wait_ge(S["resid_step"], 5 * m + 5)

            dve.sem_inc(S["att_read"], 1)
            normalize(0, 0)
            dve.memset(spread[:, :, :, :, :], 0.0)
            dve.memset(inv[:, :, :, :], 0.0)
            dve.memset(mix[:, :, :, :], 0.0).then_inc(S["spread_zero"], 1)
            keys_and_queries(0)
            normalize(1, 1)
            with dve.Fori(1, NG) as g:
                keys_and_queries(g)
                normalize(g + 1, 3 * g - 1)
                add_output(g - 1, 3 * g)
            last = solver(NG - 1)
            for i in range(SOLVE_PARTS):
                last(i)
            add_output(NG - 1, 3 * NG - 1)


def build(nc, a):
    inp = {"x": a["L0_attn_a_x"], "W_qkv": a["L0_attn_a_W_qkv"], "RF": a["L0_attn_a_RF"], "W_out": a["L0_attn_a_W_out"],
           "b_out": a["L0_attn_a_b_out"], "w_qkvb": a["L0_attn_b_w_qkvb"], "w_o": a["L0_attn_b_w_o"],
           "ln_g": a["L0_attn_b_ln_g"], "ln_b": a["L0_attn_b_ln_b"], "Wr": a["L0_ffn_Wr"], "W1": a["L0_ffn_W1"],
           "W2": a["L0_ffn_W2"]}
    gd = nc.dram_tensor("gram_compact", [P, T, T * 2 * HEADS], F32, kind="Internal").ap()
    cd = nc.dram_tensor("mix_compact", [P, T, 4, T * HEADS // 4], F32, kind="Internal").ap()
    rows = nc.dram_tensor("expert_rows", [UNUSED + P, ROW], F32, kind="Internal").ap()
    parts = nc.dram_tensor("expert_parts", [2 * TOKENS, DIM], F32, kind="Internal").ap()
    with ExitStack() as ctx:
        K = Kernel(nc, ctx)
        C = {
            "x": K.sb(ctx, "x", [P, BATCH * NT + 1, DIM]),
            "ident": K.sb(ctx, "ident", [P, P]),
            "b_out": K.sb(ctx, "b_out", [P, DIM]),
            "ln_g": K.sb(ctx, "ln_g", [P, DIM]),
            "ln_b": K.sb(ctx, "ln_b", [P, DIM]),
            "w_r": K.sb(ctx, "w_r", [P, EXPERTS]),
            "ones": K.sb(ctx, "ones", [P, P]),
            "earlier": K.sb(ctx, "earlier", [P, P]),
            "filler": K.sb(ctx, "filler", [P, ROW]),
            "part_ids": K.sb(ctx, "part_ids", [P, BATCH * NT, 2], U32),
            "block_rows": K.sb(ctx, "block_rows", [P, BLOCKS]),
            "regions": K.sb(ctx, "regions", [P, EXPERTS]),
            "minus_half": K.sb(ctx, "minus_half", [P, T]),
            "expert_ids": K.sb(ctx, "expert_ids", [P, EXPERTS]),
            "head_ind": K.sb(ctx, "head_ind", [P, 2, PAIRS, 32]),
            "b_qkT": K.sb(ctx, "b_qkT", [P, 2 * HD]),
            "b_vT": K.sb(ctx, "b_vT", [P, HD]),
            "b_betaT": K.sb(ctx, "b_betaT", [P, 32]),
            "b_oT": K.sb(ctx, "b_oT", [P, PAIRS, DIM]),
        }
        with ExitStack() as actx:
            A = {
                "feat_q": K.sb(actx, "feat_q", [P, HD]),
                "feat_k": K.sb(actx, "feat_k", [P, HD]),
                "vo": K.sb(actx, "vo", [P, HEADS, DIM]),
            }
            load_and_fold_weights(K, C, A, inp)
            linear_attention(K, C, A)
        expert_ffn(K, C, "f", inp, rows, parts)
        delta_memory(K, C, cd, gd)
        expert_ffn(K, C, "g", inp, rows, parts, out=a["out"])


_INS = ["L0_attn_a_x", "L0_attn_a_W_qkv", "L0_attn_a_RF", "L0_attn_a_W_out", "L0_attn_a_b_out", "L0_attn_b_w_qkvb",
        "L0_attn_b_w_o", "L0_attn_b_ln_g", "L0_attn_b_ln_b", "L0_ffn_Wr", "L0_ffn_W1", "L0_ffn_W2"]


def kernel(**inputs):
    import numpy as np
    import concourse.bacc as bacc
    from concourse.bass_utils import run_bass_kernel_spmd

    nc = bacc.Bacc("TRN2", target_bir_lowering=False, num_devices=1)
    arrays, args = {}, {}
    for name in _INS:
        arr = np.ascontiguousarray(inputs[name])
        arrays[f"in_{name}"] = arr
        args[name] = nc.dram_tensor(f"in_{name}", arr.shape, mybir.dt.from_np(arr.dtype), kind="ExternalInput").ap()
    args["out"] = nc.dram_tensor("out_x", (BATCH, SEQ, DIM), F32, kind="ExternalOutput").ap()
    build(nc, args)
    r = run_bass_kernel_spmd(nc, [arrays], core_ids=[0])
    return r.results[0]["out_x"]
```

```python
from contextlib import ExitStack

import concourse.bass as bass
from concourse import mybir

F32 = mybir.dt.float32
U32 = mybir.dt.uint32
ALU = mybir.AluOpType
ACT = mybir.ActivationFunctionType
AX_X = mybir.AxisListType.X

P = 128
BATCH, SEQ, DIM = 8, 512, 128
NT = SEQ // P
HEADS, DH = 16, 64
PAIRS = HEADS // 2
HD = HEADS * DH
STAB = 1e-6
LN_EPS = 1e-5
EPS = 1e-5
EXPERTS, FF = 8, 512
FC = FF // P
TOKENS = BATCH * SEQ
UNROLL = 6
BLOCKS = -(-(2 * TOKENS // P + EXPERTS - 1) // UNROLL) * UNROLL
REGION = TOKENS + P
UNUSED = EXPERTS * REGION
ROW = DIM + 2
NOWHERE = 2 * TOKENS
T = BATCH
NG = SEQ // P
TOK = P * T
BL = P // T
NTAU = P // BL
SCALE = float(DH) ** -0.5


class Kernel:

    def __init__(self, nc, ctx):
        self.nc, self.ctx = nc, ctx
        self.passed = self.sem("passed")

    def sem(self, name):
        return self.ctx.enter_context(self.nc.semaphore(name))

    def sb(self, ctx, name, shape, dt=F32):
        return ctx.enter_context(self.nc.sbuf_tensor(name, shape, dt))

    def pb(self, ctx, name, shape=(P, 512), dt=F32):
        return ctx.enter_context(self.nc.psum_tensor(name, list(shape), dt))


def wait_apart(eng, sem, value, passed):
    eng.wait_ge(sem, value)
    eng.sem_inc(passed, 1)


class LayerNorm:

    def __init__(self, K, ctx, tag, n):
        self.n = n
        self.stats = K.sb(ctx, f"{tag}_stats", [P, n, 6])
        self.meanvar = K.sb(ctx, f"{tag}_meanvar", [P, n, 2])
        self.var_eps = K.sb(ctx, f"{tag}_var_eps", [P, n])
        self.rstd = K.sb(ctx, f"{tag}_rstd", [P, n])
        self.stats_step = K.sem(f"{tag}_stats_step")
        self.passed = K.passed
        self.var_ready = K.sem(f"{tag}_var_ready")
        self.rstd_ready = K.sem(f"{tag}_rstd_ready")

    def statistics(self, dve, tiles, k, eps=LN_EPS):
        for n, x in enumerate(tiles):
            ins = dve.bn_stats(self.stats[:, n, :], x)
        ins.then_inc(self.stats_step, 1)
        wait_apart(dve, self.stats_step, 2 * k + 1, self.passed)
        for n in range(self.n):
            ins = dve.bn_aggr(self.meanvar[:, n, :], self.stats[:, n, :])
        ins.then_inc(self.stats_step, 1)
        dve.wait_ge(self.stats_step, 2 * k + 2)
        dve.tensor_scalar(self.var_eps[:, :], self.meanvar[:, :, 1], eps, None, ALU.add).then_inc(self.var_ready, 1)

    def root(self, pool, minus_half, k):
        pool.wait_ge(self.var_ready, k + 1)
        pool.tensor_tensor(self.rstd[:, :], self.var_eps[:, :], minus_half[:, 0:self.n], ALU.pow).then_inc(self.rstd_ready, 1)

    def apply(self, dve, tiles, outs, k):
        dve.wait_ge(self.rstd_ready, k + 1)
        for n, (x, o) in enumerate(zip(tiles, outs)):
            ins = dve.tensor_scalar(o, x, self.meanvar[:, n, 0:1], self.rstd[:, n:n + 1], ALU.subtract, ALU.mult)
        return ins


class Router:
    STEPS = 16

    def __init__(self, K, C, ctx, tag, bank, tiles, ids, rows):
        self.C, self.bank, self.tiles, self.ids, self.rows = C, bank, tiles, ids, rows
        self.sent = K.sb(ctx, f"{tag}_sent", [P, NT, 2, ROW])
        self.xnT = K.sb(ctx, f"{tag}_xnT", [P, SEQ])
        self.logits = K.sb(ctx, f"{tag}_logits", [P, NT, EXPERTS])
        self.best = K.sb(ctx, f"{tag}_best", [P, NT, 8])
        self.best_id = K.sb(ctx, f"{tag}_best_id", [P, NT, 8], U32)
        self.best_idf = K.sb(ctx, f"{tag}_best_idf", [P, NT, 2])
        self.gap = K.sb(ctx, f"{tag}_gap", [P, NT])
        self.ratio = K.sb(ctx, f"{tag}_ratio", [P, NT])
        self.denom = K.sb(ctx, f"{tag}_denom", [P, NT])
        self.weight = K.sb(ctx, f"{tag}_weight", [P, 2, NT])
        self.picked = K.sb(ctx, f"{tag}_picked", [P, 2, NT, EXPERTS])
        self.member = K.sb(ctx, f"{tag}_member", [P, NT, EXPERTS])
        self.before = K.sb(ctx, f"{tag}_before", [P, NT, EXPERTS])
        self.place = K.sb(ctx, f"{tag}_place", [P, NT, EXPERTS])
        self.place_of = K.sb(ctx, f"{tag}_place_of", [P, 2, NT])
        self.place_ids = K.sb(ctx, f"{tag}_place_id", [P, 2, 2, NT], U32)
        self.sents = [self.sent[:, :, :, :]]
        self.use(0)
        self.ln = LayerNorm(K, ctx, f"{tag}_ln", NT)
        self.begun = K.sem(f"{tag}_begun")
        self.xn_ready = K.sem(f"{tag}_xn_ready")
        self.xnT_done = K.sem(f"{tag}_xnT_done")
        self.xnT_ready = K.sem(f"{tag}_xnT_ready")
        self.logits_done = K.sem(f"{tag}_logits_done")
        self.gap_ready = K.sem(f"{tag}_gap_ready")
        self.ratio_ready = K.sem(f"{tag}_ratio_ready")
        self.route_step = K.sem(f"{tag}_route_step")
        self.member_ready = K.sem(f"{tag}_member_ready")
        self.rank_done = K.sem(f"{tag}_rank_done")
        self.place_ready = K.sem(f"{tag}_place_ready")
        self.sent_done = K.sem(f"{tag}_sent_done")

    def use(self, slot):
        self.slot, self.sent, self.place_id = slot, self.sents[slot], self.place_ids[:, slot, :, :]


    def begin(self, dve):
        dve.tensor_copy(self.C["filled"][:, :], self.C["regions"][:, :]).then_inc(self.begun, 1)
        dve.wait_ge(self.begun, 1)

    def then(self, dve, ins, r, step):
        ins.then_inc(self.route_step, 1)
        dve.wait_ge(self.route_step, r * self.STEPS + step)

    def statistics(self, dve, r):
        self.ln.statistics(dve, self.tiles(r), r)

    def normalize(self, dve, r):
        if self.slot == 0 and not (isinstance(r, int) and r == 0):
            dve.wait_ge(self.sent_done, r * 2 * NT * 16)
        self.ln.apply(dve, self.tiles(r), [self.sent[:, n, 0, 0:DIM] for n in range(NT)], r).then_inc(self.xn_ready, 1)
        dve.wait_ge(self.xn_ready, r + 1)
        dve.tensor_copy(self.sent[:, :, 1, 0:DIM], self.sent[:, :, 0, 0:DIM])
        dve.tensor_copy(self.sent[:, :, :, DIM + 1].bitcast(U32), self.ids(r))

    def choose(self, dve, r):
        dve.wait_ge(self.logits_done, r + 1)
        self.then(dve, dve.tensor_copy(self.logits[:, :, :],
                                       self.bank[:, 0:NT * EXPERTS].rearrange("p (a e) -> p a e", a=NT)), r, 1)
        wait_apart(dve, self.route_step, r * self.STEPS + 1, self.ln.passed)
        for n in range(NT):
            ins = dve.max(self.best[:, n, :], self.logits[:, n, :])
        self.then(dve, ins, r, 2)
        wait_apart(dve, self.route_step, r * self.STEPS + 2, self.ln.passed)
        for n in range(NT):
            dve.max_index(self.best_id[:, n, :], self.best[:, n, :], self.logits[:, n, :])
        dve.tensor_tensor(self.gap[:, :], self.best[:, :, 1], self.best[:, :, 0], ALU.subtract).then_inc(self.gap_ready, 1)
        dve.wait_ge(self.gap_ready, r + 1)
        self.then(dve, dve.tensor_copy(self.best_idf[:, :, :], self.best_id[:, :, 0:2]), r, 3)
        for k in range(2):
            ins = dve.tensor_tensor(self.picked[:, k, :, :],
                                    self.C["expert_ids"][:, :].unsqueeze(1).to_broadcast([P, NT, EXPERTS]),
                                    self.best_idf[:, :, k:k + 1].to_broadcast([P, NT, EXPERTS]), ALU.is_equal)
        self.then(dve, ins, r, 4)
        dve.tensor_tensor(self.member[:, :, :], self.picked[:, 0, :, :], self.picked[:, 1, :, :], ALU.add)\
            .then_inc(self.member_ready, 1)

    def weigh(self, dve, r):
        dve.wait_ge(self.ratio_ready, r + 1)
        self.then(dve, dve.tensor_scalar(self.denom[:, :], self.ratio[:, :], 1.0, None, ALU.add), r, 5)
        self.then(dve, dve.reciprocal(self.weight[:, 0, :], self.denom[:, :]), r, 6)
        self.then(dve, dve.tensor_tensor(self.weight[:, 1, :], self.weight[:, 0, :], self.ratio[:, :], ALU.mult), r, 7)
        for k in range(2):
            ins = dve.tensor_copy(self.sent[:, :, k, DIM], self.weight[:, k, :])
        self.then(dve, ins, r, 8)

    def placed(self, dve, r):
        dve.wait_ge(self.rank_done, r + 1)
        filled = self.C["filled"]
        total = self.bank[:, 64:96].rearrange("p (a e) -> p a e", a=NT)
        self.then(dve, dve.tensor_copy(self.before[:, 0, :], filled[:, :]), r, 9)
        for n in range(1, NT):
            self.then(dve, dve.tensor_tensor(self.before[:, n, :], self.before[:, n - 1, :], total[:, n - 1, :], ALU.add),
                      r, 9 + n)
        self.then(dve, dve.tensor_tensor(filled[:, :], self.before[:, NT - 1, :], total[:, NT - 1, :], ALU.add), r, 13)
        self.then(dve, dve.tensor_tensor(self.place[:, :, :], self.before[:, :, :],
                                         self.bank[:, 32:64].rearrange("p (a e) -> p a e", a=NT), ALU.add), r, 14)
        for k in range(2):
            ins = dve.tensor_tensor(self.picked[:, k, :, :], self.picked[:, k, :, :], self.place[:, :, :], ALU.mult)
        self.then(dve, ins, r, 15)
        self.then(dve, dve.tensor_reduce(self.place_of[:, :, :], self.picked[:, :, :, :], AX_X, ALU.add), r, 16)
        dve.tensor_copy(self.place_id, self.place_of[:, :, :]).then_inc(self.place_ready, 1)


    def turn(self, pe, r):
        if not (isinstance(r, int) and r == 0):
            pe.wait_ge(self.place_ready, r)
        pe.wait_ge(self.xn_ready, r + 1)
        for n in range(NT):
            ins = pe.transpose(self.bank[:, n * P:(n + 1) * P], self.sent[:, n, 0, 0:DIM], self.C["ident"][:, :])
        ins.then_inc(self.xnT_done, 1)

    def score(self, pe, r):
        pe.wait_ge(self.xnT_ready, r + 1)
        for n in range(NT):
            ins = pe.matmul(self.bank[:, n * EXPERTS:(n + 1) * EXPERTS], self.xnT[:, n * P:(n + 1) * P],
                            self.C["w_r"][:, :], start=True, stop=True)
        ins.then_inc(self.logits_done, 1)

    def rank(self, pe, r):
        pe.wait_ge(self.member_ready, r + 1)
        pe.matmul(self.bank[:, 32:64], self.C["earlier"][:, :], self.member[:, :, :], start=True, stop=True)
        pe.matmul(self.bank[:, 64:96], self.C["ones"][:, :], self.member[:, :, :], start=True, stop=True)\
            .then_inc(self.rank_done, 1)


    def turned(self, act, r):
        act.wait_ge(self.xnT_done, r + 1)
        act.copy(self.xnT[:, :], self.bank[:, :]).then_inc(self.xnT_ready, 1)

    def exponent(self, act, r):
        act.wait_ge(self.gap_ready, r + 1)
        act.activation(self.ratio[:, :], self.gap[:, :], ACT.Exp).then_inc(self.ratio_ready, 1)


    def root(self, pool, r):
        self.ln.root(pool, self.C["minus_half"], r)

    def send(self, pool, r):
        wait_apart(pool, self.place_ready, r + 1, self.ln.passed)
        for n in range(NT):
            for k in range(2):
                pool.indirect_dma_start(self.rows, bass.IndirectOffsetOnAxis(self.place_id[:, k, n:n + 1], 0),
                                        self.sent[:, n, k, :], None).then_inc(self.sent_done, 16)

    def finish(self, pool):
        pool.wait_ge(self.sent_done, BATCH * 2 * NT * 16)


class BlockTable:

    def __init__(self, K, C, tag, rows, scratch):
        self.C, self.rows, self.scratch = C, rows, scratch
        self.tail_ready, self.table_step = K.sem(f"{tag}_tail_ready"), K.sem(f"{tag}_table_step")
        self.table_ready = K.sem(f"{tag}_table_ready")
        self.filler_stored = K.sem(f"{tag}_filler_stored")

    def store_filler(self, sp):
        sp.dma_start(self.rows[UNUSED:UNUSED + P, :], self.C["filler"][:, :]).then_inc(self.filler_stored, 16)
        sp.wait_ge(self.tail_ready, 1)
        for e in range(EXPERTS):
            end = sp.value_load(self.C["tail"][0:1, e:e + 1], min_val=e * REGION, max_val=e * REGION + TOKENS)
            sp.dma_start(self.rows[bass.ds(end, P), :], self.C["filler"][:, :]).then_inc(self.filler_stored, 16)
        sp.wait_ge(self.filler_stored, 16 * (EXPERTS + 1))

    def make(self, dve):
        filled = self.C["filled"]
        o, parts = 0, []
        for shape in ((BLOCKS, EXPERTS + 1), (BLOCKS, EXPERTS), (2, BLOCKS)):
            parts.append(self.scratch[:, o:o + shape[0] * shape[1]].rearrange("p (a b) -> p a b", a=shape[0]))
            o += shape[0] * shape[1]
        past, inside, table_f = parts
        n_blocks, shift = self.scratch[:, o:o + EXPERTS], self.scratch[:, o + EXPERTS:o + 2 * EXPERTS]
        ends = self.scratch[:, o + 2 * EXPERTS:o + 3 * EXPERTS + 1]
        dve.tensor_copy(self.C["tail"][:, :], filled[:, :]).then_inc(self.tail_ready, 1)
        step = [0]

        def then(ins):
            step[0] += 1
            ins.then_inc(self.table_step, 1)
            dve.wait_ge(self.table_step, step[0])

        then(dve.tensor_tensor(shift[:, :], filled[:, :], self.C["regions"][:, :], ALU.subtract))
        then(dve.tensor_tensor(past[:, 0:TOKENS // P, 0:EXPERTS],
                               shift[:, :].unsqueeze(1).to_broadcast([P, TOKENS // P, EXPERTS]),
                               self.C["block_rows"][:, 0:TOKENS // P].unsqueeze(2).to_broadcast([P, TOKENS // P, EXPERTS]),
                               ALU.is_gt))
        then(dve.tensor_reduce(n_blocks[:, :], past[:, 0:TOKENS // P, 0:EXPERTS].rearrange("p b e -> p e b"), AX_X, ALU.add))
        then(dve.memset(ends[:, 0:1], 0.0))
        for e in range(EXPERTS):
            then(dve.scalar_tensor_tensor(out=ends[:, e + 1:e + 2], in0=n_blocks[:, e:e + 1], scalar=float(P),
                                          in1=ends[:, e:e + 1], op0=ALU.mult, op1=ALU.add))
        then(dve.tensor_tensor(past[:, :, :], self.C["block_rows"][:, :].unsqueeze(2).to_broadcast([P, BLOCKS, EXPERTS + 1]),
                               ends[:, :].unsqueeze(1).to_broadcast([P, BLOCKS, EXPERTS + 1]), ALU.is_ge))
        then(dve.tensor_tensor(inside[:, :, :], past[:, :, 0:EXPERTS], past[:, :, 1:EXPERTS + 1], ALU.subtract))
        then(dve.tensor_tensor(shift[:, :], self.C["regions"][:, :], ends[:, 0:EXPERTS], ALU.subtract))
        then(dve.tensor_scalar(shift[:, :], shift[:, :], -float(UNUSED), None, ALU.add))
        then(dve.tensor_reduce(table_f[:, 1, :], past[:, :, 1:EXPERTS + 1], AX_X, ALU.add))
        then(dve.tensor_scalar(table_f[:, 1, :], table_f[:, 1, :], float(EXPERTS - 1), None, ALU.min))
        then(dve.tensor_tensor(past[:, :, 0:EXPERTS], self.C["block_rows"][:, :].unsqueeze(2).to_broadcast([P, BLOCKS, EXPERTS]),
                               shift[:, :].unsqueeze(1).to_broadcast([P, BLOCKS, EXPERTS]), ALU.add))
        then(dve.tensor_tensor(inside[:, :, :], inside[:, :, :], past[:, :, 0:EXPERTS], ALU.mult))
        then(dve.tensor_reduce(table_f[:, 0, :], inside[:, :, :], AX_X, ALU.add))
        then(dve.tensor_scalar(table_f[:, 0, :], table_f[:, 0, :], float(UNUSED), None, ALU.add))
        dve.tensor_copy(self.C["table"][:, :, :], table_f[:, :, :]).then_inc(self.table_ready, 1)
        dve.wait_ge(self.table_ready, 1)


def load_experts(eng, C, inp, w_in):
    for e in range(EXPERTS):
        eng.dma_start(C["w1"][:, e, :], inp["W1"][e]).then_inc(w_in, 16)
        eng.dma_start(C["w2"][:, e, :, :], inp["W2"][e].rearrange("(a p) c -> p a c", p=P)).then_inc(w_in, 16)


def load_and_fold_weights(K, C, A, inp):
    nc = K.nc
    with ExitStack() as ctx:
        w_qkv = K.sb(ctx, "w_qkv", [P, 3 * HD])
        w_qkvT = K.sb(ctx, "w_qkvT", [P, 3 * PAIRS, P])
        rf_blk = K.sb(ctx, "rf_blk", [P, PAIRS, 2, DH])
        wout_blk = K.sb(ctx, "wout_blk", [P, PAIRS, 2, DIM])
        b_rows = K.sb(ctx, "b_rows", [P, 3 * PAIRS, DIM])
        beta_rows = K.sb(ctx, "beta_rows", [HEADS, DIM])
        wo_rows = K.sb(ctx, "wo_rows", [P, HD])
        banks = [K.pb(ctx, f"w_bank{i}") for i in range(8)]

        x_in = K.sem("x_in")
        wqkv_in = K.sem("wqkv_in")
        blk_zero = K.sem("blk_zero")
        blk_in = K.sem("blk_in")
        brows_in = K.sem("brows_in")
        ident_step = K.sem("ident_step")
        masks_ready = K.sem("masks_ready")
        w_bank_full = K.sem("w_bank_full")
        w_bank_read = [K.sem("w_bank_read0"), K.sem("w_bank_read1")]
        block = ctx.enter_context(nc.Block())

        fills = [("qkvT", i) for i in range(6)] + [("feat", i) for i in range(4)] + [("vo", i) for i in range(4)] \
            + [("bT", i) for i in range(6)] + [("betaT", 0)] + [("woT", i) for i in range(2)]

        def reader(n):
            return 1 if n < 6 or n % 2 else 0

        def reads(n):
            return sum(reader(i) == reader(n) for i in range(n + 1))

        def read_banks(eng, copy, which):
            for n, (kind, i) in enumerate(fills):
                if reader(n) != which:
                    continue
                eng.wait_ge(w_bank_full, n + 1)
                b = banks[n % 8]
                if kind == "qkvT":
                    ins = copy(w_qkvT[:, 4 * i:4 * i + 4, :], b[:, :].rearrange("p (a c) -> p a c", a=4))
                elif kind == "feat":
                    dst = A["feat_q"] if i < 2 else A["feat_k"]
                    ins = copy(dst[:, (i % 2) * 512:(i % 2) * 512 + 512], b[:, :])
                elif kind == "vo":
                    ins = copy(A["vo"][:, 4 * i:4 * i + 4, :], b[:, :].rearrange("p (a c) -> p a c", a=4))
                elif kind == "bT":
                    dst, o = (C["b_qkT"], i) if i < 4 else (C["b_vT"], i - 4)
                    ins = copy(dst[:, o * 512:o * 512 + 512], b[:, :])
                elif kind == "betaT":
                    eng.wait_ge(masks_ready, 1)
                    ins = copy(C["b_betaT"][:, 0:HEADS], b[:, 0:HEADS])
                else:
                    ins = copy(C["b_oT"][:, 4 * i:4 * i + 4, :], b[:, :].rearrange("p (a c) -> p a c", a=4))
                ins.then_inc(w_bank_read[which], 1)

        @block.sync
        def _(sp):
            sp.dma_start(w_qkv[:, :], inp["W_qkv"]).then_inc(wqkv_in, 16)
            for t in range(BATCH):
                sp.dma_start(C["x"][:, t * NT:(t + 1) * NT, :],
                             inp["x"][t].rearrange("(g p) c -> p g c", p=P)).then_inc(x_in, 16)
            sp.dma_start(C["b_out"][:, :], inp["b_out"].partition_broadcast(P)).then_inc(x_in, 16)
            sp.dma_start(C["ln_g"][:, :], inp["ln_g"].partition_broadcast(P)).then_inc(x_in, 16)
            sp.dma_start(C["ln_b"][:, :], inp["ln_b"].partition_broadcast(P)).then_inc(x_in, 16)
            sp.dma_start(C["w_r"][:, :], inp["Wr"]).then_inc(x_in, 16)
            sp.wait_ge(x_in, 16 * (BATCH + 4))
            load_experts(sp, C, inp, C["w_in"][0])

        @block.scalar
        def _(act):
            act.wait_ge(blk_zero, 2)
            for hh in range(2):
                rows = slice(hh * DH, (hh + 1) * DH)
                act.dma_start(rf_blk[rows, :, hh, :], inp["RF"].rearrange("(p e) d r -> e d p r", e=2)[hh]).then_inc(blk_in, 16)
                act.dma_start(wout_blk[rows, :, hh, :],
                              inp["W_out"].rearrange("(p e d) c -> e d p c", e=2, d=DH)[hh]).then_inc(blk_in, 16)
            qkvb = inp["w_qkvb"].rearrange("(p e r) c -> e r p c", e=2, r=3 * DH + 1)
            for kind in range(3):
                for hh in range(2):
                    act.dma_start(b_rows[hh * DH:(hh + 1) * DH, kind * PAIRS:(kind + 1) * PAIRS, :],
                                  qkvb[hh, kind * DH:(kind + 1) * DH]).then_inc(brows_in, 16)
            act.dma_start(beta_rows[:, :], inp["w_qkvb"].rearrange("(h r) c -> h r c", h=HEADS)[:, 3 * DH, :]).then_inc(brows_in, 16)
            act.dma_start(wo_rows[:, :], inp["w_o"]).then_inc(brows_in, 16)
            read_banks(act, act.copy, 0)

        @block.gpsimd
        def _(pool):
            pool.memset(rf_blk[:, :, :, :], 0.0).then_inc(blk_zero, 1)
            pool.memset(wout_blk[:, :, :, :], 0.0).then_inc(blk_zero, 1)
            pool.memset(C["ident"][:, :], 0.0).then_inc(ident_step, 1)
            pool.wait_ge(ident_step, 1)
            pool.affine_select(out=C["ident"][:, :], in_=C["ident"][:, :], compare_op=ALU.not_equal, fill=1.0, base=0,
                               pattern=[[-1, P]], channel_multiplier=1).then_inc(ident_step, 1)
            pool.wait_ge(masks_ready, 3)
            pool.affine_select(out=C["earlier"][:, :], in_=C["ones"][:, :], compare_op=ALU.is_gt, fill=0.0, base=0,
                               pattern=[[1, P]], channel_multiplier=-1).then_inc(ident_step, 1)
            pool.iota(C["part_ids"][:, :, :], [[P, BATCH * NT], [TOKENS, 2]], base=0, channel_multiplier=1)

        @block.vector
        def _(dve):
            dve.memset(C["b_betaT"][:, :], 0.0).then_inc(masks_ready, 1)
            dve.memset(C["head_ind"][:, :, :, :], 0.0).then_inc(masks_ready, 1)
            dve.memset(C["ones"][:, :], 1.0).then_inc(masks_ready, 1)
            dve.memset(C["filler"][:, 0:DIM + 1], 0.0)
            dve.memset(C["x"][:, BATCH * NT, :], 0.0)
            dve.memset(C["filler"][:, DIM + 1:ROW].bitcast(U32), NOWHERE)
            for j in range(BLOCKS):
                dve.memset(C["block_rows"][:, j:j + 1], float(P * j))
            for e in range(EXPERTS):
                dve.memset(C["regions"][:, e:e + 1], float(e * REGION))
            dve.memset(C["minus_half"][:, :], -0.5)
            for e in range(EXPERTS):
                dve.memset(C["expert_ids"][:, e:e + 1], float(e))
            dve.wait_ge(masks_ready, 2)
            for kind in range(2):
                for p in range(PAIRS):
                    for hh in range(2):
                        col = HEADS * kind + 2 * p + hh
                        dve.memset(C["head_ind"][hh * DH:(hh + 1) * DH, kind, p, col:col + 1], 1.0)
            read_banks(dve, dve.tensor_copy, 1)

        @block.tensor
        def _(pe):
            pe.wait_ge(ident_step, 2)
            ident = C["ident"]
            for n, (kind, i) in enumerate(fills):
                b = banks[n % 8]
                if n >= 8:
                    pe.wait_ge(w_bank_read[reader(n - 8)], reads(n - 8))
                if kind == "qkvT":
                    if i == 0:
                        pe.wait_ge(wqkv_in, 16)
                    for j in range(4):
                        q = 4 * i + j
                        ins = pe.transpose(b[:, j * P:(j + 1) * P], w_qkv[:, q * P:(q + 1) * P], ident[:, :])
                elif kind == "feat":
                    if i == 0:
                        pe.wait_ge(blk_in, 64)
                    pe.wait_ge(w_bank_read[1], 6)
                    for j in range(4):
                        q = 4 * i + j
                        ins = pe.matmul(b[:, j * P:(j + 1) * P], w_qkvT[:, q, :], rf_blk[:, q % PAIRS, :, :],
                                        start=True, stop=True)
                elif kind == "vo":
                    for j in range(2):
                        q = 2 * i + j
                        ins = pe.matmul(b[:, j * 256:(j + 1) * 256], w_qkvT[:, 2 * PAIRS + q, :], wout_blk[:, q, :, :],
                                        start=True, stop=True)
                elif kind == "bT":
                    if i == 0:
                        pe.wait_ge(brows_in, 128)
                    for j in range(4):
                        ins = pe.transpose(b[:, j * P:(j + 1) * P], b_rows[:, 4 * i + j, :], ident[:, :])
                elif kind == "betaT":
                    ins = pe.transpose(b[:, 0:HEADS], beta_rows[:, :], ident[0:HEADS, 0:HEADS])
                else:
                    for j in range(4):
                        q = 4 * i + j
                        ins = pe.transpose(b[:, j * P:(j + 1) * P], wo_rows[:, q * P:(q + 1) * P], ident[:, :])
                ins.then_inc(w_bank_full, 1)


def linear_attention(K, C, A, rows):
    nc = K.nc
    x = C["x"]
    with ExitStack() as ctx:
        xn = K.sb(ctx, "a_xn", [P, NT, DIM])
        xnT = K.sb(ctx, "a_xnT", [P, SEQ])
        phik = K.sb(ctx, "phik", [P, NT, HD])
        phik_sum = K.sb(ctx, "phik_sum", [P, HD])
        phiq = K.sb(ctx, "phiq", [P, NT, HD])
        phiqT = K.sb(ctx, "phiqT", [P, 2, PAIRS, P])
        kxT = K.sb(ctx, "kxT", [P, HD])
        kv = K.sb(ctx, "kv", [P, PAIRS, DIM])
        ksum = K.sb(ctx, "ksum", [P, HD])
        prod = K.sb(ctx, "a_prod", [P, HD])
        norm = K.sb(ctx, "a_norm", [P, HEADS])
        rnorm = K.sb(ctx, "a_rnorm", [P, 2, HEADS])
        ln = LayerNorm(K, ctx, "a_ln", NT)
        ring = [K.pb(ctx, f"a_ring{i}") for i in range(4)]
        kx_bank = [K.pb(ctx, f"a_kx{i}") for i in range(2)]
        y_bank = K.pb(ctx, "a_y")
        t_bank = K.pb(ctx, "a_t")

        xn_ready = K.sem("a_xn_ready")
        xnT_done = K.sem("a_xnT_done")
        xnT_ready = K.sem("a_xnT_ready")
        ring_full = K.sem("a_ring_full")
        act_read = K.sem("a_act_read")
        dve_read = K.sem("a_dve_read")
        presum_step = K.sem("a_presum_step")
        kx_done = K.sem("a_kx_done")
        kxT_ready = K.sem("a_kxT_ready")
        norm_step = K.sem("a_norm_step")
        rnorm_ready = K.sem("a_rnorm_ready")
        phiq_scaled = K.sem("a_phiq_scaled")
        bias_added = K.sem("a_bias_added")
        y_done = K.sem("a_y_done")
        y_added = K.sem("a_y_added")

        KSUM, KV, PHIQT, FILLS = 16, 18, 20, 28
        ACT_READS, DVE_READS = 24, 4

        def tiles(t):
            return [x[:, t * NT + n, :] if isinstance(t, int) else
                    x[:, bass.ds(t * NT + n, 1), :].rearrange("p a c -> p (a c)") for n in range(NT)]

        def x_of(t):
            return x[:, t * NT:(t + 1) * NT, :] if isinstance(t, int) else x[:, bass.ds(t * NT, NT), :]

        xn_tiles = [xn[:, n, :] for n in range(NT)]
        router = Router(K, C, ctx, "f_route", t_bank, tiles, lambda t: C["part_ids"][:, t * NT:(t + 1) * NT, :]
                        if isinstance(t, int) else C["part_ids"][:, bass.ds(t * NT, NT), :], rows)
        block_table = BlockTable(K, C, "f", rows, phik[:, 0:2, :].rearrange("p n c -> p (n c)"))
        block = ctx.enter_context(nc.Block())

        @block.sync
        def _(sp):
            block_table.store_filler(sp)

        @block.tensor
        def _(pe):
            def transposes(t):
                pe.wait_ge(xn_ready, t + 1)
                for n in range(NT):
                    ins = pe.transpose(t_bank[:, n * P:(n + 1) * P], xn[:, n, :], C["ident"][:, :])
                ins.then_inc(xnT_done, 1)

            def body(t, first, more):
                pe.wait_ge(xnT_ready, t + 1)
                for k in range(16):
                    if k == 9 and not first:
                        router.turn(pe, t - 1)
                    if k == 13 and not first:
                        router.score(pe, t - 1)
                    if k >= 4:
                        pe.wait_ge(act_read, t * ACT_READS + k - 3)
                    n, half = k % 8 // 2, k % 2
                    w = A["feat_k"] if k < 8 else A["feat_q"]
                    pe.matmul(ring[k % 4][:, :], xnT[:, n * P:(n + 1) * P], w[:, half * 512:half * 512 + 512],
                              start=True, stop=True).then_inc(ring_full, 1)
                pe.wait_ge(presum_step, 3 * t + 3)
                for half in range(2):
                    pe.wait_ge(act_read, t * ACT_READS + 13 + half)
                    pe.matmul(ring[half][:, :], C["ones"][:, :], phik_sum[:, half * 512:half * 512 + 512],
                              start=True, stop=True).then_inc(ring_full, 1)
                for half in range(2):
                    for n in range(NT):
                        ins = pe.matmul(kx_bank[half][:, :], xn[:, n, :], phik[:, n, half * 512:half * 512 + 512],
                                        start=(n == 0), stop=(n == NT - 1))
                    ins.then_inc(kx_done, 1)
                if not first:
                    router.rank(pe, t - 1)
                pe.wait_ge(kxT_ready, 2 * t + 2)
                for q in range(2):
                    pe.wait_ge(act_read, t * ACT_READS + 15 + q)
                    for j in range(4):
                        for hh in range(2):
                            h = 2 * (4 * q + j) + hh
                            ins = pe.matmul(ring[2 + q][hh * DH:(hh + 1) * DH, j * P:(j + 1) * P],
                                            kxT[:, h * DH:(h + 1) * DH], A["vo"][:, h, :], start=True, stop=True)
                    ins.then_inc(ring_full, 1)

                def turn_phiq(n):
                    pe.wait_ge(phiq_scaled, t * NT + n + 1)
                    for q in range(2):
                        if n < 2:
                            pe.wait_ge(dve_read, t * DVE_READS + 2 * n + q + 1)
                        else:
                            pe.wait_ge(act_read, t * ACT_READS + 16 + 2 * (n - 2) + q + 1)
                        for j in range(4):
                            p = 4 * q + j
                            ins = pe.transpose(ring[(2 * n + q) % 4][:, j * P:(j + 1) * P], phiq[:, n, p * P:(p + 1) * P],
                                               C["ident"][:, :])
                        ins.then_inc(ring_full, 1)

                def output(n):
                    pe.wait_ge(act_read, t * ACT_READS + 16 + 2 * n + 2)
                    pe.wait_ge(dve_read, t * DVE_READS + 4)
                    for p in range(PAIRS):
                        ins = pe.matmul(y_bank[:, n * P:(n + 1) * P], phiqT[:, n % 2, p, :], kv[:, p, :],
                                        start=(p == 0), stop=(p == PAIRS - 1))
                    ins.then_inc(y_done, 1)

                turn_phiq(0)
                for n in range(NT):
                    if n + 1 < NT:
                        turn_phiq(n + 1)
                    elif more:
                        if not first:
                            pe.wait_ge(router.place_ready, t)
                        transposes(t + 1)
                    output(n)

            transposes(0)
            body(0, True, True)
            with pe.Fori(1, BATCH - 1) as t:
                body(t, False, True)
            body(BATCH - 1, False, False)
            router.turn(pe, BATCH - 1)
            router.score(pe, BATCH - 1)
            router.rank(pe, BATCH - 1)

        @block.scalar
        def _(act):
            def copy_xnT(t):
                act.wait_ge(xnT_done, t + 1)
                act.copy(xnT[:, :], t_bank[:, :]).then_inc(xnT_ready, 1)

            def body(t, first, more):
                for k in range(16):
                    if k == 12 and not first:
                        router.turned(act, t - 1)
                    act.wait_ge(ring_full, t * FILLS + k + 1)
                    dst = phik if k < 8 else phiq
                    act.activation(dst[:, k % 8 // 2, (k % 2) * 512:(k % 2) * 512 + 512], ring[k % 4][:, :], ACT.Relu)\
                        .then_inc(act_read, 1)
                if not first:
                    router.exponent(act, t - 1)
                for n in range(NT):
                    for q in range(2):
                        act.wait_ge(ring_full, t * FILLS + PHIQT + 2 * n + q + 1)
                        if n >= 2 and q == 0:
                            act.wait_ge(y_done, t * NT + n - 1)
                        act.copy(phiqT[:, n % 2, 4 * q:4 * q + 4, :],
                                 ring[(2 * n + q) % 4][:, :].rearrange("p (a c) -> p a c", a=4)).then_inc(act_read, 1)
                if more:
                    copy_xnT(t + 1)

            copy_xnT(0)
            body(0, True, True)
            with act.Fori(1, BATCH - 1) as t:
                body(t, False, True)
            body(BATCH - 1, False, False)
            router.turned(act, BATCH - 1)
            router.exponent(act, BATCH - 1)

        @block.gpsimd
        def _(pool):
            def body(t, first, more):
                if not first:
                    router.root(pool, t - 1)
                pool.wait_ge(act_read, t * ACT_READS + 4)
                pool.tensor_tensor(phik_sum[:, :], phik[:, 0, :], phik[:, 1, :], ALU.add).then_inc(presum_step, 1)
                for n in range(2, NT):
                    pool.wait_ge(act_read, t * ACT_READS + 2 * n + 2)
                    pool.wait_ge(presum_step, 3 * t + n - 1)
                    pool.tensor_tensor(phik_sum[:, :], phik_sum[:, :], phik[:, n, :], ALU.add).then_inc(presum_step, 1)
                pool.wait_ge(xn_ready, t + 1)
                pool.tensor_tensor(x_of(t), x_of(t), C["b_out"][:, :].unsqueeze(1).to_broadcast([P, NT, DIM]), ALU.add)\
                    .then_inc(bias_added, 1)
                if more:
                    ln.root(pool, C["minus_half"], t + 1)
                for n in range(NT):
                    pool.wait_ge(rnorm_ready, t * NT + n + 1)
                    by_head = phiq[:, n, :].rearrange("p (h r) -> p h r", h=HEADS)
                    pool.tensor_tensor(by_head, by_head, rnorm[:, n % 2, :].unsqueeze(2).to_broadcast([P, HEADS, DH]),
                                       ALU.mult).then_inc(phiq_scaled, 1)
                if not first:
                    router.send(pool, t - 1)

            ln.root(pool, C["minus_half"], 0)
            body(0, True, True)
            with pool.Fori(1, BATCH - 1) as t:
                body(t, False, True)
            body(BATCH - 1, False, False)
            router.root(pool, BATCH - 1)
            router.send(pool, BATCH - 1)
            router.finish(pool)

        @block.vector
        def _(dve):
            def body(t, first, more):
                if not first:
                    router.statistics(dve, t - 1)
                    router.normalize(dve, t - 1)
                    router.choose(dve, t - 1)
                if more:
                    ln.statistics(dve, tiles(t + 1), t + 1)
                for half in range(2):
                    dve.wait_ge(ring_full, t * FILLS + KSUM + half + 1)
                    dve.tensor_copy(ksum[:, half * 512:half * 512 + 512], ring[half][:, :]).then_inc(dve_read, 1)
                dve.wait_ge(dve_read, t * DVE_READS + 2)

                def normalizer(n):
                    dve.wait_ge(act_read, t * ACT_READS + 8 + 2 * n + 2)
                    dve.tensor_tensor(prod[:, :], phiq[:, n, :], ksum[:, :], ALU.mult).then_inc(norm_step, 1)
                    dve.wait_ge(norm_step, (t * NT + n) * 3 + 1)
                    dve.tensor_reduce(norm[:, :], prod[:, :].rearrange("p (h r) -> p h r", h=HEADS), AX_X, ALU.add)\
                        .then_inc(norm_step, 1)
                    dve.wait_ge(norm_step, (t * NT + n) * 3 + 2)
                    dve.tensor_scalar(norm[:, :], norm[:, :], STAB, None, ALU.add).then_inc(norm_step, 1)
                    dve.wait_ge(norm_step, (t * NT + n) * 3 + 3)
                    if n >= 2:
                        dve.wait_ge(phiq_scaled, t * NT + n - 1)
                    dve.reciprocal(rnorm[:, n % 2, :], norm[:, :]).then_inc(rnorm_ready, 1)

                normalizer(0)
                normalizer(1)
                for half in range(2):
                    dve.wait_ge(kx_done, 2 * t + half + 1)
                    dve.tensor_copy(kxT[:, half * 512:half * 512 + 512], kx_bank[half][:, :]).then_inc(kxT_ready, 1)
                normalizer(2)
                for q in range(2):
                    dve.wait_ge(ring_full, t * FILLS + KV + q + 1)
                    dve.tensor_copy(kv[:, 4 * q:4 * q + 4, :], ring[2 + q][:, :].rearrange("p (a c) -> p a c", a=4))\
                        .then_inc(dve_read, 1)
                normalizer(3)
                if more:
                    ln.apply(dve, tiles(t + 1), xn_tiles, t + 1).then_inc(xn_ready, 1)
                if not first:
                    router.weigh(dve, t - 1)
                    router.placed(dve, t - 1)
                dve.wait_ge(y_done, (t + 1) * NT)
                dve.wait_ge(bias_added, t + 1)
                dve.tensor_tensor(x_of(t), x_of(t), y_bank[:, :].rearrange("p (a c) -> p a c", a=NT), ALU.add)\
                    .then_inc(y_added, 1)
                dve.wait_ge(y_added, t + 1)

            router.begin(dve)
            ln.statistics(dve, tiles(0), 0)
            ln.apply(dve, tiles(0), xn_tiles, 0).then_inc(xn_ready, 1)
            body(0, True, True)
            with dve.Fori(1, BATCH - 1) as t:
                body(t, False, True)
            body(BATCH - 1, False, False)
            router.statistics(dve, BATCH - 1)
            router.normalize(dve, BATCH - 1)
            router.choose(dve, BATCH - 1)
            router.weigh(dve, BATCH - 1)
            router.placed(dve, BATCH - 1)
            block_table.make(dve)


def expert_ffn(K, C, tag, n_use, rows, parts, out=None):
    nc = K.nc
    x = C["x"]
    with ExitStack() as ctx:
        w1, w2, table = C["w1"], C["w2"], C["table"]
        blk = K.sb(ctx, f"{tag}_blk", [P, UNROLL, ROW])
        meta = K.sb(ctx, f"{tag}_meta", [P, UNROLL, ROW - DIM])
        blkT = K.sb(ctx, f"{tag}_blkT", [P, UNROLL, P])
        w1_now = K.sb(ctx, f"{tag}_w1_now", [P, UNROLL, FF])
        w2_now = K.sb(ctx, f"{tag}_w2_now", [P, UNROLL, FC * DIM])
        hidT = K.sb(ctx, f"{tag}_hidT", [P, UNROLL, FC, P])
        y = K.sb(ctx, f"{tag}_y", [P, UNROLL, DIM])
        PART_SLOTS = 4
        part = K.sb(ctx, f"{tag}_part", [P, PART_SLOTS, 2, NT, DIM]) if out is not None else None
        t_bank = [K.pb(ctx, f"{tag}_t{i}") for i in range(2)]
        hid_bank = [K.pb(ctx, f"{tag}_hid{i}") for i in range(2)]
        y_bank = [K.pb(ctx, f"{tag}_yb{i}") for i in range(2)]

        def sem(name):
            return K.sem(f"{tag}_{name}")

        w_in = C["w_in"][n_use]
        blk_in = [sem(f"blk_in{i}") for i in range(UNROLL)]
        blkT_done, blkT_ready, meta_ready = sem("blkT_done"), sem("blkT_ready"), sem("meta_ready")
        w1_ready, w2_ready = sem("w1_ready"), sem("w2_ready")
        hid_done, hid_ready, y_done, y_ready = sem("hid_done"), sem("hid_ready"), sem("y_done"), sem("y_ready")
        y_stored = [sem(f"y_stored{i}") for i in range(UNROLL)]
        if out is not None:
            part_in = [sem(f"part_in{i}") for i in range(PART_SLOTS)]
            sum_step, x_stored = sem("sum_step"), sem("x_stored")
        block = ctx.enter_context(nc.Block())

        def x_of(t):
            return x[:, t * NT:(t + 1) * NT, :]

        @block.sync
        def _(sp):
            with sp.Fori(0, BLOCKS // UNROLL) as i:
                for u in range(UNROLL):
                    first = sp.value_load(table[0:1, 0, bass.ds(i * UNROLL + u, 1)], min_val=0, max_val=UNUSED)
                    sp.wait_ge(blkT_done, i * UNROLL + u + 1)
                    sp.wait_ge(meta_ready, i * UNROLL + u + 1)
                    sp.dma_start(blk[:, u, :], rows[bass.ds(first, P), :]).then_inc(blk_in[u], 16)
            for u in range(UNROLL):
                sp.wait_ge(y_stored[u], BLOCKS // UNROLL * 16)
            if out is None:
                return
            for t in range(BATCH):
                if t >= PART_SLOTS:
                    sp.wait_ge(sum_step, 2 * (t - PART_SLOTS) + 2)
                for k in range(2):
                    sp.dma_start(part[:, t % PART_SLOTS, k, :, :],
                                 parts.rearrange("(k t g p) c -> k t p g c", k=2, t=BATCH, p=P)[k, t])\
                        .then_inc(part_in[t % PART_SLOTS], 16)

        @block.gpsimd
        def _(pool):
            with pool.Fori(0, BLOCKS // UNROLL) as i:
                for u in range(UNROLL):
                    wait_apart(pool, y_ready, i * UNROLL + u + 1, K.passed)
                    pool.indirect_dma_start(parts, bass.IndirectOffsetOnAxis(meta[:, u, 1:2].bitcast(U32), 0), y[:, u, :], None,
                                            bounds_check=2 * TOKENS - 1, oob_is_err=False).then_inc(y_stored[u], 16)

        @block.tensor
        def _(pe):
            pe.sem_inc(blkT_done, UNROLL)
            pe.wait_ge(w_in, 32 * EXPERTS)

            def turn(i, u, done):
                pe.wait_ge(blk_in[u], 16 * (i + 1))
                if done is not None:
                    pe.wait_ge(blkT_ready, done - 1)
                pe.transpose(t_bank[u % 2][:, 0:P], blk[:, u, 0:DIM], C["ident"][:, :]).then_inc(blkT_done, 1)

            def hidden(i, u, j):
                pe.wait_ge(blkT_ready, j + 1)
                pe.wait_ge(w1_ready, j + 1)
                if not (isinstance(j, int) and j < 2):
                    pe.wait_ge(hid_ready, j - 1)
                for f in range(FC):
                    ins = pe.matmul(hid_bank[u % 2][:, f * P:(f + 1) * P], w1_now[:, u, f * P:(f + 1) * P], blkT[:, u, :],
                                    start=True, stop=True)
                ins.then_inc(hid_done, 1)

            def output(i, u, j, first):
                pe.wait_ge(w2_ready, j + 1)
                pe.wait_ge(hid_ready, j + 1)
                if not first:
                    pe.wait_ge(y_ready, j - 1)
                for f in range(FC):
                    ins = pe.matmul(y_bank[u % 2][:, 0:P], hidT[:, u, f, :], w2_now[:, u, f * DIM:(f + 1) * DIM],
                                    start=(f == 0), stop=(f == FC - 1))
                ins.then_inc(y_done, 1)

            turn(0, 0, None)
            turn(0, 1, None)
            hidden(0, 0, 0)

            def body(i, lead, tail_end):
                for u in range(UNROLL):
                    j = i * UNROLL + u
                    if not (tail_end and u + 2 >= UNROLL):
                        turn(i + (u + 2) // UNROLL, (u + 2) % UNROLL, j + 2)
                    if not (tail_end and u + 1 >= UNROLL):
                        hidden(i + (u + 1) // UNROLL, (u + 1) % UNROLL, j + 1)
                    output(i, u, j, lead and u < 2)

            body(0, True, False)
            with pe.Fori(1, BLOCKS // UNROLL - 1) as i:
                body(i, False, False)
            body(BLOCKS // UNROLL - 1, False, True)

        @block.scalar
        def _(act):
            def turned(i, u):
                j = i * UNROLL + u
                act.wait_ge(blkT_done, UNROLL + j + 1)
                act.copy(blkT[:, u, :], t_bank[u % 2][:, 0:P]).then_inc(blkT_ready, 1)

            turned(0, 0)
            turned(0, 1)

            def body(i, tail_end):
                for u in range(UNROLL):
                    j = i * UNROLL + u
                    act.wait_ge(hid_done, j + 1)
                    act.activation(hidT[:, u, :, :], hid_bank[u % 2][:, :].rearrange("p (f n) -> p f n", f=FC), ACT.Relu)\
                        .then_inc(hid_ready, 1)
                    if not (tail_end and u + 2 >= UNROLL):
                        turned(i + (u + 2) // UNROLL, (u + 2) % UNROLL)

            with act.Fori(0, BLOCKS // UNROLL - 1) as i:
                body(i, False)
            body(BLOCKS // UNROLL - 1, True)
            if out is None:
                return
            for t in range(BATCH):
                act.wait_ge(sum_step, 2 * t + 2)
                act.dma_start(out[t].rearrange("(g p) c -> p g c", p=P), x_of(t)).then_inc(x_stored, 16)
            act.wait_ge(x_stored, 16 * BATCH)

        @block.vector
        def _(dve):
            dve.sem_inc(meta_ready, UNROLL)
            dve.wait_ge(w_in, 32 * EXPERTS)

            def take(i, u, j, first):
                e = dve.value_load(table[0:1, 1, bass.ds(i * UNROLL + u, 1)], min_val=0, max_val=EXPERTS - 1)
                dve.wait_ge(blk_in[u], 16 * (i + 1))
                if not first:
                    dve.wait_ge(y_done, j - UNROLL + 1)
                    dve.wait_ge(y_stored[u], 16 * i)
                dve.tensor_copy(meta[:, u, :], blk[:, u, DIM:ROW]).then_inc(meta_ready, 1)
                dve.tensor_copy(w1_now[:, u, :], w1[:, bass.ds(e, 1), :].rearrange("p a f -> p (a f)")).then_inc(w1_ready, 1)
                dve.tensor_copy(w2_now[:, u, :], w2[:, bass.ds(e, 1), :, :].rearrange("p a f c -> p (a f c)")).then_inc(w2_ready, 1)

            def weigh(i, u, j):
                dve.wait_ge(y_done, j + 1)
                dve.wait_ge(meta_ready, UNROLL + j + 1)
                dve.tensor_scalar(y[:, u, :], y_bank[u % 2][:, 0:P], meta[:, u, 0:1], None, ALU.mult).then_inc(y_ready, 1)

            AHEAD = 2
            take(0, 0, 0, True)
            take(0, 1, 1, True)

            def body(i, lead, tail_end):
                for u in range(UNROLL):
                    j = i * UNROLL + u
                    if not (tail_end and u + AHEAD >= UNROLL):
                        take(i + (u + AHEAD) // UNROLL, (u + AHEAD) % UNROLL, j + AHEAD, lead and u + AHEAD < UNROLL)
                    weigh(i, u, j)

            body(0, True, False)
            with dve.Fori(1, BLOCKS // UNROLL - 1) as i:
                body(i, False, False)
            body(BLOCKS // UNROLL - 1, False, True)

            if out is None:
                return
            for t in range(BATCH):
                dve.wait_ge(part_in[t % PART_SLOTS], 32 * (t // PART_SLOTS + 1))
                for k in range(2):
                    if k:
                        dve.wait_ge(sum_step, 2 * t + 1)
                    dve.tensor_tensor(x_of(t), x_of(t), part[:, t % PART_SLOTS, k, :, :], ALU.add).then_inc(sum_step, 1)


def delta_memory(K, C, cd, gd, inp, rows, parts):
    nc = K.nc
    x = C["x"]
    QH = HEADS // 4
    with ExitStack() as ctx:
        h = K.sb(ctx, "b_h", [P, T, DIM])
        hT = K.sb(ctx, "b_hT", [P, TOK])
        pos_exp = K.sb(ctx, "b_exp", [P, 2, 512])
        kq = K.sb(ctx, "b_kq", [P, 2, 2, TOK])
        gram = C["wide"][:, :].rearrange("p (a b k h) -> p a b k h", a=NTAU, b=32, k=2)
        outT = K.sb(ctx, "b_outT", [P, 2, TOK])
        res = outT[:, 0, :].rearrange("p (t c) -> p t c", t=T)
        v = K.sb(ctx, "b_v", [P, NTAU, HD])
        part = v[:, :, :].rearrange("p (g k) c -> p g k c", k=2)
        coef = K.sb(ctx, "b_coef", [P, T, T, 2, HEADS])
        sums = K.sb(ctx, "b_sums", [P, 2, T, 2, HEADS])
        rsum = K.sb(ctx, "b_rsum", [P, T, 2, HEADS])
        den = K.sb(ctx, "b_den", [P, T, 2, HEADS])
        rden = K.sb(ctx, "b_rden", [P, T, 2, HEADS])
        beta = K.sb(ctx, "b_beta", [P, T, HEADS])
        gamma = K.sb(ctx, "b_gamma", [P, T, HEADS])
        alpha = K.sb(ctx, "b_alpha", [P, T, HEADS])
        inv = K.sb(ctx, "b_inv", [P, T, T, HEADS])
        prod = K.sb(ctx, "b_prod", [P, T, T, HEADS])
        mix = K.sb(ctx, "b_mix", [P, T, T, HEADS])
        spread = K.sb(ctx, "b_spread", [P, 2, NTAU, BL * T, QH])
        sums_raw = prod[:, 0:4, :, :].rearrange("p a t h -> p (a t h)").rearrange("p (a t b) -> p a t b", a=2, t=T)
        mix_q = prod[:, :, :, :].rearrange("p u t h -> p u (t h)").rearrange("p u (q t h) -> p u q t h", q=4, t=T)
        ln = LayerNorm(K, ctx, "b_ln", T)
        ring = [K.pb(ctx, f"b_ring{i}") for i in range(4)]
        g_bank = [K.pb(ctx, f"b_g{i}") for i in range(2)]
        s_bank = K.pb(ctx, "b_s")
        r_bank = K.pb(ctx, "b_r")

        names = ["h_ready", "hT_full", "hT_ready", "v_full", "v_ready", "kq_full", "rel_read", "kq_ready",
                 "gram_done", "gram_read0", "gram_read1", "sums_read", "beta_logit", "beta_exp", "solve_step",
                 "gram_stored", "coef_loaded", "mix_stored", "spread_loaded0", "spread_loaded1", "spread_zero", "mixed_full", "outT_ready",
                 "att_done", "att_read", "resid_step", "normed", "scaled", "x_ready", "parts_added"]
        S = {n: K.sem(f"b_{n}") for n in names}
        part_in = [K.sem(f"b_part_in{g}") for g in range(NG)]
        STEPS = 50

        def x_tile(g, t):
            return x[:, bass.ds(g + t * NG, 1), :].rearrange("p a c -> p (a c)") if not isinstance(g, int) \
                else x[:, g + t * NG, :]

        def routed_ids(m, j):
            by_group = C["part_ids"][:, :, :].rearrange("p (t g) k -> p g t k", g=NG)
            return by_group[:, m, 4 * j:4 * j + 4, :] if isinstance(m, int) else \
                by_group[:, bass.ds(m, 1), 4 * j:4 * j + 4, :].rearrange("p a t k -> p (a t) k")

        router = Router(K, C, ctx, "g_route", r_bank, None, None, rows)
        kq_flat = kq[:, :, :, :].rearrange("p a b n -> p (a b n)")
        router.sents.append(kq_flat[:, TOK * 2:TOK * 2 + 2 * NT * ROW].rearrange("p (n k c) -> p n k c", n=NT, k=2))
        block_table = BlockTable(K, C, "g", rows, kq_flat[:, 0:TOK * 2])

        def route(m, j):
            router.tiles = lambda r: [x_tile(m, 4 * j + n) for n in range(NT)]
            router.ids = lambda r: routed_ids(m, j)
            return 2 * m + j

        block = ctx.enter_context(nc.Block())

        def scale_and_add(eng, m):
            by_group = x[:, 0:BATCH * NT, :].rearrange("p (t g) c -> p g t c", g=NG)
            x_m = by_group[:, m, :, :] if isinstance(m, int) else by_group[:, bass.ds(m, 1), :, :].rearrange("p a t c -> p (a t) c")
            eng.wait_ge(S["normed"], m + 1)
            eng.tensor_tensor(res, res, C["ln_g"][:, :].unsqueeze(1).to_broadcast([P, T, DIM]), ALU.mult)\
                .then_inc(S["scaled"], 1)
            eng.wait_ge(S["scaled"], 2 * m + 1)
            eng.tensor_tensor(res, res, C["ln_b"][:, :].unsqueeze(1).to_broadcast([P, T, DIM]), ALU.add)\
                .then_inc(S["scaled"], 1)
            eng.wait_ge(S["scaled"], 2 * m + 2)
            eng.tensor_tensor(x_m, x_m, res, ALU.add).then_inc(S["x_ready"], 1)

        @block.sync
        def _(sp):
            def store_products(g):
                sp.wait_ge(S["gram_read0"], (g + 1) * PAIRS)
                wait_apart(sp, S["gram_read1"], (g + 1) * PAIRS, K.passed)
                if not (isinstance(g, int) and g == 0):
                    sp.wait_ge(S["coef_loaded"], g * 16)
                for b in range(BL):
                    sp.dma_start(gd.rearrange("(a b) s n -> b s a n", b=BL)[b],
                                 gram[b * T:(b + 1) * T, :, (b % 4) * T:(b % 4 + 1) * T, :, :]
                                 .rearrange("p a t k h -> p a (t k h)")).then_inc(S["gram_stored"], 16)

            def load_coef(g):
                wait_apart(sp, S["gram_stored"], (g + 1) * 16 * BL, K.passed)
                if not (isinstance(g, int) and g == 0):
                    sp.wait_ge(S["solve_step"], g * STEPS)
                sp.dma_start(coef[:, :, :, :, :].rearrange("p s t k h -> p (s t k h)"), gd.rearrange("b s n -> b (s n)"))\
                    .then_inc(S["coef_loaded"], 16)

            def store_mix(m):
                sp.wait_ge(S["solve_step"], (m + 1) * STEPS)
                sp.dma_start(cd.rearrange("b u q n -> b (u q n)"), prod[:, :, :, :].rearrange("p u t h -> p (u t h)"))\
                    .then_inc(S["mix_stored"], 16)
                wait_apart(sp, S["mix_stored"], (m + 1) * 16, K.passed)

            def load_spread(m, q):
                sp.wait_ge(S["outT_ready"], 16 * (m + 1) + 4 * (q - 1))
                for b in range(BL):
                    sp.dma_start(spread[b * T:(b + 1) * T, q % 2, :, b * T:(b + 1) * T, :].rearrange("p a t h -> p a (t h)"),
                                 cd.rearrange("(a b) u q n -> q b u a n", b=BL)[q, b])\
                        .then_inc(S[f"spread_loaded{q % 2}"], 16)

            for g in range(NG):
                for k in range(2):
                    sp.dma_start(part[:, g, k, :].rearrange("p (t c) -> p t c", t=T),
                                 parts.rearrange("(k t g p) c -> k g p t c", k=2, t=T, p=P)[k, g]).then_inc(part_in[g], 16)
            sp.wait_ge(S["spread_zero"], 1)
            def body(g):
                m = g - 1
                store_mix(m)
                load_spread(m, 0)
                load_spread(m, 1)
                store_products(g)
                load_spread(m, 2)
                load_coef(g)
                load_spread(m, 3)
                for i in range(2):
                    wait_apart(sp, S[f"spread_loaded{i}"], (m + 1) * 2 * 16 * BL, K.passed)

            store_products(0)
            load_coef(0)
            body(1)
            with sp.Fori(2, NG) as g:
                body(g)
            load_experts(sp, C, inp, C["w_in"][1])
            store_mix(NG - 1)
            for q in range(4):
                load_spread(NG - 1, q)
            block_table.store_filler(sp)

        @block.gpsimd
        def _(pool):
            def routed(m, j):
                router.root(pool, 2 * m + j)
                router.send(pool, 2 * m + j)

            def root(k):
                ln.root(pool, C["minus_half"], k)

            root(0)
            root(1)
            for i in range(3):
                root(2 + i)
            scale_and_add(pool, 0)
            with pool.Fori(2, NG) as g:
                for j in range(2):
                    routed(g - 2, j)
                for i in range(3):
                    root(3 * g - 1 + i)
                scale_and_add(pool, g - 1)
            for j in range(2):
                router.use(j)
                routed(NG - 2, j)
            for i in range(2):
                root(3 * NG - 1 + i)
            for j in range(2):
                router.root(pool, 2 * (NG - 1) + j)
            for j in range(2):
                router.use(j)
                router.send(pool, 2 * (NG - 1) + j)
            router.use(0)
            router.finish(pool)

        @block.tensor
        def _(pe):
            def values(m):
                pe.wait_ge(S["rel_read"], 32 * (m + 1))
                pe.wait_ge(S["outT_ready"], 16 * (m + 1))
                for k in range(16):
                    if k >= 4:
                        pe.wait_ge(S["v_ready"], 16 * m + k - 3)
                    pe.matmul(ring[k % 4][:, :], hT[:, (k // 2) * P:(k // 2 + 1) * P],
                              C["b_vT"][:, (k % 2) * 512:(k % 2) * 512 + 512], start=True, stop=True)\
                        .then_inc(S["v_full"], 1)

            def routing(m, p):
                j = p // 4
                if p % 4 == 1:
                    router.turn(pe, 2 * m + j)
                elif p % 4 == 2:
                    router.score(pe, 2 * m + j)
                elif p % 4 == 3:
                    router.rank(pe, 2 * m + j)

            def keys_and_queries(g, routed):
                later = not (isinstance(g, int) and g == 0)
                if later:
                    pe.wait_ge(S["v_ready"], 16 * g)
                pe.wait_ge(S["h_ready"], g + 1)
                for q in range(2):
                    for j in range(4):
                        ins = pe.transpose(ring[q][:, j * P:(j + 1) * P], h[:, 4 * q + j, :], C["ident"][:, :])
                    ins.then_inc(S["hT_full"], 1)
                pe.wait_ge(S["hT_ready"], 2 * g + 2)
                if later:
                    pe.wait_ge(S["sums_read"], g)
                for j in range(4):
                    pe.matmul(s_bank[32 * j:32 * j + 32, 256:512], C["b_betaT"][:, :], hT[:, 256 * j:256 * j + 256],
                              start=True, stop=True)

                def project(p):
                    for k in range(4):
                        n = 4 * p + k
                        if n >= 4:
                            pe.wait_ge(S["rel_read"], 32 * g + n - 3)
                        kind, half = k // 2, k % 2
                        w = C["b_qkT"][:, (1 - kind) * HD + p * P:(1 - kind) * HD + (p + 1) * P]
                        pe.matmul(ring[n % 4][:, :], w, hT[:, half * 512:half * 512 + 512], start=True, stop=True)\
                            .then_inc(S["kq_full"], 1)

                def products(p):
                    pe.wait_ge(S["kq_ready"], 32 * g + 4 * p + 4)
                    for kind in range(2):
                        for j in range(4):
                            pe.matmul(s_bank[32 * j:32 * j + 32, 0:256], C["head_ind"][:, kind, p, :],
                                      kq[:, p % 2, kind, 256 * j:256 * j + 256], start=(p == 0 and kind == 0),
                                      stop=(p == PAIRS - 1 and kind == 1), skip_group_check=True)
                    if p >= 1:
                        pe.wait_ge(S["gram_read0"], PAIRS * g + p)
                        pe.wait_ge(S["gram_read1"], PAIRS * g + p)
                    elif later:
                        pe.wait_ge(S["att_read"], g)
                    wait_apart(pe, S["kq_ready"], 32 * g + 4 * p + 4, K.passed)
                    for a in range(NTAU):
                        for j in range(4):
                            c = (4 * a + j) * 32
                            for hh in range(2):
                                r = slice(hh * DH, (hh + 1) * DH)
                                ins = pe.matmul(g_bank[hh][32 * j:32 * j + 32, a * 64:(a + 1) * 64],
                                                kq[r, p % 2, 0, c:c + 32], kq[r, p % 2, :, c:c + 32], start=True, stop=True)
                    ins.then_inc(S["gram_done"], 1)

                project(0)
                for p in range(PAIRS):
                    if p + 1 < PAIRS:
                        project(p + 1)
                    products(p)
                    if routed is not None:
                        routing(routed, p)

            def mix_values(m, grams, routed=None):
                pe.wait_ge(S["rel_read"], 32 * grams)
                pe.wait_ge(S["v_ready"], 16 * (m + 1))
                pe.wait_ge(S["gram_read0"], PAIRS * grams)
                pe.wait_ge(S["gram_read1"], PAIRS * grams)

                def project_out(p):
                    pe.wait_ge(S["outT_ready"], 16 * (m + 1) + 2 * p + 2)
                    for t in range(T):
                        ins = pe.matmul(g_bank[t // 4][:, (t % 4) * P:(t % 4 + 1) * P], outT[:, p % 2, t::T],
                                        C["b_oT"][:, p, :], start=(p == 0 and t % 4 == 0),
                                        stop=(p == PAIRS - 1 and t % 4 == 3), skip_group_check=True)
                    ins.then_inc(S["att_done"], 1)

                for p in range(PAIRS):
                    if p % 2 == 0:
                        pe.wait_ge(S[f"spread_loaded{p // 2 % 2}"], (m * 2 + p // 4 + 1) * 16 * BL)
                    for q in range(2):
                        n = 2 * p + q
                        if n >= 4:
                            pe.wait_ge(S["outT_ready"], 16 * (m + 1) + n - 3)
                        for a in range(NTAU // 2):
                            for hh in range(2):
                                hd = (2 * p + hh) * DH
                                ins = pe.matmul(ring[n % 4][hh * DH:(hh + 1) * DH, a * P:(a + 1) * P],
                                                v[:, q * 4 + a, hd:hd + DH],
                                                spread[:, (p // 2) % 2, q * 4 + a, :, (2 * p + hh) % QH],
                                                start=True, stop=True)
                        ins.then_inc(S["mixed_full"], 1)
                    if p >= 1:
                        project_out(p - 1)
                    if routed is not None and p < 4:
                        routing(routed, 4 + p)
                project_out(PAIRS - 1)

            keys_and_queries(0, None)
            values(0)
            keys_and_queries(1, None)
            mix_values(0, 2)
            with pe.Fori(2, NG) as g:
                values(g - 1)
                keys_and_queries(g, g - 2)
                mix_values(g - 1, g + 1)
            values(NG - 1)
            for p in range(4):
                routing(NG - 2, p)
            router.use(1)
            mix_values(NG - 1, NG, NG - 2)
            for j in range(2):
                router.use(j)
                for p in range(4):
                    routing(NG - 1, 4 * j + p)
            router.use(0)

        @block.scalar
        def _(act):
            def values(m):
                if isinstance(m, int) and m == 0:
                    act.wait_ge(S["parts_added"], 2 * NG)
                for k in range(16):
                    act.wait_ge(S["v_full"], 16 * m + k + 1)
                    act.copy(v[:, k // 2, (k % 2) * 512:(k % 2) * 512 + 512], ring[k % 4][:, :]).then_inc(S["v_ready"], 1)

            def routing(m, p):
                j = p // 4
                if p % 4 == 1:
                    router.turned(act, 2 * m + j)
                elif p % 4 == 2:
                    router.exponent(act, 2 * m + j)

            def keys_and_queries(g, routed):
                for q in range(2):
                    act.wait_ge(S["hT_full"], 2 * g + q + 1)
                    act.copy(hT[:, :].rearrange("c (b t) -> c t b", t=T)[:, 4 * q:4 * q + 4, :],
                             ring[q][:, :].rearrange("c (t b) -> c t b", t=4)).then_inc(S["hT_ready"], 1)

                def gram_copy(p):
                    act.wait_ge(S["gram_done"], g * PAIRS + p + 1)
                    if p == 0 and not (isinstance(g, int) and g == 0):
                        act.wait_ge(S["gram_stored"], g * 16 * BL)
                    act.copy(gram[:, :, :, :, 2 * p].rearrange("p a b k -> p a k b"),
                             g_bank[0][:, :].rearrange("p (a k b) -> p a k b", a=NTAU, k=2)).then_inc(S["gram_read0"], 1)
                    act.copy(gram[:, :, :, :, 2 * p + 1].rearrange("p a b k -> p a k b"),
                             g_bank[1][:, :].rearrange("p (a k b) -> p a k b", a=NTAU, k=2)).then_inc(S["gram_read1"], 1)

                for n in range(32):
                    act.wait_ge(S["kq_full"], g * 32 + n + 1)
                    if n >= 2:
                        act.wait_ge(S["kq_ready"], g * 32 + n - 1)
                    act.activation(pos_exp[:, n % 2, :], ring[n % 4][:, :], ACT.Exp)
                    p, k = n // 4, n % 4
                    if p >= 2 and k == 0:
                        act.wait_ge(S["gram_done"], g * PAIRS + p - 1)
                    act.activation(kq[:, p % 2, k // 2, (k % 2) * 512:(k % 2) * 512 + 512], ring[n % 4][:, :], ACT.Relu)\
                        .then_inc(S["rel_read"], 1)
                    if k == 3 and p >= 1:
                        gram_copy(p - 1)
                        if routed is not None:
                            routing(routed, p - 1)
                gram_copy(PAIRS - 1)
                act.wait_ge(S["beta_logit"], g + 1)
                act.activation(beta[:, :, :], sums[:, 1, :, 0, :], ACT.Exp, scale=-1.0).then_inc(S["beta_exp"], 1)

            def mix_values(m, routed=None):
                for n in range(16):
                    p, q = n // 2, n % 2
                    act.wait_ge(S["mixed_full"], 16 * m + n + 1)
                    if n % 2 == 0 and p >= 2:
                        act.wait_ge(S["att_done"], PAIRS * m + p - 1)
                    if n == 0 and not (isinstance(m, int) and m == 0):
                        act.wait_ge(S["x_ready"], m)
                    act.copy(outT[:, p % 2, q * 512:(q + 1) * 512], ring[n % 4][:, :]).then_inc(S["outT_ready"], 1)
                    if routed is not None and q == 1 and p < 4:
                        routing(routed, 4 + p)

            act.sem_inc(S["outT_ready"], 16)
            keys_and_queries(0, None)
            values(0)
            keys_and_queries(1, None)
            mix_values(0)
            with act.Fori(2, NG) as g:
                values(g - 1)
                keys_and_queries(g, g - 2)
                mix_values(g - 1)
            values(NG - 1)
            for p in range(4):
                routing(NG - 2, p)
            mix_values(NG - 1, NG - 2)
            for p in range(PAIRS):
                routing(NG - 1, p)

        @block.vector
        def _(dve):
            def normalize(g, k):
                tiles = [x_tile(g, t) for t in range(T)]
                ln.statistics(dve, tiles, k)
                if not (isinstance(g, int) and g == 0):
                    dve.wait_ge(S["hT_full"], 2 * g)
                ln.apply(dve, tiles, [h[:, t, :] for t in range(T)], k).then_inc(S["h_ready"], 1)

            def solver(m, step):

                def then(ins):
                    step[0] += 1
                    ins.then_inc(S["solve_step"], 1)
                    dve.wait_ge(S["solve_step"], m * STEPS + step[0])

                def unit_sums():
                    then(dve.reciprocal(rsum[:, :, :, :], sums[:, 0, :, :, :]))
                    dve.wait_ge(S["coef_loaded"], (m + 1) * 16)
                    by_s = coef[:, :, :, :, :].rearrange("p s t k h -> p s (t k h)")
                    then(dve.tensor_tensor(by_s, by_s, rsum[:, :, :, :].rearrange("p t k h -> p (t k h)").unsqueeze(1)
                                           .to_broadcast([P, T, T * 2 * HEADS]), ALU.mult))

                def unit_sums_of_keys():
                    by_tk = coef[:, :, :, :, :].rearrange("p s t k h -> p s (t k) h")
                    then(dve.tensor_tensor(by_tk, by_tk, rsum[:, :, 0, :].unsqueeze(2).to_broadcast([P, T, 2 * T, HEADS]),
                                           ALU.mult))

                def denominators():
                    dve.memset(den[:, 0, 0, :], 1.0)
                    dve.tensor_copy(den[:, 0, 1, :], coef[:, 0, 0, 1, :])
                    then(dve.tensor_copy(den[:, 1:T, :, :], coef[:, 0, 1:T, :, :]))
                    for s in range(1, T - 1):
                        then(dve.tensor_tensor(den[:, s + 1:T, :, :], den[:, s + 1:T, :, :], coef[:, s, s + 1:T, :, :],
                                               ALU.add))
                    diag = coef[:, :, :, 1, :].rearrange("p s t h -> p (s t) h")[:, T + 1::T + 1, :]
                    then(dve.tensor_tensor(den[:, 1:T, 1, :], den[:, 1:T, 1, :], diag, ALU.add))

                def reciprocals():
                    then(dve.tensor_scalar(rden[:, :, :, :], den[:, :, :, :], EPS, None, ALU.add))
                    then(dve.reciprocal(rden[:, :, :, :], rden[:, :, :, :]))
                    dve.wait_ge(S["beta_exp"], m + 1)
                    then(dve.tensor_scalar(beta[:, :, :], beta[:, :, :], 1.0, None, ALU.add))
                    then(dve.reciprocal(beta[:, :, :], beta[:, :, :]))

                def factors():
                    then(dve.tensor_tensor(gamma[:, :, :], beta[:, :, :], den[:, :, 0, :], ALU.mult))
                    then(dve.tensor_tensor(gamma[:, :, :], gamma[:, :, :], rden[:, :, 0, :], ALU.mult))
                    dve.tensor_copy(inv[:, :, :, :].rearrange("p t u h -> p (t u) h")[:, ::T + 1, :], gamma[:, :, :])
                    dve.tensor_scalar(rden[:, :, 1, :], rden[:, :, 1, :], SCALE, None, ALU.mult)
                    then(dve.scalar_tensor_tensor(out=alpha[:, :, :], in0=gamma[:, :, :], scalar=-1.0, in1=rden[:, :, 0, :],
                                                  op0=ALU.mult, op1=ALU.mult))

                def apply_factors():
                    dve.tensor_tensor(coef[:, :, :, 0, :], coef[:, :, :, 0, :], alpha[:, :, :].unsqueeze(1)
                                      .to_broadcast([P, T, T, HEADS]), ALU.mult)
                    then(dve.tensor_tensor(coef[:, :, :, 1, :], coef[:, :, :, 1, :], rden[:, :, 1, :].unsqueeze(1)
                                           .to_broadcast([P, T, T, HEADS]), ALU.mult))

                def inverse_row(t):
                    then(dve.tensor_tensor(prod[:, 0:t, 0:t, :], inv[:, 0:t, 0:t, :],
                                           coef[:, 0:t, t, 0, :].unsqueeze(2).to_broadcast([P, t, t, HEADS]), ALU.mult))
                    then(dve.tensor_reduce(inv[:, t, 0:t, :], prod[:, 0:t, 0:t, :].rearrange("p s u h -> p u h s"),
                                           AX_X, ALU.add))

                def mix_column(t):
                    n = t + 1
                    then(dve.tensor_tensor(prod[:, 0:n, 0:n, :], inv[:, 0:n, 0:n, :],
                                           coef[:, 0:n, t, 1, :].unsqueeze(2).to_broadcast([P, n, n, HEADS]), ALU.mult))
                    then(dve.tensor_reduce(mix[:, 0:n, t, :], prod[:, 0:n, 0:n, :].rearrange("p s u h -> p u h s"),
                                           AX_X, ALU.add))

                def by_quarters():
                    for q in range(4):
                        ins = dve.tensor_copy(mix_q[:, :, q, :, :], mix[:, :, :, q * QH:(q + 1) * QH])
                    then(ins)
                    assert step[0] == STEPS, step

                def part(i):
                    if i < 6:
                        (unit_sums, unit_sums_of_keys, denominators, reciprocals, factors, apply_factors)[i]()
                    elif i < 6 + T - 1:
                        inverse_row(i - 5)
                    elif i < 6 + 2 * T - 1:
                        mix_column(i - 5 - T)
                    else:
                        by_quarters()

                return part

            SOLVE_PARTS = 6 + 2 * T
            EARLY = 6
            EARLY_STEPS = 19

            def solve_early(g):
                step = [0]
                solve = solver(g, step)
                for i in range(EARLY):
                    solve(i)
                assert step[0] == EARLY_STEPS, step

            def routing(m, p):
                r = route(m, p // 4)
                if p % 4 == 0:
                    if p == 0:
                        dve.wait_ge(S["x_ready"], m + 1)
                    router.statistics(dve, r)
                    router.normalize(dve, r)
                elif p % 4 == 2:
                    router.choose(dve, r)
                elif p % 4 == 3:
                    router.weigh(dve, r)
                    router.placed(dve, r)

            def keys_and_queries(g, routed):
                later = not (isinstance(g, int) and g == 0)
                early = later and not (isinstance(g, int) and g == 1)
                solve = solver(g - 1, [EARLY_STEPS if early else 0]) if later else None
                for n in range(32):
                    dve.wait_ge(S["rel_read"], g * 32 + n + 1)
                    p, k = n // 4, n % 4
                    tile = kq[:, p % 2, k // 2, (k % 2) * 512:(k % 2) * 512 + 512]
                    dve.scalar_tensor_tensor(out=tile, in0=pos_exp[:, n % 2, :], scalar=1.0, in1=tile,
                                             op0=ALU.min, op1=ALU.add).then_inc(S["kq_ready"], 1)
                    if k == 3 and p >= 1 and routed is not None:
                        routing(routed, p - 1)
                    if not later and n in (8, 16, 24):
                        add_parts(n // 8)
                    part_now = n + EARLY - 1 if early else n - 2
                    if later and (EARLY if early else 0) <= part_now < SOLVE_PARTS:
                        solve(part_now)
                if routed is not None:
                    routing(routed, PAIRS - 1)
                dve.wait_ge(S["gram_done"], (g + 1) * PAIRS)
                if later:
                    dve.wait_ge(S["mix_stored"], g * 16)
                dve.tensor_copy(sums_raw, s_bank[:, :].rearrange("p (a b t) -> p a t b", a=2, t=T)).then_inc(S["sums_read"], 1)
                dve.wait_ge(S["sums_read"], g + 1)
                dve.transpose(sums[:, :, :, :, :].rearrange("p a t k h -> p (a t k h)"),
                              sums_raw.rearrange("p a t b -> p (a t b)")).then_inc(S["beta_logit"], 1)
                dve.wait_ge(S["beta_logit"], g + 1)

            def add_output(m, k, m_next):
                tiles = [x_tile(m, t) for t in range(T)]
                res_tiles = [res[:, t, :] for t in range(T)]
                ln.statistics(dve, tiles, k)
                if m_next is not None:
                    solve_early(m_next)
                dve.wait_ge(S["att_done"], PAIRS * m + PAIRS - 1)
                ln.apply(dve, tiles, res_tiles, k).then_inc(S["resid_step"], 1)
                dve.wait_ge(S["resid_step"], m + 1)
                dve.wait_ge(S["att_done"], PAIRS * (m + 1))
                for q in range(2):
                    ins = dve.tensor_tensor(res[:, 4 * q:4 * q + 4, :], res[:, 4 * q:4 * q + 4, :],
                                            g_bank[q][:, :].rearrange("p (t c) -> p t c", t=4), ALU.add)
                ins.then_inc(S["att_read"], 1)
                dve.wait_ge(S["att_read"], m + 2)
                ln.statistics(dve, res_tiles, k + 1)
                ln.apply(dve, res_tiles, res_tiles, k + 1).then_inc(S["normed"], 1)

            def add_parts(g):
                dve.wait_ge(part_in[g], 32)
                x_g = x[:, 0:BATCH * NT, :].rearrange("p (t g) c -> p g t c", g=NG)[:, g, :, :]
                for k in range(2):
                    dve.tensor_tensor(x_g, x_g, part[:, g, k, :].rearrange("p (t c) -> p t c", t=T), ALU.add)\
                        .then_inc(S["parts_added"], 1)
                    dve.wait_ge(S["parts_added"], 2 * g + k + 1)

            dve.sem_inc(S["att_read"], 1)
            add_parts(0)
            normalize(0, 0)
            dve.memset(spread[:, :, :, :, :], 0.0)
            dve.memset(inv[:, :, :, :], 0.0)
            dve.memset(mix[:, :, :, :], 0.0).then_inc(S["spread_zero"], 1)
            router.begin(dve)
            keys_and_queries(0, None)
            normalize(1, 1)
            keys_and_queries(1, None)
            normalize(2, 2)
            add_output(0, 3, 1)
            with dve.Fori(2, NG) as g:
                keys_and_queries(g, g - 2)
                normalize(g + 1, 3 * g - 1)
                add_output(g - 1, 3 * g, g)
            last = solver(NG - 1, [EARLY_STEPS])
            beside = {9: 0, 13: 2, 17: 3}
            for i in range(EARLY, SOLVE_PARTS):
                last(i)
                if i in beside:
                    routing(NG - 2, beside[i])
            router.use(1)
            for p in (4, 6, 7):
                routing(NG - 2, p)
            add_output(NG - 1, 3 * NG - 1, None)
            scale_and_add(dve, NG - 1)
            for p in (0, 4, 2, 3, 6, 7):
                router.use(p // 4)
                routing(NG - 1, p)
            router.use(0)
            block_table.make(dve)


def build(nc, a):
    inp = {"x": a["L0_attn_a_x"], "W_qkv": a["L0_attn_a_W_qkv"], "RF": a["L0_attn_a_RF"], "W_out": a["L0_attn_a_W_out"],
           "b_out": a["L0_attn_a_b_out"], "w_qkvb": a["L0_attn_b_w_qkvb"], "w_o": a["L0_attn_b_w_o"],
           "ln_g": a["L0_attn_b_ln_g"], "ln_b": a["L0_attn_b_ln_b"], "Wr": a["L0_ffn_Wr"], "W1": a["L0_ffn_W1"],
           "W2": a["L0_ffn_W2"]}
    gd = nc.dram_tensor("gram_compact", [P, T, T * 2 * HEADS], F32, kind="Internal").ap()
    cd = nc.dram_tensor("mix_compact", [P, T, 4, T * HEADS // 4], F32, kind="Internal").ap()
    rows = nc.dram_tensor("expert_rows", [UNUSED + P, ROW], F32, kind="Internal").ap()
    parts = nc.dram_tensor("expert_parts", [2 * TOKENS, DIM], F32, kind="Internal").ap()
    with ExitStack() as ctx:
        K = Kernel(nc, ctx)
        C = {
            "x": K.sb(ctx, "x", [P, BATCH * NT + 1, DIM]),
            "ident": K.sb(ctx, "ident", [P, P]),
            "b_out": K.sb(ctx, "b_out", [P, DIM]),
            "ln_g": K.sb(ctx, "ln_g", [P, DIM]),
            "ln_b": K.sb(ctx, "ln_b", [P, DIM]),
            "w_r": K.sb(ctx, "w_r", [P, EXPERTS]),
            "ones": K.sb(ctx, "ones", [P, P]),
            "earlier": K.sb(ctx, "earlier", [P, P]),
            "filler": K.sb(ctx, "filler", [P, ROW]),
            "part_ids": K.sb(ctx, "part_ids", [P, BATCH * NT, 2], U32),
            "block_rows": K.sb(ctx, "block_rows", [P, BLOCKS]),
            "regions": K.sb(ctx, "regions", [P, EXPERTS]),
            "minus_half": K.sb(ctx, "minus_half", [P, T]),
            "expert_ids": K.sb(ctx, "expert_ids", [P, EXPERTS]),
            "head_ind": K.sb(ctx, "head_ind", [P, 2, PAIRS, 32]),
            "b_qkT": K.sb(ctx, "b_qkT", [P, 2 * HD]),
            "b_vT": K.sb(ctx, "b_vT", [P, HD]),
            "b_betaT": K.sb(ctx, "b_betaT", [P, 32]),
            "b_oT": K.sb(ctx, "b_oT", [P, PAIRS, DIM]),
            "wide": K.sb(ctx, "wide", [P, 2 * EXPERTS * FF]),
            "table": K.sb(ctx, "table", [P, 2, BLOCKS], U32),
            "tail": K.sb(ctx, "tail", [P, EXPERTS], U32),
            "filled": K.sb(ctx, "filled", [P, EXPERTS]),
            "w_in": [K.sem("w_in0"), K.sem("w_in1")],
        }
        C["w1"] = C["wide"][:, 0:EXPERTS * FF].rearrange("p (e f) -> p e f", e=EXPERTS)
        C["w2"] = C["wide"][:, EXPERTS * FF:2 * EXPERTS * FF].rearrange("p (e a c) -> p e a c", e=EXPERTS, a=FC)
        with ExitStack() as actx:
            A = {
                "feat_q": K.sb(actx, "feat_q", [P, HD]),
                "feat_k": K.sb(actx, "feat_k", [P, HD]),
                "vo": K.sb(actx, "vo", [P, HEADS, DIM]),
            }
            load_and_fold_weights(K, C, A, inp)
            linear_attention(K, C, A, rows)
        expert_ffn(K, C, "f", 0, rows, parts)
        delta_memory(K, C, cd, gd, inp, rows, parts)
        expert_ffn(K, C, "g", 1, rows, parts, out=a["out"])


_INS = ["L0_attn_a_x", "L0_attn_a_W_qkv", "L0_attn_a_RF", "L0_attn_a_W_out", "L0_attn_a_b_out", "L0_attn_b_w_qkvb",
        "L0_attn_b_w_o", "L0_attn_b_ln_g", "L0_attn_b_ln_b", "L0_ffn_Wr", "L0_ffn_W1", "L0_ffn_W2"]


def kernel(**inputs):
    import numpy as np
    import concourse.bacc as bacc
    from concourse.bass_utils import run_bass_kernel_spmd

    nc = bacc.Bacc("TRN2", target_bir_lowering=False, num_devices=1)
    arrays, args = {}, {}
    for name in _INS:
        arr = np.ascontiguousarray(inputs[name])
        arrays[f"in_{name}"] = arr
        args[name] = nc.dram_tensor(f"in_{name}", arr.shape, mybir.dt.from_np(arr.dtype), kind="ExternalInput").ap()
    args["out"] = nc.dram_tensor("out_x", (BATCH, SEQ, DIM), F32, kind="ExternalOutput").ap()
    build(nc, args)
    r = run_bass_kernel_spmd(nc, [arrays], core_ids=[0])
    return r.results[0]["out_x"]
```
